# Optimizing a Trainium2 kernel written in Bass

```python
import numpy as np
import jax
import jax.numpy as jnp

def _softmax(x, axis=-1):
    return jax.nn.softmax(x, axis=axis)

def _gelu(x):
    return jax.nn.gelu(x, approximate=True)

def _silu(x):
    return jax.nn.silu(x)

def _sigmoid(x):
    return jax.nn.sigmoid(x)

def _layernorm(x, axis=-1, eps=1e-05):
    m = jnp.mean(x, axis=axis, keepdims=True)
    v = jnp.var(x, axis=axis, keepdims=True)
    return (x - m) / jnp.sqrt(v + eps)

def _scatter_add(tgt, idx, src, axis=0):
    return tgt.at[idx].add(src)

def _segment_sum(src, seg, n):
    return jax.ops.segment_sum(src, seg, n)
kernel_name = 'mk_gps_d1_gnn_r32_7a973b'

def setup_inputs(seed: int=0):
    np.random.seed(seed)
    _w = jnp.asarray

    def _rec_inputs():
        import jax
        import jax.numpy as jnp
        _gk = jax.random.key(seed)
        x = -0.0002117 + 1 * jax.random.normal(jax.random.fold_in(_gk, 1), (3125, 256), jnp.float32)
        _s = jax.random.randint(jax.random.fold_in(_gk, 2), (25000,), 0, 3125, jnp.int32)
        _d = jax.random.randint(jax.random.fold_in(_gk, 3), (25000,), 0, 3125, jnp.int32)
        _loop = jnp.arange(3125, dtype=jnp.int32)
        src = jnp.concatenate([_s, _d, _loop])
        dst = jnp.concatenate([_d, _s, _loop])
        _o = jnp.argsort(dst, stable=True)
        src = src[_o]
        dst = dst[_o]
        return (x, src, dst)
    x, src, dst = _rec_inputs()

    def _L0_gnn_setup():
        import jax, jax.numpy as jnp
        import numpy as np
        N, D_DIM, K, R = (3125, 256, 4, 16)
        E_RAND = 50000
        ETA, LAM, C = (0.5, 0.1, 0.5)
        key = jax.random.key(seed)
        k1, k2, k3, k4 = jax.random.split(key, 4)
        Z = jax.random.normal(k1, (N, D_DIM), jnp.float32)
        U = jax.random.normal(k2, (K, D_DIM, R), jnp.float32) / np.float32(np.sqrt(D_DIM))
        Dmat = jax.random.normal(k3, (D_DIM, D_DIM), jnp.float32) / np.float32(np.sqrt(D_DIM))
        head_w = jnp.ones((K,), jnp.float32) / K
        rnd = jax.random.randint(k4, (2, E_RAND), 0, N)
        loops = jnp.stack([jnp.arange(N), jnp.arange(N)])
        edge_index = jnp.concatenate([rnd, loops], axis=1)
        return {'Z': Z, 'U': U, 'Dmat': Dmat, 'head_w': head_w, 'edge_index': edge_index}
    _L0_gnn_all = _L0_gnn_setup()
    _L0_gnn_in = {k: v for k, v in _L0_gnn_all.items() if k in ('U', 'Dmat', 'head_w')}
    del _L0_gnn_all

    def _L0_mix_setup():
        import jax, jax.numpy as jnp
        import numpy as np
        MIDC = 256
        HEADS = 8
        HEADC = MIDC // HEADS
        EPS = 1e-05

        def _ln(x, gamma, beta):
            mu = jnp.mean(x, axis=-1, keepdims=True)
            var = jnp.var(x, axis=-1, keepdims=True)
            return (x - mu) * jax.lax.rsqrt(var + EPS) * gamma + beta
        key = jax.random.key(seed)
        ks = jax.random.split(key, 8)
        B, HW, C = (8, 128, MIDC)
        s = 1.0 / np.sqrt(C)
        return {'x': jax.random.normal(ks[0], (B, HW, C), jnp.float32), 'w_qkv': jax.random.normal(ks[1], (C, 3 * C), jnp.float32) * s, 'b_qkv': jnp.zeros((3 * C,), jnp.float32), 'kln_g': jnp.ones((HEADC,), jnp.float32), 'kln_b': jnp.zeros((HEADC,), jnp.float32), 'vln_g': jnp.ones((HEADC,), jnp.float32), 'vln_b': jnp.zeros((HEADC,), jnp.float32), 'w1': jax.random.normal(ks[2], (C, C), jnp.float32) * s, 'b1': jnp.zeros((C,), jnp.float32), 'w2': jax.random.normal(ks[3], (C, C), jnp.float32) * s, 'b2': jnp.zeros((C,), jnp.float32)}
    _L0_mix_all = _L0_mix_setup()
    _L0_mix_in = {k: v for k, v in _L0_mix_all.items() if k in ('w_qkv', 'b_qkv', 'kln_g', 'kln_b', 'vln_g', 'vln_b', 'w1', 'b1', 'w2', 'b2')}
    del _L0_mix_all

    def _L0_ffn_setup():
        import jax, jax.numpy as jnp
        import numpy as np
        NUM_EXPERTS = 8
        TOP_K = 2
        B, S, D = (8, 256, 256)

        def _moe(tokens, router_w, w1, b1, w2, b2):
            N = tokens.shape[0]
            E = router_w.shape[0]
            logits = tokens.astype(jnp.float32) @ router_w.astype(jnp.float32).T
            probs = jax.nn.softmax(logits, axis=-1)
            rw, re = jax.lax.top_k(probs, TOP_K)
            if TOP_K > 1:
                rw = rw / jnp.maximum(rw.sum(-1, keepdims=True), 1e-12)
            rw = rw.astype(tokens.dtype)
            combine = jnp.zeros((N, E), tokens.dtype).at[jnp.arange(N)[:, None], re].set(rw)
            out = tokens
            for e in range(E):
                h = jax.nn.gelu(tokens @ w1[e] + b1[e], approximate=False)
                y = h @ w2[e] + b2[e]
                out = out + combine[:, e:e + 1] * y
            return out
        key = jax.random.key(seed)
        ks = jax.random.split(key, 4)
        scale = 1.0 / np.sqrt(D).astype(np.float32)
        return {'input_embeddings': jax.random.normal(ks[0], (B, S, D), jnp.float32), 'router_w': jax.random.normal(ks[1], (NUM_EXPERTS, D), jnp.float32) * scale, 'w1': jax.random.normal(ks[2], (NUM_EXPERTS, D, D), jnp.float32) * scale, 'b1': jnp.zeros((NUM_EXPERTS, D), jnp.float32), 'w2': jax.random.normal(ks[3], (NUM_EXPERTS, D, D), jnp.float32) * scale, 'b2': jnp.zeros((NUM_EXPERTS, D), jnp.float32)}
    _L0_ffn_all = _L0_ffn_setup()
    _L0_ffn_in = {k: v for k, v in _L0_ffn_all.items() if k in ('router_w', 'w1', 'b1', 'w2', 'b2')}
    del _L0_ffn_all
    return {'x': x, 'src': src, 'dst': dst, 'L0_gnn_U': _L0_gnn_in['U'], 'L0_gnn_Dmat': _L0_gnn_in['Dmat'], 'L0_gnn_head_w': _L0_gnn_in['head_w'], 'L0_mix_w_qkv': _L0_mix_in['w_qkv'], 'L0_mix_b_qkv': _L0_mix_in['b_qkv'], 'L0_mix_kln_g': _L0_mix_in['kln_g'], 'L0_mix_kln_b': _L0_mix_in['kln_b'], 'L0_mix_vln_g': _L0_mix_in['vln_g'], 'L0_mix_vln_b': _L0_mix_in['vln_b'], 'L0_mix_w1': _L0_mix_in['w1'], 'L0_mix_b1': _L0_mix_in['b1'], 'L0_mix_w2': _L0_mix_in['w2'], 'L0_mix_b2': _L0_mix_in['b2'], 'L0_ffn_router_w': _L0_ffn_in['router_w'], 'L0_ffn_w1': _L0_ffn_in['w1'], 'L0_ffn_b1': _L0_ffn_in['b1'], 'L0_ffn_w2': _L0_ffn_in['w2'], 'L0_ffn_b2': _L0_ffn_in['b2']}

def reference(x, src, dst, L0_gnn_U, L0_gnn_Dmat, L0_gnn_head_w, L0_mix_w_qkv, L0_mix_b_qkv, L0_mix_kln_g, L0_mix_kln_b, L0_mix_vln_g, L0_mix_vln_b, L0_mix_w1, L0_mix_b1, L0_mix_w2, L0_mix_b2, L0_ffn_router_w, L0_ffn_w1, L0_ffn_b1, L0_ffn_w2, L0_ffn_b2):
    import jax
    import jax.numpy as jnp

    def _L0_gnn_ref(Z, U, Dmat, head_w, edge_index):
        import jax, jax.numpy as jnp
        import numpy as np
        N, D_DIM, K, R = (3125, 256, 4, 16)
        E_RAND = 50000
        ETA, LAM, C = (0.5, 0.1, 0.5)
        src, dst = (edge_index[0], edge_index[1])
        scale = np.float32(np.sqrt(R))
        ZU = jnp.einsum('nd,kdr->knr', Z, U)
        zs = ZU[:, src, :]
        zd = ZU[:, dst, :]
        logits = (zs * zd).sum(-1) / scale
        seg_max = jax.vmap(lambda l: jax.ops.segment_max(l, dst, num_segments=N))(logits)
        exp_l = jnp.exp(logits - seg_max[:, dst])
        seg_sum = jax.vmap(lambda e: jax.ops.segment_sum(e, dst, num_segments=N))(exp_l)
        alpha = exp_l / (seg_sum[:, dst] + 1e-16)
        weighted = alpha[..., None] * zs
        agg = jax.vmap(lambda w_: jax.ops.segment_sum(w_, dst, num_segments=N))(weighted)
        w = jax.nn.softmax(head_w)
        ssa = jnp.einsum('k,knr,kdr->nd', w, agg, U)
        Z_half = (1.0 - C) * Z + C * ssa
        DZ = Z_half @ Dmat.T
        residual = Z_half - DZ @ Dmat
        grad_step = Z_half + ETA * (residual @ Dmat)
        return jax.nn.relu(grad_step - ETA * LAM)

    def _L0_mix_ref(x, w_qkv, b_qkv, kln_g, kln_b, vln_g, vln_b, w1, b1, w2, b2):
        import jax, jax.numpy as jnp
        import numpy as np
        MIDC = 256
        HEADS = 8
        HEADC = MIDC // HEADS
        EPS = 1e-05

        def _ln(x, gamma, beta):
            mu = jnp.mean(x, axis=-1, keepdims=True)
            var = jnp.var(x, axis=-1, keepdims=True)
            return (x - mu) * jax.lax.rsqrt(var + EPS) * gamma + beta
        B, HW, C = x.shape
        bias = x
        qkv = (x @ w_qkv + b_qkv).reshape(B, HW, HEADS, 3 * HEADC)
        qkv = qkv.transpose(0, 2, 1, 3)
        q, k, v = jnp.split(qkv, 3, axis=-1)
        k = _ln(k, kln_g, kln_b)
        v = _ln(v, vln_g, vln_b)
        kv = jnp.einsum('bhnd,bhne->bhde', k, v) / HW
        out = jnp.einsum('bhnd,bhde->bhne', q, kv)
        out = out.transpose(0, 2, 1, 3).reshape(B, HW, C)
        ret = out + bias
        h = jax.nn.gelu(ret @ w1 + b1, approximate=False)
        return h @ w2 + b2 + bias

    def _L0_ffn_ref(input_embeddings, router_w, w1, b1, w2, b2):
        import jax, jax.numpy as jnp
        import numpy as np
        NUM_EXPERTS = 8
        TOP_K = 2
        B, S, D = (8, 256, 256)

        def _moe(tokens, router_w, w1, b1, w2, b2):
            N = tokens.shape[0]
            E = router_w.shape[0]
            logits = tokens.astype(jnp.float32) @ router_w.astype(jnp.float32).T
            probs = jax.nn.softmax(logits, axis=-1)
            rw, re = jax.lax.top_k(probs, TOP_K)
            if TOP_K > 1:
                rw = rw / jnp.maximum(rw.sum(-1, keepdims=True), 1e-12)
            rw = rw.astype(tokens.dtype)
            combine = jnp.zeros((N, E), tokens.dtype).at[jnp.arange(N)[:, None], re].set(rw)
            out = tokens
            for e in range(E):
                h = jax.nn.gelu(tokens @ w1[e] + b1[e], approximate=False)
                y = h @ w2[e] + b2[e]
                out = out + combine[:, e:e + 1] * y
            return out
        b, s, d = input_embeddings.shape
        tokens = input_embeddings.reshape(b * s, d)
        return _moe(tokens, router_w, w1, b1, w2, b2).reshape(b, s, d)
    edge_index = jnp.stack([src, dst])
    xn = _layernorm(x, axis=-1)
    x = x + _L0_gnn_ref(xn, L0_gnn_U, L0_gnn_Dmat, L0_gnn_head_w, edge_index) + _L0_mix_ref(xn[None], L0_mix_w_qkv, L0_mix_b_qkv, L0_mix_kln_g, L0_mix_kln_b, L0_mix_vln_g, L0_mix_vln_b, L0_mix_w1, L0_mix_b1, L0_mix_w2, L0_mix_b2)[0]
    x = x + _L0_ffn_ref(_layernorm(x, axis=-1)[None], L0_ffn_router_w, L0_ffn_w1, L0_ffn_b1, L0_ffn_w2, L0_ffn_b2)[0]
    return x

_drawn_inputs = setup_inputs


def setup_inputs(seed=0):
    import zlib

    import numpy as np

    out = dict(_drawn_inputs(seed))
    spreads = {'L0_gnn_head_w': (0.25, 0.6),
     'L0_mix_b_qkv': (0.0, 0.1),
     'L0_mix_kln_g': (1.0, 0.6),
     'L0_mix_kln_b': (0.0, 0.374),
     'L0_mix_vln_g': (1.0, 0.546),
     'L0_mix_vln_b': (0.0, 0.352),
     'L0_mix_b1': (0.0, 0.1),
     'L0_mix_b2': (0.0, 0.1),
     'L0_ffn_b1': (0.0, 0.546),
     'L0_ffn_b2': (0.0, 0.369)}
    factors = {'L0_gnn_U': 2.933}
    for name, (base, spread) in spreads.items():
        noise = np.random.default_rng([zlib.crc32(name.encode()), seed]).standard_normal(out[name].shape)
        drawn = base * np.exp(spread * noise) if base else spread * noise
        out[name] = jnp.asarray(drawn.astype(out[name].dtype))
    for name, factor in factors.items():
        out[name] = (out[name] * factor).astype(out[name].dtype)
    return out
```

```python
import concourse.bass as bass
from concourse import mybir
from contextlib import ExitStack
import numpy as np

F32 = mybir.dt.float32
BF16 = mybir.dt.bfloat16
I32 = mybir.dt.int32
ALU = mybir.AluOpType
ACT = mybir.ActivationFunctionType
AX = mybir.AxisListType

N, D, E = 3125, 256, 53125
P = 125
T = N // P
GT = 5
G = T // GT
EP = E // P
CE = 85
C = EP // CE
K, R = 4, 16
KR = K * R
SW = KR + 2 * K
H, HC = 8, 32
X = 8
BIG = 1.0e38
OUT_OF_RANGE = 60000.0
LOGIT_SCALE = 1.0 / np.sqrt(np.float32(R))
EPS = 1e-5
COLS = GT * P
HALF = ((0, 313), (313, 312))


def build(nc, x, src, dst, U, Dmat, head_w, w_qkv, b_qkv, kln_g, kln_b, vln_g, vln_b,
          w1, b1, w2, b2, router_w, ew1, eb1, ew2, eb2, out):
    ctx = ExitStack()

    def sb(name, shape, dt=F32):
        return ctx.enter_context(nc.sbuf_tensor(name, shape, dt))

    def sem(name):
        return ctx.enter_context(nc.semaphore(name))

    with ctx:
        zu_dram = nc.dram_tensor("zu_table", (N, KR), F32).ap()
        zd_dram = nc.dram_tensor("zd_rows", (E, KR), F32).ap()
        st_dram = nc.dram_tensor("edge_states", (E, SW), F32).ap()
        g0_dram = nc.dram_tensor("grad_part", (N, D), F32).ap()

        acc = sb("acc", [P, T, D])
        xT = sb("xT", [128, 2, N])
        edge_buf = sb("edge_buf", [128, 2, CE * SW])
        slot = [edge_buf[0:P, s, :].rearrange("p (j f) -> p j f", f=SW) for s in range(2)]
        oh_all = edge_buf[0:P, 1, :].bitcast(BF16)
        oh_i = oh_all[:, 0:CE * P].rearrange("p (j a) -> p j a", a=P)
        small = sb("small", [128, 5 * CE * K])
        logit, dm, dl, rescale, weight = (small[0:P, n * CE * K:(n + 1) * CE * K].rearrange("p (j k) -> p j k", k=K)
                                          for n in range(5))
        oh_t = small[0:P, :].bitcast(BF16)[:, 0:CE * T].rearrange("p (j a) -> p j a", a=T)

        def small_part(at, shape):
            size = int(np.prod(shape[1:]))
            part = small[0:shape[0], at:at + size]
            if len(shape) == 3:
                part = part.rearrange("p (a b) -> p a b", b=shape[2])
            if len(shape) == 4:
                part = part.rearrange("p (a b c) -> p a b c", b=shape[2], c=shape[3])
            return part
        KA = KR + K
        cat = small_part(0, [P, 3, KA])
        car = small_part(3 * KA, [P, 2, KA])
        rows = small_part(5 * KA, [KA, 4, P + 1])
        moe_at = 5 * KA + 4 * (P + 1)
        lg = small_part(moe_at, [P, T, X])
        pr = small_part(moe_at + T * X, [P, T, X])
        oh = small_part(moe_at + 2 * T * X, [P, 2, T, X])
        g0 = edge_buf[0:P, :, :].rearrange("p s f -> p (s f)")[:, 0:T * D].rearrange("p (t f) -> p t f", f=D)
        zd_buf = sb("zd_buf", [128, CE * KR])
        zd = zd_buf[0:P, :].rearrange("p (j f) -> p j f", f=KR)
        ew = zd_buf[:, 0:2 * 4 * D].rearrange("p (s w c f) -> p s w c f", s=2, w=2, c=2)
        hbuf = sb("hbuf", [128, 2 * 2 * COLS])
        hT = hbuf[:, :].rearrange("p (b m n) -> p b m n", b=2, m=2)
        khv = hbuf[0:P, 0:1024].rearrange("p (b f) -> p b f", b=2)
        wqkv = hbuf[:, 0:6 * D].rearrange("p (c f) -> p c f", c=2)
        Q_sb = hbuf[:, 6 * D:8 * D].rearrange("p (c f) -> p c f", c=2)
        sq = hbuf[0:P, 1024:2048].rearrange("p (b f) -> p b f", b=2)
        agg = sb("agg", [P, T, SW])
        zu_sb = agg[:, :, 0:KR]

        ident = sb("ident", [128, 128])
        eye2 = sb("eye2", [128, 2, D])
        tri = sb("tri", [P, P])
        iota_i = sb("iota_i", [128, 128], I32)
        iota_f = sb("iota_f", [128, 128], BF16)
        rank8_i = sb("rank8_i", [P, X], I32)
        rank8 = sb("rank8", [P, 1, X])
        ones = sb("ones", [P, 128])
        zero_b = sb("zero_b", [P, P], BF16)

        U_sb = sb("U_sb", [128, 2, KR])
        D_sb = sb("D_sb", [128, 2, D])
        M_sb = sb("M_sb", [128, 2, D])
        UM_sb = sb("UM_sb", [KR, D])
        hw_all = sb("hw_all", [KR, K])
        hw_own = sb("hw_own", [KR, 1])
        hw_m = sb("hw_m", [KR, 4])
        wq = sb("wq", [128, 2, D])
        wkv = sb("wkv", [128, 2, 2 * D])
        wmean = sb("wmean", [128, 2, 2 * H])
        bqkv_row = sb("bqkv_row", [1, 3 * D])
        bkv_row = sb("bkv_row", [1, 2 * D])
        bmean = sb("bmean", [1, 2 * H])
        bq_col = sb("bq_col", [128, 2])
        gk_row = sb("gk_row", [128, 1, HC])
        bk_row = sb("bk_row", [128, 1, HC])
        gv_col = sb("gv_col", [128, 1])
        bv_col = sb("bv_col", [128, 1])
        kvt_a = sb("kvt_a", [128, 128])
        kvt_b = sb("kvt_b", [128, 128])
        kvt_c = sb("kvt_c", [128, 1])
        KVT = sb("KVT", [128, 2, 128])
        WqT = sb("WqT", [128, 2, D])
        w1_sb = sb("w1_sb", [128, 2, D])
        w2_sb = sb("w2_sb", [128, 2, D])
        b1_col = sb("b1_col", [128, 2])
        b2_row = sb("b2_row", [1, D])
        A_sb = sb("A_sb", [128, 2, D])
        B_sb = sb("B_sb", [128, 2, D])
        bh_col = sb("bh_col", [128, 2])
        rw_in = sb("rw_in", [X, D])
        rwT = sb("rwT", [128, 2, X])
        eb1_in = sb("eb1_in", [2 * X, 128])
        eb1_col = sb("eb1_col", [128, 2 * X])
        eb_pair = sb("eb_pair", [128, 4])
        eb2_sb = sb("eb2_sb", [X, D])

        stats = sb("stats", [P, T, 6])
        mv = sb("mv", [P, T, 2])
        sd = sb("sd", [P, T, 1])
        rstd = sb("rstd", [P, T, 1])
        xn = sb("xn", [P, 3, D])
        ss = sb("ss", [P, 3, 2 * H])
        g0_out = sb("g0_out", [P, 2, D])

        src_i = sb("src_i", [P, EP], I32)
        dst_i = sb("dst_i", [P, EP], I32)
        dst_f = sb("dst_f", [P, EP])
        quo_i = sb("quo_i", [P, EP], I32)
        quo_f = sb("quo_f", [P, EP])
        rem_f = sb("rem_f", [P, EP])
        fix_f = quo_i[:, :].bitcast(F32)
        quo_b = sb("quo_b", [P, EP, 1], BF16)
        rem_b = sb("rem_b", [P, EP, 1], BF16)
        same = sb("same", [P, EP, 1])
        forget = sb("forget", [P, EP, 1])
        first_run = quo_f
        prev_last = sb("prev_last", [P, 1], I32)
        next_first = sb("next_first", [P, 1], I32)
        edge_f = sb("edge_f", [P, 8])
        cont = sb("cont", [P, 8])
        fix_row_i = sb("fix_row_i", [P, 2], I32)
        count = sb("count", [P, T])
        incl = sb("incl", [P, T])
        ends = sb("ends", [P, T])
        starts = sb("starts", [P, T])
        empty = sb("empty", [P, T])
        has_edge = sb("has_edge", [P, T, 1])
        row_base = sb("row_base", [P, 1])
        start_row = sb("start_row", [P, T], I32)
        end_row = sb("end_row", [P, T], I32)
        part_row = sb("part_row", [P, 1])
        part_row_i = sb("part_row_i", [P, 1], I32)
        z_first = sb("z_first", [P, KR])
        z_last = sb("z_last", [P, KR])
        s_last = sb("s_last", [P, SW])

        loc = sb("loc", [P, SW])
        ew_r = sb("ew_r", [P, 4, K])

        rden = sb("rden", [P, T, K])
        aggT = sb("aggT", [KR, 2, P])
        tp = sb("tp", [P, 6, T, 1])
        comb = sb("comb", [P, T, X])
        combT = sb("combT", [X, 2, P])

        bank = [ctx.enter_context(nc.psum_tensor(f"bank{i}", [128, 512], F32)) for i in range(8)]

        x_in = [sem(f"x_in{g}") for g in range(G)]
        dst_in, src_in, near_in = sem("dst_in"), sem("src_in"), sem("near_in")
        near_clear = sem("near_clear")
        u_in, gnn_in, mix_in, moe_in = sem("u_in"), sem("gnn_in"), sem("mix_in"), sem("moe_in")
        const_pool, const_ready = sem("const_pool"), sem("const_ready")
        zero_ready, zero_stored = sem("zero_ready"), sem("zero_stored")
        vch, ach, pch = sem("vector_chain"), sem("scalar_chain"), sem("pool_chain")
        stat_ready, root_ready = sem("stat_ready"), sem("root_ready")
        rstd_ready = sem("rstd_ready")
        xn_ready, xn_turned, xT_ready = sem("xn_ready"), sem("xn_turned"), sem("xT_ready")
        zu_done, zu_ready, zu_stored = sem("zu_done"), sem("zu_ready"), sem("zu_stored")
        hot_ready, hot_used = sem("hot_ready"), sem("hot_used")
        tot_ready, base_done = sem("tot_ready"), sem("base_done")
        rows_ready, zfirst_in, zd_scattered = sem("rows_ready"), sem("zfirst_in"), sem("zd_scattered")
        zd_in = [sem(f"zd_in{c}") for c in range(C)]
        zd_free = sem("zd_free")
        zs_in = [sem(f"zs_in{c}") for c in range(C)]
        exp_in, exp_done = sem("exp_in"), sem("exp_done")
        fill_done, scan_done = sem("fill_done"), sem("scan_done")
        state_ready = sem("state_ready")
        state_stored = [sem(f"state_stored{c}") for c in range(C)]
        prep_pe, prep_dve = sem("prep_pe"), sem("prep_dve")
        hw_exp_in, hw_exp = sem("hw_exp_in"), sem("hw_exp")
        kv_done, sq_ready, var_ready = sem("kv_done"), sem("sq_ready"), sem("var_ready")
        std_ready, khv_ready, kvt_step = sem("std_ready"), sem("khv_ready"), sem("kvt_step")
        g0_done, g0_ready, g0_in = sem("g0_done"), sem("g0_ready"), sem("g0_in")
        g0_stored = [sem(f"g0_stored{s}") for s in range(2)]
        up_done, h_ready, down_done, y_used = sem("up_done"), sem("h_ready"), sem("down_done"), sem("y_used")
        fix_in, fix_out = sem("fix_in"), sem("fix_out")
        fix_rows = sem("fix_rows")
        cat_ready, cat_turned, car_ready, car_turned = sem("cat_ready"), sem("cat_turned"), sem("car_ready"), sem("car_turned")
        cexp_in, cexp_done = sem("cexp_in"), sem("cexp_done")
        loc_ready = sem("loc_ready")
        agg_in, agg_ready, agg_turned, aggT_ready = sem("agg_in"), sem("agg_ready"), sem("agg_turned"), sem("aggT_ready")
        ssa_done, x1_ready = sem("ssa_done"), sem("x1_ready")
        xn2_ready, xn2_turned, xT2_ready = sem("xn2_ready"), sem("xn2_turned"), sem("xT2_ready")
        logit_done, pexp_in, pexp_done = sem("logit_done"), sem("pexp_in"), sem("pexp_done")
        comb_ready, comb_turned, combT_ready, bias_done = sem("comb_ready"), sem("comb_turned"), sem("combT_ready"), sem("bias_done")
        ew_in = [sem(f"ew_in{s}") for s in range(2)]
        eup_done, eh_ready, edown_done, acc_step = sem("eup_done"), sem("eh_ready"), sem("edown_done"), sem("acc_step")
        eb_ready = sem("eb_ready")
        out_stored = sem("out_stored")

        block = ctx.enter_context(nc.Block())

        def chain(eng, s):
            count_ = [0]

            def link(ins, wait=True):
                count_[0] += 1
                ins.then_inc(s, 1)
                if wait:
                    eng.wait_ge(s, count_[0])
            return link

        x_v = x.rearrange("(i t) f -> i t f", t=T)
        out_v = out.rearrange("(i t) f -> i t f", t=T)
        g0_v = g0_dram.rearrange("(i t) f -> i t f", t=T)
        zu_v = zu_dram.rearrange("(i t) f -> i t f", t=T)
        zd_v = zd_dram.rearrange("(p c j) f -> p c (j f)", p=P, c=C)
        st_v = st_dram.rearrange("(p c j) f -> p c (j f)", p=P, c=C)
        dst_v = dst.rearrange("(p j) -> p j", j=EP)

        def two(w):
            return w.rearrange("(c p) f -> p c f", p=128)

        @block.sync
        def _(sp):
            for g in range(G):
                sp.dma_start(acc[:, g * GT:(g + 1) * GT, :], x_v[:, g * GT:(g + 1) * GT, :]).then_inc(x_in[g], 16)
            for h in range(2):
                sp.dma_start(U_sb[:, h, :].rearrange("p (k r) -> p k r", r=R),
                             U[:, h * 128:(h + 1) * 128, :].rearrange("k p r -> p k r")).then_inc(u_in, 16)
            sp.dma_start(dst_i[:], dst_v).then_inc(dst_in, 16)
            sp.dma_start(src_i[:], src.rearrange("(p j) -> p j", j=EP)).then_inc(src_in, 16)
            sp.wait_ge(near_clear, 2)
            sp.dma_start(prev_last[1:P, :], dst_v[0:P - 1, EP - 1:EP], allow_slow_non_contiguous=True).then_inc(near_in, 16)
            sp.dma_start(next_first[0:P - 1, :], dst_v[1:P, 0:1], allow_slow_non_contiguous=True).then_inc(near_in, 16)
            sp.wait_ge(zero_ready, 1)
            for c in range(C):
                sp.dma_start(zd_v[:, c, :], zd_buf[0:P, :]).then_inc(zero_stored, 16)
            for g in range(G):
                sp.wait_ge(zu_ready, (g + 1) * GT)
                sp.dma_start(zu_v[:, g * GT:(g + 1) * GT, :], zu_sb[:, g * GT:(g + 1) * GT, :]).then_inc(zu_stored, 16)
            for t in range(T):
                sp.wait_ge(g0_ready, t + 1)
                sp.dma_start(g0_v[:, t, :], g0_out[:, t % 2, :]).then_inc(g0_stored[t % 2], 16)
            sp.wait_ge(zd_scattered, 16 * T)
            for c in range(C):
                if c:
                    sp.wait_ge(zd_free, c)
                sp.dma_start(zd_buf[0:P, :], zd_v[:, c, :]).then_inc(zd_in[c], 16)
                if c >= 1:
                    sp.wait_ge(state_ready, c)
                    sp.dma_start(st_v[:, c - 1, :], edge_buf[0:P, (c - 1) % 2, :]).then_inc(state_stored[c - 1], 16)
            sp.wait_ge(zd_free, C)
            for e in range(2):
                for w, wd in enumerate((ew1, ew2)):
                    sp.dma_start(ew[:, e, w, :, :], two(wd[e])).then_inc(ew_in[e], 16)
            sp.wait_ge(state_ready, C)
            sp.dma_start(st_v[:, C - 1, :], edge_buf[0:P, (C - 1) % 2, :]).then_inc(state_stored[C - 1], 16)
            for c in (C - 2, C - 1):
                sp.wait_ge(state_stored[c], 16)
            for s in range(2):
                sp.wait_ge(g0_stored[s], 16 * ((T + 1 - s) // 2))
            sp.dma_start(g0, g0_v).then_inc(g0_in, 16)
            with sp.Fori(0, X // 2 - 1) as ep:
                for s in range(2):
                    sp.wait_ge(edown_done, ep * (2 * T) + (s + 1) * T)
                    for w, wd in enumerate((ew1, ew2)):
                        sp.dma_start(ew[:, s, w, :, :],
                                     wd[bass.ds(ep * 2 + (s + 2), 1)].rearrange("e (c p) f -> p (e c) f", p=128)).then_inc(ew_in[s], 16)
            for g in range(G):
                sp.wait_ge(acc_step, X * T + (g + 1) * GT)
                sp.dma_start(out_v[:, g * GT:(g + 1) * GT, :], acc[:, g * GT:(g + 1) * GT, :]).then_inc(out_stored, 16)
            sp.wait_ge(out_stored, 16 * G)

        @block.gpsimd
        def _(pool):
            link = chain(pool, pch)
            gp = nc.gpsimd
            gp.memset(prev_last[:], -1).then_inc(near_clear, 1)
            gp.memset(next_first[:], -1).then_inc(near_clear, 1)
            link(gp.memset(ident[:], 0.0), False)
            link(gp.memset(tri[:], 1.0))
            gp.affine_select(out=ident[:], in_=ident[:], compare_op=ALU.not_equal, fill=1.0, base=0,
                             pattern=[[-1, 128]], channel_multiplier=1).then_inc(const_pool, 1)
            gp.affine_select(out=tri[:], in_=tri[:], compare_op=ALU.is_gt, fill=0.0, base=0,
                             pattern=[[1, P]], channel_multiplier=-1).then_inc(const_pool, 1)
            gp.iota(iota_i[:], pattern=[[1, 128]], base=0, channel_multiplier=0).then_inc(const_pool, 1)
            gp.iota(rank8_i[:], pattern=[[-1, X]], base=X, channel_multiplier=0).then_inc(const_pool, 1)
            gp.iota(part_row_i[:], pattern=[[0, 1]], base=0, channel_multiplier=EP).then_inc(const_pool, 1)
            def gather(c):
                for j in range(CE):
                    gp.indirect_dma_start(
                        out=slot[c % 2][:, j, 0:KR], out_offset=None, in_=zu_dram,
                        in_offset=bass.IndirectOffsetOnAxis(ap=src_i[:, c * CE + j:c * CE + j + 1], axis=0)
                    ).then_inc(zs_in[c], 16)

            pool.wait_ge(src_in, 16)
            pool.wait_ge(dst_in, 16)
            pool.wait_ge(zu_stored, 16 * G)
            gp.indirect_dma_start(out=z_first[:], out_offset=None, in_=zu_dram,
                                  in_offset=bass.IndirectOffsetOnAxis(ap=dst_i[:, 0:1], axis=0)).then_inc(zfirst_in, 16)
            gather(0)
            pool.wait_ge(rows_ready, 1)
            pool.wait_ge(zero_stored, 16 * C)
            for t in range(T):
                gp.indirect_dma_start(
                    out=zd_dram, out_offset=bass.IndirectOffsetOnAxis(ap=start_row[:, t:t + 1], axis=0),
                    in_=zu_sb[:, t, :], in_offset=None, bounds_check=E - 1, oob_is_err=False).then_inc(zd_scattered, 16)
            pool.wait_ge(hot_used, C)
            gather(1)
            for c in range(2, C):
                pool.wait_ge(state_stored[c - 2], 16)
                gather(c)
            for c in range(C):
                pool.wait_ge(state_stored[c], 16)
            pool.wait_ge(fix_rows, 1)
            pool.wait_ge(loc_ready, 1)
            gp.indirect_dma_start(out=s_last[:], out_offset=None, in_=st_dram,
                                  in_offset=bass.IndirectOffsetOnAxis(ap=fix_row_i[:, 0:1], axis=0)).then_inc(fix_in, 16)
            pool.wait_ge(fix_rows, 2)
            gp.indirect_dma_start(
                out=st_dram, out_offset=bass.IndirectOffsetOnAxis(ap=fix_row_i[:, 1:2], axis=0),
                in_=s_last[:], in_offset=None, bounds_check=E - 1, oob_is_err=False).then_inc(fix_out, 16)
            pool.wait_ge(fix_out, 16)
            pool.wait_ge(zd_scattered, 16 * T)
            for t in range(T):
                gp.indirect_dma_start(out=agg[:, t, :], out_offset=None, in_=st_dram,
                                      in_offset=bass.IndirectOffsetOnAxis(ap=end_row[:, t:t + 1], axis=0)).then_inc(agg_in, 16)

        @block.scalar
        def _(act):
            sc = nc.scalar
            for h in range(K):
                act.dma_start(hw_own[h * R:(h + 1) * R, :], head_w[h:h + 1].rearrange("(a b) -> a b", a=1).to_broadcast([R, 1])).then_inc(gnn_in, 16)
            act.dma_start(hw_all[:], head_w.rearrange("(a k) -> a k", a=1).to_broadcast([KR, K])).then_inc(gnn_in, 16)
            act.dma_start(D_sb[:], two(Dmat)).then_inc(gnn_in, 16)
            act.dma_start(wqkv[:], two(w_qkv)).then_inc(mix_in, 16)
            act.dma_start(bqkv_row[:], b_qkv.rearrange("(a f) -> a f", a=1)).then_inc(mix_in, 16)
            for h in range(H):
                act.dma_start(bq_col[(h % 4) * HC:(h % 4 + 1) * HC, h // 4:h // 4 + 1],
                              b_qkv[h * 3 * HC:h * 3 * HC + HC].rearrange("(a b) -> a b", b=1)).then_inc(mix_in, 16)
            for row, v in ((gk_row, kln_g), (bk_row, kln_b)):
                act.dma_start(row[:, 0, :], v.rearrange("(a f) -> a f", a=1).to_broadcast([128, HC])).then_inc(mix_in, 16)
            for col, v in ((gv_col, vln_g), (bv_col, vln_b)):
                for q in range(4):
                    act.dma_start(col[q * HC:(q + 1) * HC, :], v.rearrange("(a b) -> a b", b=1)).then_inc(mix_in, 16)
            act.dma_start(w1_sb[:], two(w1)).then_inc(mix_in, 16)
            act.dma_start(w2_sb[:], two(w2)).then_inc(mix_in, 16)
            act.dma_start(b2_row[:], b2.rearrange("(a f) -> a f", a=1)).then_inc(mix_in, 16)
            for m in range(2):
                act.dma_start(b1_col[:, m:m + 1], b1[m * 128:(m + 1) * 128].rearrange("(a b) -> a b", b=1)).then_inc(mix_in, 16)
            act.dma_start(rw_in[:], router_w).then_inc(moe_in, 16)
            act.dma_start(eb1_in[:], eb1.rearrange("e (m p) -> (e m) p", p=128)).then_inc(moe_in, 16)
            act.dma_start(eb2_sb[:], eb2).then_inc(moe_in, 16)

            def layernorm_roots(n):
                act.wait_ge(stat_ready, n + 1)
                sc.activation(sd[:, (n % G) * GT:(n % G + 1) * GT, :], mv[:, (n % G) * GT:(n % G + 1) * GT, 1:2], ACT.Sqrt).then_inc(root_ready, 1)

            def evict_zu(t):
                act.wait_ge(zu_done, t + 1)
                sc.activation(zu_sb[:, t, :], bank[2 + t % 2][0:P, 0:KR], ACT.Copy).then_inc(zu_ready, 1)

            layernorm_roots(0)
            for t in range(T):
                if t % GT == 0 and t // GT + 1 < G:
                    layernorm_roots(t // GT + 1)
                act.wait_ge(xn_turned, t + 1)
                sc.activation(xT[:, :, t * P:(t + 1) * P],
                              bank[t % 2][:, 0:2 * P].rearrange("p (c n) -> p c n", c=2), ACT.Copy).then_inc(xT_ready, 1)
                if t >= 1:
                    evict_zu(t - 1)
            evict_zu(T - 1)
            act.wait_ge(hw_exp_in, 1)
            sc.activation(hw_all[:], hw_all[:], ACT.Exp, bias=hw_m[:, 1:2]).then_inc(hw_exp, 1)
            sc.activation(hw_own[:], hw_own[:], ACT.Exp, bias=hw_m[:, 1:2]).then_inc(hw_exp, 1)

            def kv_root(t):
                act.wait_ge(var_ready, t + 1)
                sc.activation(ss[:, t % 3, :], ss[:, t % 3, :], ACT.Sqrt).then_inc(std_ready, 1)

            def g0_evict(t):
                act.wait_ge(g0_done, t + 1)
                if t >= 2:
                    act.wait_ge(g0_stored[t % 2], 16 * (t // 2))
                sc.activation(g0_out[:, t % 2, :], bank[2 + t % 2][0:P, 0:D], ACT.Copy).then_inc(g0_ready, 1)

            for t in range(T):
                act.wait_ge(kv_done, t + 1)
                if t >= 2:
                    act.wait_ge(var_ready, t - 1)
                sc.activation(sq[:, t % 2, :], bank[t % 2][0:P, :], ACT.Square).then_inc(sq_ready, 1)
                if t >= 1:
                    kv_root(t - 1)
                g0_evict(t)
            kv_root(T - 1)

            def edge_exps(c):
                act.wait_ge(exp_in, 2 * c + 1)
                sc.activation(weight[:], dl[:], ACT.Exp, scale=LOGIT_SCALE).then_inc(exp_done, 1)
                act.wait_ge(exp_in, 2 * c + 2)
                sc.activation(rescale[:], dm[:], ACT.Exp, scale=LOGIT_SCALE).then_inc(exp_done, 1)

            edge_exps(0)
            for g in range(G):
                for q in range(4):
                    u = g * 4 + q
                    m, (o, w) = q // 2, HALF[q % 2]
                    act.wait_ge(up_done, u + 1)
                    sc.activation(hT[:, g % 2, m, o:o + w], bank[q][:, 0:w], ACT.Gelu, bias=bh_col[:, m:m + 1]).then_inc(h_ready, 1)
            for c in range(1, C):
                edge_exps(c)
            for n in range(4):
                act.wait_ge(cexp_in, n + 1)
                if n < 2:
                    buf = rows[:, n, 0:P]
                else:
                    buf = ew_r[:, n - 2, :]
                sc.activation(buf, buf, ACT.Exp, scale=LOGIT_SCALE).then_inc(cexp_done, 1)
            for t in range(T):
                act.wait_ge(agg_turned, t + 1)
                if t >= 2:
                    act.wait_ge(ssa_done, t - 1)
                sc.activation(aggT[:, t % 2, :], bank[t % 2][0:KR, 0:P], ACT.Copy).then_inc(aggT_ready, 1)
            for g in range(G):
                layernorm_roots(G + g)
            for t in range(T):
                act.wait_ge(xn2_turned, t + 1)
                sc.activation(xT[:, :, t * P:(t + 1) * P],
                              bank[4 + t % 2][:, 0:2 * P].rearrange("p (c n) -> p c n", c=2), ACT.Copy).then_inc(xT2_ready, 1)
            act.wait_ge(pexp_in, 1)
            sc.activation(pr[:], lg[:], ACT.Exp).then_inc(pexp_done, 1)
            for t in range(T):
                act.wait_ge(comb_turned, t + 1)
                if t >= 2:
                    act.wait_ge(bias_done, t - 1)
                sc.activation(combT[:, t % 2, :], bank[t % 2][0:X, 0:P], ACT.Copy).then_inc(combT_ready, 1)
            NU = 2 * G * 4
            with act.Fori(0, X // 2) as ep:
                act.wait_ge(eb_ready, ep + 1)
                for n in range(2 * G):
                    s, g = n // G, n % G
                    for q in range(4):
                        m, (o, w) = q // 2, HALF[q % 2]
                        act.wait_ge(eup_done, ep * NU + (n * 4 + q + 1))
                        sc.activation(hT[:, n % 2, m, o:o + w], bank[q][:, 0:w], ACT.Gelu,
                                      bias=eb_pair[:, s * 2 + m:s * 2 + m + 1]).then_inc(eh_ready, 1)

        @block.tensor
        def _(pe):
            mm = nc.tensor.matmul
            tr = nc.tensor.transpose
            pe.wait_ge(const_pool, 2)
            pe.wait_ge(u_in, 32)

            def zu(t):
                pe.wait_ge(xT_ready, t + 1)
                if t >= 2:
                    pe.wait_ge(zu_ready, t - 1)
                for c in range(2):
                    last = mm(bank[2 + t % 2][0:P, 0:KR], xT[:, c, t * P:(t + 1) * P], U_sb[:, c, :], start=c == 0, stop=c == 1)
                last.then_inc(zu_done, 1)

            for t in range(T):
                pe.wait_ge(xn_ready, t + 1)
                if t >= 2:
                    pe.wait_ge(xT_ready, t - 1)
                for c in range(2):
                    last = tr(bank[t % 2][:, c * P:(c + 1) * P], xn[:, t % 3, c * 128:(c + 1) * 128], ident[0:P, 0:P])
                last.then_inc(xn_turned, 1)
                if t >= 1:
                    zu(t - 1)
            zu(T - 1)

            pe.wait_ge(const_ready, 1)
            mm(bank[4][0:P, 0:T], zero_b[:, :], zero_b[:, 0:T], start=True, stop=False)
            for c in range(C):
                pe.wait_ge(hot_ready, c + 1)
                with pe.Fori(0, CE - 5, 5) as j:
                    for q in range(5):
                        mm(bank[4][0:P, 0:T], oh_i[:, bass.ds(j + q, 1), :].rearrange("p a b -> p (a b)"),
                           oh_t[:, bass.ds(j + q, 1), :].rearrange("p a b -> p (a b)"), start=False, stop=False)
                for q in range(5):
                    last = mm(bank[4][0:P, 0:T], oh_i[:, CE - 5 + q, :], oh_t[:, CE - 5 + q, :], start=False, stop=c == C - 1 and q == 4)
                last.then_inc(hot_used, 1)
            pe.wait_ge(tot_ready, 1)
            mm(bank[4][0:P, T:T + 1], tri[:, :], incl[:, T - 1:T], start=True, stop=True).then_inc(base_done, 1)

            pe.wait_ge(gnn_in, 16 * (K + 2))
            pe.wait_ge(const_ready, 1)
            for a in range(2):
                for c in range(2):
                    last = mm(bank[5][:, a * D:(a + 1) * D], D_sb[:, c, a * 128:(a + 1) * 128], D_sb[:, c, :], start=c == 0, stop=c == 1)
            last.then_inc(prep_pe, 1)
            pe.wait_ge(prep_dve, 1)
            for a in range(2):
                for c in range(2):
                    last = mm(bank[6][:, a * D:(a + 1) * D], Q_sb[:, c, a * 128:(a + 1) * 128], D_sb[:, c, :], start=c == 0, stop=c == 1)
            last.then_inc(prep_pe, 1)
            pe.wait_ge(prep_dve, 2)
            for c in range(2):
                last = mm(bank[5][0:KR, 0:D], U_sb[:, c, :], M_sb[:, c, :], start=c == 0, stop=c == 1)
            last.then_inc(prep_pe, 1)
            pe.wait_ge(prep_dve, 4)
            for g in range(2):
                for c in range(2):
                    last = tr(bank[6][:, g * D + c * 128:g * D + (c + 1) * 128], wq[:, c, g * 128:(g + 1) * 128], ident[:, :])
            last.then_inc(prep_pe, 1)
            pe.wait_ge(moe_in, 48)
            for c in range(2):
                tr(bank[7][:, c * X:(c + 1) * X], rw_in[:, c * 128:(c + 1) * 128], ident[0:X, 0:X])
            tr(bank[7][:, 32:32 + 2 * X], eb1_in[:, :], ident[0:2 * X, 0:2 * X]).then_inc(prep_pe, 1)

            pe.wait_ge(prep_dve, 6)

            def kvt(t):
                pe.wait_ge(khv_ready, t + 1)
                for g in range(2):
                    kg = khv[:, t % 2, g * 128:(g + 1) * 128]
                    vg = khv[:, t % 2, D + g * 128:D + (g + 1) * 128]
                    first = t == 0 and g == 0
                    mm(bank[5][:, g * D:g * D + 128], vg, kg, start=first, stop=t == T - 1, skip_group_check=True)
                    mm(bank[5][:, g * D + 128:g * D + 129], vg, ones[:, 0:1], start=False, stop=t == T - 1, skip_group_check=True)
                mm(bank[6][:, 0:D], ones[:, :], khv[:, t % 2, 0:D], start=t == 0, stop=t == T - 1).then_inc(kvt_step, 1)

            for t in range(T):
                if t >= 2:
                    pe.wait_ge(khv_ready, t - 1)
                for c in range(2):
                    mm(bank[t % 2][0:P, :], xT[:, c, t * P:(t + 1) * P], wkv[:, c, :], start=c == 0, stop=False)
                mm(bank[t % 2][0:P, :], ones[0:1, 0:P], bkv_row[:, :], start=False, stop=True).then_inc(kv_done, 1)
                if t >= 2:
                    pe.wait_ge(g0_ready, t - 1)
                for c in range(2):
                    last = mm(bank[2 + t % 2][0:P, 0:D], xT[:, c, t * P:(t + 1) * P], M_sb[:, c, :], start=c == 0, stop=c == 1)
                last.then_inc(g0_done, 1)
                if t >= 1:
                    kvt(t - 1)
            kvt(T - 1)
            pe.wait_ge(prep_dve, 7)
            for g in range(2):
                last = mm(bank[7][:, g * D:(g + 1) * D], KVT[:, g, :], w1_sb[:, g, :], start=True, stop=True)
            last.then_inc(prep_pe, 1)
            pe.wait_ge(prep_dve, 8)
            for c in range(2):
                for g in range(2):
                    mm(bank[5][:, c * D:(c + 1) * D], WqT[:, g, c * 128:(c + 1) * 128], B_sb[:, g, :], start=g == 0, stop=g == 1)
            for m in range(2):
                for g in range(2):
                    last = mm(bank[6][:, m:m + 1], B_sb[:, g, m * 128:(m + 1) * 128], bq_col[:, g:g + 1], start=g == 0, stop=g == 1)
            last.then_inc(prep_pe, 1)
            pe.wait_ge(prep_dve, 9)

            def mix_up(g):
                for q in range(4):
                    m, (o, w) = q // 2, HALF[q % 2]
                    if g:
                        pe.wait_ge(h_ready, (g - 1) * 4 + q + 1)
                    for c in range(2):
                        last = mm(bank[q][:, 0:w], A_sb[:, c, m * 128:(m + 1) * 128],
                                  xT[:, c, g * COLS + o:g * COLS + o + w], start=c == 0, stop=c == 1)
                    last.then_inc(up_done, 1)

            def mix_down(g):
                pe.wait_ge(h_ready, (g + 1) * 4)
                for u in range(GT):
                    y = g * GT + u
                    if y >= 4:
                        pe.wait_ge(y_used, y - 3)
                    for m in range(2):
                        mm(bank[4 + y % 4][0:P, 0:D], hT[:, g % 2, m, u * P:(u + 1) * P], w2_sb[:, m, :], start=m == 0, stop=False)
                    mm(bank[4 + y % 4][0:P, 0:D], ones[0:1, 0:P], b2_row[:, :], start=False, stop=True).then_inc(down_done, 1)

            mix_up(0)
            for g in range(G):
                if g + 1 < G:
                    mix_up(g + 1)
                mix_down(g)

            pe.wait_ge(cat_ready, 1)
            pe.wait_ge(y_used, T)
            for n in range(3):
                last = tr(bank[n][0:KR + K, 0:P], cat[:, n, :], ident[0:P, 0:P])
            last.then_inc(cat_turned, 1)
            pe.wait_ge(car_ready, 1)
            for n in range(2):
                last = tr(bank[4 + n][0:P, 0:KR + K], rows[:, 2 + n, 0:P], ident[0:KR + K, 0:KR + K])
            last.then_inc(car_turned, 1)

            def ssa(t):
                pe.wait_ge(aggT_ready, t + 1)
                if t >= 2:
                    pe.wait_ge(x1_ready, t - 1)
                mm(bank[2 + t % 2][0:P, 0:D], aggT[:, t % 2, :], UM_sb[:, :], start=True, stop=True).then_inc(ssa_done, 1)

            pe.wait_ge(agg_ready, 1)
            for t in range(T):
                if t >= 2:
                    pe.wait_ge(aggT_ready, t - 1)
                tr(bank[t % 2][0:KR, 0:P], agg[:, t, 0:KR], ident[0:P, 0:P]).then_inc(agg_turned, 1)
                if t >= 1:
                    ssa(t - 1)
            ssa(T - 1)

            def route(t):
                pe.wait_ge(xT2_ready, t + 1)
                for c in range(2):
                    last = mm(bank[6][0:P, t * X:(t + 1) * X], xT[:, c, t * P:(t + 1) * P], rwT[:, c, :], start=c == 0, stop=c == 1)
                last.then_inc(logit_done, 1)

            for t in range(T):
                pe.wait_ge(xn2_ready, t + 1)
                if t >= 2:
                    pe.wait_ge(xT2_ready, t - 1)
                for c in range(2):
                    last = tr(bank[4 + t % 2][:, c * P:(c + 1) * P], xn[:, t % 3, c * 128:(c + 1) * 128], ident[0:P, 0:P])
                last.then_inc(xn2_turned, 1)
                if t >= 1:
                    route(t - 1)
            route(T - 1)
            pe.wait_ge(comb_ready, 1)

            def moe_bias(t):
                pe.wait_ge(combT_ready, t + 1)
                if t >= 2:
                    pe.wait_ge(acc_step, t - 1)
                mm(bank[2 + t % 2][0:P, 0:D], combT[:, t % 2, :], eb2_sb[:, :], start=True, stop=True).then_inc(bias_done, 1)

            for t in range(T):
                if t >= 2:
                    pe.wait_ge(combT_ready, t - 1)
                tr(bank[t % 2][0:X, 0:P], comb[:, t, :], ident[0:P, 0:P]).then_inc(comb_turned, 1)
                if t >= 1:
                    moe_bias(t - 1)
            moe_bias(T - 1)
            pe.wait_ge(acc_step, T)

            NU = 2 * G * 4
            with pe.Fori(0, X // 2) as ep:
                def up(n):
                    s, g = n // G, n % G
                    if g == 0:
                        pe.wait_ge(ew_in[s], (ep + 1) * 32)
                    for q in range(4):
                        m, (o, w) = q // 2, HALF[q % 2]
                        if n:
                            pe.wait_ge(eh_ready, ep * NU + ((n - 1) * 4 + q + 1))
                        for c in range(2):
                            last = mm(bank[q][:, 0:w], ew[:, s, 0, c, m * 128:(m + 1) * 128],
                                      xT[:, c, g * COLS + o:g * COLS + o + w], start=c == 0, stop=c == 1)
                        last.then_inc(eup_done, 1)

                def down(n):
                    s, g = n // G, n % G
                    pe.wait_ge(eh_ready, ep * NU + (n + 1) * 4)
                    for u in range(GT):
                        y = n * GT + u
                        pe.wait_ge(acc_step, ep * (2 * T) + (T + y - 3))
                        for m in range(2):
                            last = mm(bank[4 + y % 4][0:P, 0:D], hT[:, n % 2, m, u * P:(u + 1) * P], ew[:, s, 1, m, :],
                                      start=m == 0, stop=m == 1)
                        last.then_inc(edown_done, 1)

                up(0)
                for n in range(2 * G):
                    if n + 1 < 2 * G:
                        up(n + 1)
                    down(n)

        @block.vector
        def _(dve):
            v = nc.vector
            link = chain(dve, vch)
            v.memset(zd_buf[0:P, :], 0.0).then_inc(zero_ready, 1)

            def layernorm_stats(g, n):
                for u in range(GT):
                    link(v.bn_stats(stats[:, g * GT + u, :], acc[:, g * GT + u, :]), u == GT - 1)
                for u in range(GT):
                    link(v.bn_aggr(mv[:, g * GT + u, :], stats[:, g * GT + u, :]), u == GT - 1)
                part = mv[:, g * GT:(g + 1) * GT, 1:2]
                v.tensor_scalar(part, part, EPS, None, ALU.add).then_inc(stat_ready, 1)

            def reciprocal_roots(g, n):
                dve.wait_ge(root_ready, n + 1)
                link(v.reciprocal(rstd[:, g * GT:(g + 1) * GT, :], sd[:, g * GT:(g + 1) * GT, :]))

            def normalise(t, ready, turned):
                if t >= 3:
                    dve.wait_ge(turned, t - 2)
                v.tensor_scalar(xn[:, t % 3, :], acc[:, t, :], mv[:, t, 0:1], rstd[:, t, :], ALU.subtract, ALU.mult).then_inc(ready, 1)

            dve.wait_ge(x_in[0], 16)
            layernorm_stats(0, 0)
            for g in range(G):
                if g + 1 < G:
                    dve.wait_ge(x_in[g + 1], 16)
                    layernorm_stats(g + 1, g + 1)
                reciprocal_roots(g, g)
                for u in range(GT):
                    t = g * GT + u
                    normalise(t, xn_ready, xn_turned)
                    dve.wait_ge(xn_ready, t + 1)
                    link(v.tensor_tensor(acc[:, t, :], acc[:, t, :], xn[:, t % 3, :], ALU.add), u == GT - 1)

            dve.wait_ge(const_pool, 5)
            link(v.memset(ones[:], 1.0), False)
            link(v.memset(zero_b[:], 0.0), False)
            link(v.tensor_copy(iota_f[:], iota_i[:]), False)
            link(v.tensor_copy(rank8[:, 0, :], rank8_i[:]), False)
            link(v.tensor_copy(part_row[:], part_row_i[:]), False)
            link(v.memset(eye2[:], 0.0))
            for c in range(2):
                link(v.tensor_copy(eye2[:, c, c * 128:(c + 1) * 128], ident[:, :]), c == 1)
            v.memset(KVT[:], 0.0).then_inc(const_ready, 1)
            dve.wait_ge(dst_in, 16)
            dve.wait_ge(near_in, 32)
            link(v.tensor_copy(dst_f[:], dst_i[:]))
            link(v.tensor_scalar(quo_i[:], dst_f[:], 1.0 / T, -(T - 1) / 2.0 / T, ALU.mult, ALU.add))
            link(v.tensor_copy(quo_f[:], quo_i[:]))
            for lim, op, sign in ((-0.5, ALU.is_lt, -1.0), (T - 0.5, ALU.is_gt, 1.0)):
                link(v.scalar_tensor_tensor(rem_f[:], quo_f[:], -float(T), dst_f[:], ALU.mult, ALU.add))
                link(v.tensor_scalar(fix_f, rem_f[:], lim, sign, op, ALU.mult))
                link(v.tensor_tensor(quo_f[:], quo_f[:], fix_f, ALU.add))
            link(v.scalar_tensor_tensor(rem_f[:], quo_f[:], -float(T), dst_f[:], ALU.mult, ALU.add))
            link(v.tensor_copy(quo_b[:, :, 0], quo_f[:]), False)
            link(v.tensor_copy(rem_b[:, :, 0], rem_f[:]))
            for c in range(C):
                if c:
                    dve.wait_ge(hot_used, c)
                link(v.tensor_tensor(oh_i, quo_b[:, c * CE:(c + 1) * CE, :].to_broadcast([P, CE, P]),
                                     iota_f[0:P, 0:P].rearrange("p (a b) -> p a b", a=1).to_broadcast([P, CE, P]), ALU.is_equal), False)
                v.tensor_tensor(oh_t[:], rem_b[:, c * CE:(c + 1) * CE, :].to_broadcast([P, CE, T]),
                                iota_f[0:P, 0:T].rearrange("p (a b) -> p a b", a=1).to_broadcast([P, CE, T]), ALU.is_equal).then_inc(hot_ready, 1)
            link(v.tensor_copy(edge_f[:, 0:1], prev_last[:]), False)
            link(v.tensor_copy(edge_f[:, 1:2], next_first[:]))
            cont_in, cont_out, whole, joins, pos, tmp = (cont[:, n:n + 1] for n in range(6))
            link(v.tensor_tensor(cont_in, edge_f[:, 0:1], dst_f[:, 0:1], ALU.is_equal), False)
            link(v.tensor_tensor(cont_out, edge_f[:, 1:2], dst_f[:, EP - 1:EP], ALU.is_equal), False)
            link(v.tensor_tensor(same[:, 1:EP, 0], dst_f[:, 1:EP], dst_f[:, 0:EP - 1], ALU.is_equal))
            link(v.tensor_copy(same[:, 0, :], cont_in))
            link(v.tensor_scalar(forget[:, :, 0], same[:, :, 0], -1.0, BIG, ALU.add, ALU.mult))
            link(v.memset(forget[:, 0, :], -BIG), False)
            link(v.memset(first_run[:, 0:1], 1.0), False)
            link(v.tensor_tensor_scan(first_run[:, 1:EP], same[:, 1:EP, 0], same[:, 1:EP, 0], 1.0, ALU.mult, ALU.mult))
            link(v.tensor_reduce(pos, first_run[:, 1:EP], AX.X, ALU.add), False)
            link(v.tensor_copy(whole, first_run[:, EP - 1:EP]))
            link(v.tensor_tensor(joins, whole, cont_in, ALU.mult), False)
            link(v.tensor_tensor(pos, pos, part_row[:], ALU.add), False)
            link(v.tensor_tensor(tmp, whole, cont_out, ALU.mult))
            link(v.tensor_scalar(tmp, tmp, -1.0, 1.0, ALU.mult, ALU.add))
            link(v.tensor_tensor(tmp, tmp, cont_in, ALU.mult))
            link(v.tensor_copy(fix_row_i[:, 0:1], pos), False)
            link(v.tensor_scalar(tmp, tmp, -OUT_OF_RANGE, OUT_OF_RANGE, ALU.mult, ALU.add))
            link(v.tensor_tensor(tmp, tmp, pos, ALU.add))
            v.tensor_copy(fix_row_i[:, 1:2], tmp).then_inc(fix_rows, 1)
            dve.wait_ge(hot_used, C)
            link(v.tensor_copy(count[:], bank[4][0:P, 0:T]))
            link(v.memset(empty[:], 1.0))
            v.tensor_tensor_scan(incl[:], empty[:], count[:], 0.0, ALU.mult, ALU.add).then_inc(tot_ready, 1)
            link(v.tensor_scalar(has_edge[:, :, 0], count[:], 1.0, None, ALU.min), False)
            dve.wait_ge(base_done, 1)
            link(v.tensor_copy(row_base[:], bank[4][0:P, T:T + 1]))
            link(v.tensor_scalar(ends[:], incl[:], row_base[:], None, ALU.add))
            link(v.tensor_tensor(starts[:], ends[:], count[:], ALU.subtract), False)
            link(v.tensor_scalar(empty[:], has_edge[:, :, 0], -OUT_OF_RANGE, OUT_OF_RANGE, ALU.mult, ALU.add), False)
            link(v.tensor_scalar(ends[:], ends[:], -1.0, 0.0, ALU.add, ALU.max))
            link(v.tensor_tensor(starts[:], starts[:], empty[:], ALU.add), False)
            link(v.tensor_copy(end_row[:], ends[:]))
            v.tensor_copy(start_row[:], starts[:]).then_inc(rows_ready, 1)

            dve.wait_ge(gnn_in, 16 * (K + 2))
            link(v.tensor_reduce(hw_m[:, 0:1], hw_all[:], AX.X, ALU.max))
            v.tensor_scalar(hw_m[:, 1:2], hw_m[:, 0:1], -1.0, None, ALU.mult).then_inc(hw_exp_in, 1)
            dve.wait_ge(prep_pe, 1)
            v.scalar_tensor_tensor(Q_sb[:], bank[5][:, :].rearrange("p (c f) -> p c f", c=2), -1.0, eye2[:], ALU.mult, ALU.add).then_inc(prep_dve, 1)
            dve.wait_ge(prep_pe, 2)
            link(v.scalar_tensor_tensor(M_sb[:], bank[6][:, :].rearrange("p (c f) -> p c f", c=2), 0.5, eye2[:], ALU.mult, ALU.add))
            v.tensor_scalar(M_sb[:], M_sb[:], 0.5, None, ALU.mult).then_inc(prep_dve, 1)
            dve.wait_ge(hw_exp, 2)
            link(v.tensor_reduce(hw_m[:, 2:3], hw_all[:], AX.X, ALU.add))
            link(v.reciprocal(hw_m[:, 3:4], hw_m[:, 2:3]))
            dve.wait_ge(prep_pe, 3)
            v.tensor_scalar(UM_sb[:], bank[5][0:KR, 0:D], hw_own[:], hw_m[:, 3:4], ALU.mult, ALU.mult).then_inc(prep_dve, 1)
            dve.wait_ge(mix_in, 16 * 25)
            for c in range(2):
                wh = wqkv[:, c, :].rearrange("p (h s f) -> p h s f", s=3, f=HC)
                for s in range(2):
                    link(v.tensor_reduce(wmean[:, c, s * H:(s + 1) * H], wh[:, :, 1 + s, :], AX.X, ALU.add), False)
            bh = bqkv_row[:, :].rearrange("p (h s f) -> p h s f", s=3, f=HC)
            for s in range(2):
                link(v.tensor_reduce(bmean[:, s * H:(s + 1) * H], bh[:, :, 1 + s, :], AX.X, ALU.add), s == 1)
            link(v.tensor_scalar(wmean[:], wmean[:], -1.0 / HC, None, ALU.mult), False)
            link(v.tensor_scalar(bmean[:], bmean[:], -1.0 / HC, None, ALU.mult))
            for s in range(2):
                for c in range(2):
                    wh = wqkv[:, c, :].rearrange("p (h s f) -> p h s f", s=3, f=HC)
                    link(v.tensor_tensor(wkv[:, c, s * D:(s + 1) * D].rearrange("p (h f) -> p h f", f=HC), wh[:, :, 1 + s, :],
                                         wmean[:, c, s * H:(s + 1) * H].rearrange("p (h a) -> p h a", a=1).to_broadcast([128, H, HC]), ALU.add), False)
                link(v.tensor_tensor(bkv_row[:, s * D:(s + 1) * D].rearrange("p (h f) -> p h f", f=HC), bh[:, :, 1 + s, :],
                                     bmean[:, s * H:(s + 1) * H].rearrange("p (h a) -> p h a", a=1).to_broadcast([1, H, HC]), ALU.add), s == 1)
            for c in range(2):
                wh = wqkv[:, c, :].rearrange("p (h s f) -> p h s f", s=3, f=HC)
                last = v.tensor_copy(wq[:, c, :].rearrange("p (h f) -> p h f", f=HC), wh[:, :, 0, :])
            last.then_inc(prep_dve, 1)
            dve.wait_ge(prep_pe, 4)
            link(v.tensor_copy(WqT[:], bank[6][:, :].rearrange("p (c f) -> p c f", c=2)), False)
            dve.wait_ge(prep_pe, 5)
            v.tensor_copy(rwT[:], bank[7][:, 0:2 * X].rearrange("p (c f) -> p c f", c=2)).then_inc(prep_dve, 1)
            v.tensor_copy(eb1_col[:], bank[7][:, 32:32 + 2 * X]).then_inc(prep_dve, 1)

            def kv_scale(t):
                dve.wait_ge(std_ready, t + 1)
                link(v.reciprocal(ss[:, t % 3, :], ss[:, t % 3, :]))
                if t >= 2:
                    dve.wait_ge(kvt_step, t - 1)
                v.tensor_tensor(khv[:, t % 2, :].rearrange("p (h f) -> p h f", f=HC),
                                bank[t % 2][0:P, :].rearrange("p (h f) -> p h f", f=HC),
                                ss[:, t % 3, :].rearrange("p (h a) -> p h a", a=1).to_broadcast([P, 2 * H, HC]), ALU.mult).then_inc(khv_ready, 1)

            for t in range(T):
                dve.wait_ge(sq_ready, t + 1)
                link(v.tensor_reduce(ss[:, t % 3, :], sq[:, t % 2, :].rearrange("p (h f) -> p h f", f=HC), AX.X, ALU.add))
                v.tensor_scalar(ss[:, t % 3, :], ss[:, t % 3, :], 1.0 / HC, EPS, ALU.mult, ALU.add).then_inc(var_ready, 1)
                if t >= 1:
                    kv_scale(t - 1)
            kv_scale(T - 1)
            dve.wait_ge(kvt_step, T)
            for g in range(2):
                b5 = bank[5][:, g * D:g * D + 129]
                link(v.tensor_scalar(kvt_a[:], bank[6][:, g * 128:(g + 1) * 128], bv_col[:], None, ALU.mult), False)
                link(v.tensor_scalar(kvt_c[:], b5[:, 128:129], gv_col[:], None, ALU.mult), False)
                link(v.tensor_scalar(kvt_b[:, 0:1], bv_col[:], float(N), None, ALU.mult))
                link(v.tensor_tensor(kvt_c[:], kvt_c[:], kvt_b[:, 0:1], ALU.add), False)
                link(v.scalar_tensor_tensor(kvt_a[:], b5[:, 0:128], gv_col[:], kvt_a[:], ALU.mult, ALU.add))
                a4, b4 = (q[:, :].rearrange("p (h f) -> p h f", f=HC) for q in (kvt_a, kvt_b))
                link(v.tensor_tensor(a4, a4, gk_row[:, :, :].to_broadcast([128, 4, HC]), ALU.mult), False)
                link(v.tensor_scalar(b4, bk_row[:, :, :].to_broadcast([128, 4, HC]), kvt_c[:], None, ALU.mult))
                link(v.tensor_tensor(kvt_a[:], kvt_a[:], kvt_b[:], ALU.add))
                for q in range(4):
                    blk = slice(q * HC, (q + 1) * HC)
                    last = v.tensor_copy(KVT[blk, g, blk], kvt_a[blk, blk])
                if g == 0:
                    link(last)
            last.then_inc(prep_dve, 1)
            dve.wait_ge(prep_pe, 6)
            v.tensor_scalar(B_sb[:], bank[7][:, :].rearrange("p (c f) -> p c f", c=2), 1.0 / N, None, ALU.mult).then_inc(prep_dve, 1)
            dve.wait_ge(prep_pe, 7)
            link(v.tensor_tensor(A_sb[:], bank[5][:, :].rearrange("p (c f) -> p c f", c=2), w1_sb[:], ALU.add), False)
            v.tensor_tensor(bh_col[:], bank[6][:, 0:2], b1_col[:], ALU.add).then_inc(prep_dve, 1)

            def fill_rows(c):
                dve.wait_ge(zd_in[c], 16)
                init = z_first if c == 0 else z_last
                with dve.Fori(0, K) as k:
                    for r in range(R):
                        col = zd[:, :, bass.ds(k * R + r, 1)].rearrange("p j a -> p (j a)")
                        last = v.tensor_tensor_scan(col, same[:, c * CE:(c + 1) * CE, 0], col, init[:, bass.ds(k * R + r, 1)], ALU.mult, ALU.add)
                    last.then_inc(fill_done, 1)
                dve.wait_ge(fill_done, (c + 1) * K)
                link(v.tensor_copy(z_last[:], zd[:, CE - 1, :]))

            def edge_chunk(c):
                st = slot[c % 2]
                cs = slice(c * CE, (c + 1) * CE)
                dve.wait_ge(zs_in[c], 16 * CE)
                link(v.tensor_tensor(zd, zd, st[:, :, 0:KR], ALU.mult))
                v.tensor_reduce(logit[:], zd.rearrange("p j (k r) -> p j k r", r=R), AX.X, ALU.add).then_inc(zd_free, 1)
                dve.wait_ge(zd_free, c + 1)
                for k in range(K):
                    link(v.tensor_tensor_scan(st[:, :, KR + K + k], forget[:, cs, 0], logit[:, :, k],
                                              0.0 if c == 0 else s_last[:, KR + K + k:KR + K + k + 1], ALU.add, ALU.max), k == K - 1)
                m = st[:, :, KR + K:SW]
                v.tensor_tensor(dl[:], logit[:], m, ALU.subtract).then_inc(exp_in, 1)
                link(v.tensor_tensor(dm[:, 1:CE, :], m[:, 0:CE - 1, :], m[:, 1:CE, :], ALU.subtract), False)
                if c == 0:
                    link(v.memset(dm[:, 0:1, :], 0.0))
                else:
                    link(v.tensor_tensor(dm[:, 0:1, :], s_last[:, KR + K:SW].rearrange("p (a k) -> p a k", a=1), m[:, 0:1, :], ALU.subtract))
                v.tensor_tensor(dm[:], dm[:], forget[:, cs, :].to_broadcast([P, CE, K]), ALU.add).then_inc(exp_in, 1)
                dve.wait_ge(exp_done, 2 * c + 2)
                link(v.tensor_copy(st[:, :, KR:KR + K], weight[:]), False)
                z4 = st[:, :, 0:KR].rearrange("p j (k r) -> p j k r", r=R)
                link(v.tensor_tensor(z4, z4, weight[:].rearrange("p j (k a) -> p j k a", a=1).to_broadcast([P, CE, K, R]), ALU.mult))
                def state_scan(col, fac, init):
                    return v.tensor_tensor_scan(col, fac, col, init, ALU.mult, ALU.add)
                with dve.Fori(0, K) as k:
                    fac = rescale[:, :, bass.ds(k, 1)].rearrange("p j a -> p (j a)")
                    for r in range(R + 1):
                        f = k * R + r if r < R else k + KR
                        last = state_scan(st[:, :, bass.ds(f, 1)].rearrange("p j a -> p (j a)"), fac,
                                          0.0 if c == 0 else s_last[:, bass.ds(f, 1)])
                    last.then_inc(scan_done, 1)
                dve.wait_ge(scan_done, (c + 1) * K)
                v.tensor_copy(s_last[:], st[:, CE - 1, :]).then_inc(state_ready, 1)
                dve.wait_ge(state_ready, c + 1)

            dve.wait_ge(zfirst_in, 16)
            fill_rows(0)
            edge_chunk(0)
            for t in range(T):
                dve.wait_ge(down_done, t + 1)
                v.tensor_tensor(acc[:, t, :], acc[:, t, :], bank[4 + t % 4][0:P, 0:D], ALU.add).then_inc(y_used, 1)
            for c in range(1, C):
                fill_rows(c)
                edge_chunk(c)

            v.tensor_copy(loc[:], s_last[:]).then_inc(loc_ready, 1)
            dve.wait_ge(loc_ready, 1)
            mk = loc[:, KA:SW].rearrange("p (k a) -> p k a", a=1)
            link(v.tensor_copy(cat[:, 0, :], loc[:, 0:KA]), False)
            link(v.tensor_copy(cat[:, 1, 0:KR].rearrange("p (k r) -> p k r", r=R), mk.to_broadcast([P, K, R])), False)
            link(v.tensor_copy(cat[:, 1, KR:KA], loc[:, KA:SW]), False)
            link(v.tensor_copy(cat[:, 2, :], joins.to_broadcast([P, KA])), False)
            v.memset(rows[:, 2:4, 0:1], 0.0).then_inc(cat_ready, 1)
            dve.wait_ge(cat_turned, 1)
            mx, sm = rows[:, 3, :], rows[:, 2, :]
            link(v.tensor_scalar(rows[:, 0, 0:P], bank[2][0:KA, 0:P], -1.0, BIG, ALU.add, ALU.mult), False)
            link(v.tensor_copy(rows[:, 1, 0:P], bank[1][0:KA, 0:P]))
            link(v.tensor_tensor_scan(mx[:, 1:P + 1], rows[:, 0, 0:P], rows[:, 1, 0:P], -BIG, ALU.add, ALU.max))
            link(v.tensor_tensor(rows[:, 1, 0:P], rows[:, 1, 0:P], mx[:, 1:P + 1], ALU.subtract), False)
            link(v.tensor_tensor(rows[:, 0, 0:P], rows[:, 0, 0:P], mx[:, 0:P], ALU.add))
            v.tensor_tensor(rows[:, 0, 0:P], rows[:, 0, 0:P], mx[:, 1:P + 1], ALU.subtract).then_inc(cexp_in, 2)
            dve.wait_ge(cexp_done, 2)
            link(v.tensor_tensor(rows[:, 1, 0:P], rows[:, 1, 0:P], bank[0][0:KA, 0:P], ALU.mult))
            v.tensor_tensor_scan(sm[:, 1:P + 1], rows[:, 0, 0:P], rows[:, 1, 0:P], 0.0, ALU.mult, ALU.add).then_inc(car_ready, 1)
            dve.wait_ge(car_turned, 1)
            link(v.tensor_copy(car[:, 0, :], bank[4][0:P, 0:KA]), False)
            link(v.tensor_copy(car[:, 1, :], bank[5][0:P, 0:KA]), False)
            link(v.tensor_scalar(tmp, cont_in, -1.0, BIG, ALU.add, ALU.mult))
            dve.wait_ge(fix_in, 16)
            cm = ew_r[:, 0, :]
            lm = ew_r[:, 1, :]
            nm = ew_r[:, 2, :]
            link(v.tensor_scalar(cm, car[:, 1, KR:KA], tmp, None, ALU.add), False)
            link(v.tensor_copy(lm, s_last[:, KA:SW]))
            link(v.tensor_tensor(nm, cm, lm, ALU.max))
            link(v.tensor_copy(s_last[:, KA:SW], nm), False)
            link(v.tensor_tensor(cm, cm, nm, ALU.subtract), False)
            v.tensor_tensor(lm, lm, nm, ALU.subtract).then_inc(cexp_in, 2)
            dve.wait_ge(cexp_done, 4)
            for e_, buf in ((cm, car[:, 0, :]), (lm, s_last[:, 0:KA])):
                b4 = buf[:, 0:KR].rearrange("p (k r) -> p k r", r=R)
                link(v.tensor_tensor(b4, b4, e_.rearrange("p (k a) -> p k a", a=1).to_broadcast([P, K, R]), ALU.mult), False)
                link(v.tensor_tensor(buf[:, KR:KA], buf[:, KR:KA], e_, ALU.mult))
            v.tensor_tensor(s_last[:, 0:KA], s_last[:, 0:KA], car[:, 0, :], ALU.add).then_inc(fix_rows, 1)

            dve.wait_ge(agg_in, 16 * T)
            link(v.tensor_scalar(rden[:], agg[:, :, KR:KA], 1e-16, None, ALU.add))
            link(v.reciprocal(rden[:], rden[:]))
            link(v.tensor_tensor(rden[:], rden[:], has_edge[:].to_broadcast([P, T, K]), ALU.mult))
            a4 = agg[:, :, 0:KR].rearrange("p t (k r) -> p t k r", r=R)
            v.tensor_tensor(a4, a4, rden[:].rearrange("p t (k a) -> p t k a", a=1).to_broadcast([P, T, K, R]), ALU.mult).then_inc(agg_ready, 1)
            dve.wait_ge(g0_in, 16)
            for t in range(T):
                dve.wait_ge(ssa_done, t + 1)
                v.scalar_tensor_tensor(g0[:, t, :], bank[2 + t % 2][0:P, 0:D], -0.05, g0[:, t, :], ALU.add, ALU.add).then_inc(x1_ready, 1)
                dve.wait_ge(x1_ready, t + 1)
                link(v.scalar_tensor_tensor(acc[:, t, :], g0[:, t, :], 0.0, acc[:, t, :], ALU.max, ALU.add), t % GT == GT - 1)
                if t % GT == GT - 1:
                    layernorm_stats(t // GT, 0)
            for g in range(G):
                reciprocal_roots(g, G + g)
                for u in range(GT):
                    t = g * GT + u
                    if t < 3:
                        dve.wait_ge(xn_turned, T)
                    normalise(t, xn2_ready, xn2_turned)
                    dve.wait_ge(xn2_ready, t + 1)
                    link(v.tensor_tensor(acc[:, t, :], acc[:, t, :], xn[:, t % 3, :], ALU.add), u == GT - 1)
            dve.wait_ge(logit_done, T)
            link(v.tensor_copy(lg[:], bank[6][0:P, 0:T * X].rearrange("p (t e) -> p t e", e=X)))
            mxl, den, p1, p2, pick, nrm = (tp[:, n, :, :] for n in range(6))
            wide = [P, T, X]
            link(v.tensor_reduce(mxl[:, :, 0], lg[:], AX.X, ALU.max))
            v.tensor_tensor(lg[:], lg[:], mxl.to_broadcast(wide), ALU.subtract).then_inc(pexp_in, 1)
            dve.wait_ge(pexp_done, 1)
            link(v.tensor_reduce(den[:, :, 0], pr[:], AX.X, ALU.add))
            link(v.reciprocal(den, den))
            link(v.tensor_tensor(pr[:], pr[:], den.to_broadcast(wide), ALU.mult))
            r8 = rank8[:, :, :].to_broadcast(wide)
            for n, top in enumerate((p1, p2)):
                link(v.tensor_reduce(top[:, :, 0], pr[:], AX.X, ALU.max))
                link(v.tensor_tensor(oh[:, n], pr[:], top.to_broadcast(wide), ALU.is_equal))
                link(v.tensor_tensor(oh[:, n], oh[:, n], r8, ALU.mult))
                link(v.tensor_reduce(pick[:, :, 0], oh[:, n], AX.X, ALU.max))
                link(v.tensor_tensor(oh[:, n], pick.to_broadcast(wide), r8, ALU.is_equal))
                if n == 0:
                    link(v.scalar_tensor_tensor(pr[:], oh[:, 0], -2.0, pr[:], ALU.mult, ALU.add))
            link(v.tensor_tensor(nrm, p1, p2, ALU.add))
            link(v.tensor_scalar(nrm, nrm, 1e-12, None, ALU.max))
            link(v.reciprocal(nrm, nrm))
            for n, top in enumerate((p1, p2)):
                link(v.tensor_tensor(top, top, nrm, ALU.mult))
                link(v.tensor_tensor(oh[:, n], oh[:, n], top.to_broadcast(wide), ALU.mult))
            v.tensor_tensor(comb[:], oh[:, 0], oh[:, 1], ALU.add).then_inc(comb_ready, 1)
            for t in range(T):
                dve.wait_ge(bias_done, t + 1)
                v.tensor_tensor(acc[:, t, :], acc[:, t, :], bank[2 + t % 2][0:P, 0:D], ALU.add).then_inc(acc_step, 1)
            with dve.Fori(0, X // 2) as ep:
                v.tensor_copy(eb_pair[:], eb1_col[:, bass.ds(ep * 4, 4)]).then_inc(eb_ready, 1)
                for y in range(2 * T):
                    s, t = y // T, y % T
                    dve.wait_ge(edown_done, ep * (2 * T) + (y + 1))
                    dve.wait_ge(acc_step, ep * (2 * T) + (y + 1))
                    v.scalar_tensor_tensor(acc[:, t, :], bank[4 + y % 4][0:P, 0:D],
                                           comb[:, t, bass.ds(ep * 2 + s, 1)], acc[:, t, :], ALU.mult, ALU.add).then_inc(acc_step, 1)


_INS = ["x", "src", "dst", "L0_gnn_U", "L0_gnn_Dmat", "L0_gnn_head_w", "L0_mix_w_qkv", "L0_mix_b_qkv",
        "L0_mix_kln_g", "L0_mix_kln_b", "L0_mix_vln_g", "L0_mix_vln_b", "L0_mix_w1", "L0_mix_b1",
        "L0_mix_w2", "L0_mix_b2", "L0_ffn_router_w", "L0_ffn_w1", "L0_ffn_b1", "L0_ffn_w2", "L0_ffn_b2"]


def kernel(**inputs):
    import concourse.bacc as bacc
    from concourse.bass_utils import run_bass_kernel_spmd

    nc = bacc.Bacc("TRN2", target_bir_lowering=False, num_devices=1)
    arrays, args = {}, []
    for name in _INS:
        a = np.ascontiguousarray(inputs[name])
        arrays[f"in_{name}"] = a
        args.append(nc.dram_tensor(f"in_{name}", a.shape, mybir.dt.from_np(a.dtype), kind="ExternalInput").ap())
    out = nc.dram_tensor("out_0", (N, D), F32, kind="ExternalOutput").ap()
    build(nc, *args, out)
    r = run_bass_kernel_spmd(nc, [arrays], core_ids=[0])
    return r.results[0]["out_0"]
```

```python
import concourse.bass as bass
from concourse import mybir
from contextlib import ExitStack
import numpy as np

F32 = mybir.dt.float32
BF16 = mybir.dt.bfloat16
I32 = mybir.dt.int32
ALU = mybir.AluOpType
ACT = mybir.ActivationFunctionType
AX = mybir.AxisListType

N, D, E = 3125, 256, 53125
P = 125
T = N // P
GT = 5
G = T // GT
EP = E // P
SIZES = (85, 85, 85, 75, 60, 35)
C = len(SIZES)
AT = [sum(SIZES[:c]) for c in range(C + 1)]
CE = max(SIZES)
HCE = 85
HCH = EP // HCE
KV_AT = (0, 12, 17, 22, T)
MIX_AT = (0, 12, 20, T)
K, R = 4, 16
KR = K * R
SW = KR + 2 * K
H, HC = 8, 32
X = 8
BIG = 1.0e38
OUT_OF_RANGE = 60000.0
LOGIT_SCALE = 1.0 / np.sqrt(np.float32(R))
EPS = 1e-5
COLS = GT * P
HALF = ((0, 313), (313, 312))


def build(nc, x, src, dst, U, Dmat, head_w, w_qkv, b_qkv, kln_g, kln_b, vln_g, vln_b,
          w1, b1, w2, b2, router_w, ew1, eb1, ew2, eb2, out):
    ctx = ExitStack()

    def sb(name, shape, dt=F32):
        return ctx.enter_context(nc.sbuf_tensor(name, shape, dt))

    def sem(name):
        return ctx.enter_context(nc.semaphore(name))

    with ctx:
        zu_dram = nc.dram_tensor("zu_table", (N, KR), F32).ap()
        zd_dram = nc.dram_tensor("zd_rows", (E, KR), F32).ap()
        st_dram = nc.dram_tensor("edge_states", (E, SW), F32).ap()

        acc = sb("acc", [P, T, D])
        xT = sb("xT", [128, 2, N])
        edge_buf = sb("edge_buf", [128, 2, CE * SW])
        slot = [edge_buf[0:P, s, :].rearrange("p (j f) -> p j f", f=SW) for s in range(2)]
        small = sb("small", [128, 5 * CE * K])
        logit, dm, dl, rescale, weight = (small[0:P, n * CE * K:(n + 1) * CE * K].rearrange("p (j k) -> p j k", k=K)
                                          for n in range(5))
        xn_grad = sb("xn_grad", [128, 5 * D])
        xn = xn_grad[0:P, 0:3 * D].rearrange("p (b f) -> p b f", f=D)
        grad = xn_grad[0:P, 3 * D:5 * D].rearrange("p (b f) -> p b f", f=D)
        oh_t = [b.bitcast(BF16)[:, 0:HCE * T].rearrange("p (j a) -> p j a", a=T) for b in (xn_grad[0:P, :], small[0:P, :])]

        def small_part(at, shape):
            size = int(np.prod(shape[1:]))
            part = small[0:shape[0], at:at + size]
            if len(shape) == 3:
                part = part.rearrange("p (a b) -> p a b", b=shape[2])
            if len(shape) == 4:
                part = part.rearrange("p (a b c) -> p a b c", b=shape[2], c=shape[3])
            return part
        KA = KR + K
        cat = small_part(0, [P, 3, KA])
        car = small_part(3 * KA, [P, 2, KA])
        rows = small_part(5 * KA, [KA, 4, P + 1])
        moe_at = 5 * KA + 4 * (P + 1)
        lg = small_part(moe_at, [P, T, X])
        pr = small_part(moe_at + T * X, [P, T, X])
        oh = small_part(moe_at + 2 * T * X, [P, 2, T, X])
        zd_buf = sb("zd_buf", [128, CE * KR])
        oh_i = [b.bitcast(BF16)[:, 0:HCE * P].rearrange("p (j a) -> p j a", a=P)
                for b in (edge_buf[0:P, 1, :], zd_buf[0:P, :])]
        zd = zd_buf[0:P, :].rearrange("p (j f) -> p j f", f=KR)
        ew = zd_buf[:, 0:2 * 4 * D].rearrange("p (s w c f) -> p s w c f", s=2, w=2, c=2)
        hbuf = sb("hbuf", [128, 2 * 2 * COLS])
        hT = hbuf[:, :].rearrange("p (b m n) -> p b m n", b=2, m=2)
        khv = hbuf[0:P, 0:1024].rearrange("p (b f) -> p b f", b=2)
        wqkv = hbuf[:, 0:6 * D].rearrange("p (c f) -> p c f", c=2)
        Q_sb = hbuf[:, 6 * D:8 * D].rearrange("p (c f) -> p c f", c=2)
        sq = hbuf[0:P, 1024:2048].rearrange("p (b f) -> p b f", b=2)
        agg = sb("agg", [P, T, SW])
        zu_sb = agg[:, :, 0:KR]

        ident = sb("ident", [128, 128])
        eye2 = sb("eye2", [128, 2, D])
        tri = sb("tri", [P, P])
        iota_i = sb("iota_i", [128, 128], I32)
        iota_f = sb("iota_f", [128, 128], BF16)
        rank8_i = sb("rank8_i", [P, X], I32)
        rank8 = sb("rank8", [P, 1, X])
        ones = sb("ones", [P, 128])
        zero_b = sb("zero_b", [P, P], BF16)

        U_sb = sb("U_sb", [128, 2, KR])
        D_sb = sb("D_sb", [128, 2, D])
        M_sb = sb("M_sb", [128, 2, D])
        UM_sb = sb("UM_sb", [KR, D])
        hw_all = sb("hw_all", [KR, K])
        hw_own = sb("hw_own", [KR, 1])
        hw_m = sb("hw_m", [KR, 4])
        wq = sb("wq", [128, 2, D])
        wkv = sb("wkv", [128, 2, 2 * D])
        wmean = sb("wmean", [128, 2, 2 * H])
        bqkv_row = sb("bqkv_row", [1, 3 * D])
        bkv_row = sb("bkv_row", [1, 2 * D])
        bmean = sb("bmean", [1, 2 * H])
        bq_col = sb("bq_col", [128, 2])
        gk_row = sb("gk_row", [128, 1, HC])
        bk_row = sb("bk_row", [128, 1, HC])
        gv_col = sb("gv_col", [128, 1])
        bv_col = sb("bv_col", [128, 1])
        kvt_a = sb("kvt_a", [128, 128])
        kvt_b = sb("kvt_b", [128, 128])
        kvt_c = sb("kvt_c", [128, 1])
        KVT = sb("KVT", [128, 2, 128])
        WqT = sb("WqT", [128, 2, D])
        w1_sb = sb("w1_sb", [128, 2, D])
        w2_sb = sb("w2_sb", [128, 2, D])
        b1_col = sb("b1_col", [128, 2])
        b2_row = sb("b2_row", [1, D])
        A_sb = sb("A_sb", [128, 2, D])
        B_sb = sb("B_sb", [128, 2, D])
        bh_col = sb("bh_col", [128, 2])
        rw_in = sb("rw_in", [X, D])
        rwT = sb("rwT", [128, 2, X])
        eb1_in = sb("eb1_in", [2 * X, 128])
        eb1_col = sb("eb1_col", [128, 2 * X])
        eb_pair = sb("eb_pair", [128, 4])
        eb2_sb = sb("eb2_sb", [X, D])

        stats = sb("stats", [P, T, 6])
        mv = sb("mv", [P, T, 2])
        sd = sb("sd", [P, T, 1])
        rstd = sb("rstd", [P, T, 1])
        ss = sb("ss", [P, 3, 2 * H])

        src_i = sb("src_i", [P, EP], I32)
        dst_i = sb("dst_i", [P, EP], I32)
        dst_f = sb("dst_f", [P, EP])
        quo_i = sb("quo_i", [P, EP], I32)
        quo_f = sb("quo_f", [P, EP])
        rem_f = sb("rem_f", [P, EP])
        fix_f = quo_i[:, :].bitcast(F32)
        quo_b = sb("quo_b", [P, EP, 1], BF16)
        rem_b = sb("rem_b", [P, EP, 1], BF16)
        same = sb("same", [P, EP, 1])
        forget = sb("forget", [P, EP, 1])
        first_run = quo_f
        prev_last = sb("prev_last", [P, 1], I32)
        next_first = sb("next_first", [P, 1], I32)
        edge_f = sb("edge_f", [P, 8])
        cont = sb("cont", [P, 8])
        fix_row_i = sb("fix_row_i", [P, 2], I32)
        count = sb("count", [P, T])
        incl = sb("incl", [P, T])
        ends = sb("ends", [P, T])
        starts = sb("starts", [P, T])
        empty = sb("empty", [P, T])
        has_edge = sb("has_edge", [P, T, 1])
        row_base = sb("row_base", [P, 1])
        start_row = sb("start_row", [P, T], I32)
        end_row = sb("end_row", [P, T], I32)
        part_row = sb("part_row", [P, 1])
        part_row_i = sb("part_row_i", [P, 1], I32)
        z_first = sb("z_first", [P, KR])
        z_last = sb("z_last", [P, KR])
        s_last = sb("s_last", [P, SW])

        loc = sb("loc", [P, SW])
        ew_r = sb("ew_r", [P, 4, K])

        rden = sb("rden", [P, T, K])
        aggT = sb("aggT", [KR, 2, P])
        tp = sb("tp", [P, 6, T, 1])
        comb = sb("comb", [P, T, X])
        combT = sb("combT", [X, 2, P])

        bank = [ctx.enter_context(nc.psum_tensor(f"bank{i}", [128, 512], F32)) for i in range(8)]

        x_in = [sem(f"x_in{g}") for g in range(G)]
        dst_in, src_in, near_in = sem("dst_in"), sem("src_in"), sem("near_in")
        near_clear = sem("near_clear")
        u_in, gnn_in, mix_in, moe_in = sem("u_in"), sem("gnn_in"), sem("mix_in"), sem("moe_in")
        const_pool, const_ready = sem("const_pool"), sem("const_ready")
        zero_ready, zero_stored = sem("zero_ready"), sem("zero_stored")
        vch, ach, pch = sem("vector_chain"), sem("scalar_chain"), sem("pool_chain")
        stat_ready, root_ready = sem("stat_ready"), sem("root_ready")
        rstd_ready = sem("rstd_ready")
        xn_ready, xn_turned, xT_ready = sem("xn_ready"), sem("xn_turned"), sem("xT_ready")
        zu_done, zu_ready, zu_stored = sem("zu_done"), sem("zu_ready"), sem("zu_stored")
        hot_ready, hot_used = sem("hot_ready"), sem("hot_used")
        tot_ready, base_done = sem("tot_ready"), sem("base_done")
        rows_ready, zfirst_in, zd_scattered = sem("rows_ready"), sem("zfirst_in"), sem("zd_scattered")
        zd_in = [sem(f"zd_in{c}") for c in range(C)]
        zd_free = sem("zd_free")
        zs_in = [sem(f"zs_in{c}") for c in range(C)]
        exp_in, exp_done = sem("exp_in"), sem("exp_done")
        fill_done, scan_done = sem("fill_done"), sem("scan_done")
        state_ready = sem("state_ready")
        state_stored = [sem(f"state_stored{c}") for c in range(C)]
        prep_pe, prep_dve = sem("prep_pe"), sem("prep_dve")
        hw_exp_in, hw_exp = sem("hw_exp_in"), sem("hw_exp")
        kv_done, sq_ready, var_ready = sem("kv_done"), sem("sq_ready"), sem("var_ready")
        std_ready, khv_ready, kvt_step = sem("std_ready"), sem("khv_ready"), sem("kvt_step")
        grad_ready = sem("grad_ready")
        base_ready = sem("base_ready")
        up_done, h_ready, down_done, y_used = sem("up_done"), sem("h_ready"), sem("down_done"), sem("y_used")
        fix_in, fix_out = sem("fix_in"), sem("fix_out")
        fix_rows = sem("fix_rows")
        cat_ready, cat_turned, car_ready, car_turned = sem("cat_ready"), sem("cat_turned"), sem("car_ready"), sem("car_turned")
        cexp_in, cexp_done = sem("cexp_in"), sem("cexp_done")
        loc_ready = sem("loc_ready")
        agg_in = [sem(f"agg_in{g}") for g in range(G)]
        agg_ready, agg_turned, aggT_ready = sem("agg_ready"), sem("agg_turned"), sem("aggT_ready")
        ssa_done = sem("ssa_done")
        xn2_ready, xn2_turned, xT2_ready = sem("xn2_ready"), sem("xn2_turned"), sem("xT2_ready")
        logit_done, pexp_in, pexp_done = sem("logit_done"), sem("pexp_in"), sem("pexp_done")
        comb_ready, comb_turned, combT_ready, bias_done = sem("comb_ready"), sem("comb_turned"), sem("combT_ready"), sem("bias_done")
        ew_in = [sem(f"ew_in{s}") for s in range(2)]
        eup_done, eh_ready, edown_done, acc_step = sem("eup_done"), sem("eh_ready"), sem("edown_done"), sem("acc_step")
        eb_ready = sem("eb_ready")
        out_stored = sem("out_stored")

        block = ctx.enter_context(nc.Block())

        def chain(eng, s):
            count_ = [0]

            def link(ins, wait=True):
                count_[0] += 1
                ins.then_inc(s, 1)
                if wait:
                    eng.wait_ge(s, count_[0])
            return link

        x_v = x.rearrange("(i t) f -> i t f", t=T)
        out_v = out.rearrange("(i t) f -> i t f", t=T)
        zu_v = zu_dram.rearrange("(i t) f -> i t f", t=T)
        zd_v = zd_dram.rearrange("(p j) f -> p (j f)", p=P)
        st_v = st_dram.rearrange("(p j) f -> p (j f)", p=P)
        dst_v = dst.rearrange("(p j) -> p j", j=EP)

        def two(w):
            return w.rearrange("(c p) f -> p c f", p=128)

        @block.sync
        def _(sp):
            for g in range(G):
                sp.dma_start(acc[:, g * GT:(g + 1) * GT, :], x_v[:, g * GT:(g + 1) * GT, :]).then_inc(x_in[g], 16)
            for h in range(2):
                sp.dma_start(U_sb[:, h, :].rearrange("p (k r) -> p k r", r=R),
                             U[:, h * 128:(h + 1) * 128, :].rearrange("k p r -> p k r")).then_inc(u_in, 16)
            sp.dma_start(dst_i[:], dst_v).then_inc(dst_in, 16)
            sp.dma_start(src_i[:], src.rearrange("(p j) -> p j", j=EP)).then_inc(src_in, 16)
            sp.wait_ge(near_clear, 2)
            sp.dma_start(prev_last[1:P, :], dst_v[0:P - 1, EP - 1:EP], allow_slow_non_contiguous=True).then_inc(near_in, 16)
            sp.dma_start(next_first[0:P - 1, :], dst_v[1:P, 0:1], allow_slow_non_contiguous=True).then_inc(near_in, 16)
            sp.wait_ge(zero_ready, 1)
            for c in range(EP // CE):
                sp.dma_start(zd_v[:, c * CE * KR:(c + 1) * CE * KR], zd_buf[0:P, :]).then_inc(zero_stored, 16)
            for g in range(G):
                sp.wait_ge(zu_ready, (g + 1) * GT)
                sp.dma_start(zu_v[:, g * GT:(g + 1) * GT, :], zu_sb[:, g * GT:(g + 1) * GT, :]).then_inc(zu_stored, 16)
            sp.wait_ge(zd_scattered, 16 * T)

            def store_states(c):
                sp.wait_ge(state_ready, c + 1)
                sp.dma_start(st_v[:, AT[c] * SW:AT[c + 1] * SW], edge_buf[0:P, c % 2, 0:SIZES[c] * SW]).then_inc(state_stored[c], 16)

            for c in range(C):
                if c:
                    sp.wait_ge(zd_free, c)
                sp.dma_start(zd_buf[0:P, 0:SIZES[c] * KR], zd_v[:, AT[c] * KR:AT[c + 1] * KR]).then_inc(zd_in[c], 16)
                if c >= 1:
                    store_states(c - 1)
            sp.wait_ge(zd_free, C)
            for e in range(2):
                for w, wd in enumerate((ew1, ew2)):
                    sp.dma_start(ew[:, e, w, :, :], two(wd[e])).then_inc(ew_in[e], 16)
            store_states(C - 1)
            with sp.Fori(0, X // 2 - 1) as ep:
                for s in range(2):
                    sp.wait_ge(edown_done, ep * (2 * T) + (s + 1) * T)
                    for w, wd in enumerate((ew1, ew2)):
                        sp.dma_start(ew[:, s, w, :, :],
                                     wd[bass.ds(ep * 2 + (s + 2), 1)].rearrange("e (c p) f -> p (e c) f", p=128)).then_inc(ew_in[s], 16)
            for g in range(G):
                sp.wait_ge(acc_step, X * T + (g + 1) * GT)
                sp.dma_start(out_v[:, g * GT:(g + 1) * GT, :], acc[:, g * GT:(g + 1) * GT, :]).then_inc(out_stored, 16)
            sp.wait_ge(out_stored, 16 * G)

        @block.gpsimd
        def _(pool):
            link = chain(pool, pch)
            gp = nc.gpsimd
            gp.memset(prev_last[:], -1).then_inc(near_clear, 1)
            gp.memset(next_first[:], -1).then_inc(near_clear, 1)
            link(gp.memset(ident[:], 0.0), False)
            link(gp.memset(tri[:], 1.0))
            gp.affine_select(out=ident[:], in_=ident[:], compare_op=ALU.not_equal, fill=1.0, base=0,
                             pattern=[[-1, 128]], channel_multiplier=1).then_inc(const_pool, 1)
            gp.affine_select(out=tri[:], in_=tri[:], compare_op=ALU.is_gt, fill=0.0, base=0,
                             pattern=[[1, P]], channel_multiplier=-1).then_inc(const_pool, 1)
            gp.iota(iota_i[:], pattern=[[1, 128]], base=0, channel_multiplier=0).then_inc(const_pool, 1)
            gp.iota(rank8_i[:], pattern=[[-1, X]], base=X, channel_multiplier=0).then_inc(const_pool, 1)
            gp.iota(part_row_i[:], pattern=[[0, 1]], base=0, channel_multiplier=EP).then_inc(const_pool, 1)
            gp.memset(zd_buf[0:P, :], 0.0).then_inc(zero_ready, 1)
            def gather(c):
                for j in range(SIZES[c]):
                    gp.indirect_dma_start(
                        out=slot[c % 2][:, j, 0:KR], out_offset=None, in_=zu_dram,
                        in_offset=bass.IndirectOffsetOnAxis(ap=src_i[:, AT[c] + j:AT[c] + j + 1], axis=0)
                    ).then_inc(zs_in[c], 16)

            pool.wait_ge(src_in, 16)
            pool.wait_ge(dst_in, 16)
            pool.wait_ge(zu_stored, 16 * G)
            gp.indirect_dma_start(out=z_first[:], out_offset=None, in_=zu_dram,
                                  in_offset=bass.IndirectOffsetOnAxis(ap=dst_i[:, 0:1], axis=0)).then_inc(zfirst_in, 16)
            gather(0)
            pool.wait_ge(rows_ready, 1)
            pool.wait_ge(zero_stored, 16 * (EP // CE))
            for t in range(T):
                gp.indirect_dma_start(
                    out=zd_dram, out_offset=bass.IndirectOffsetOnAxis(ap=start_row[:, t:t + 1], axis=0),
                    in_=zu_sb[:, t, :], in_offset=None, bounds_check=E - 1, oob_is_err=False).then_inc(zd_scattered, 16)
            pool.wait_ge(hot_used, HCH)
            gather(1)
            for c in range(2, C):
                pool.wait_ge(state_stored[c - 2], 16)
                gather(c)
            for c in range(C):
                pool.wait_ge(state_stored[c], 16)
            pool.wait_ge(fix_rows, 1)
            pool.wait_ge(loc_ready, 1)
            gp.indirect_dma_start(out=s_last[:], out_offset=None, in_=st_dram,
                                  in_offset=bass.IndirectOffsetOnAxis(ap=fix_row_i[:, 0:1], axis=0)).then_inc(fix_in, 16)
            pool.wait_ge(fix_rows, 2)
            gp.indirect_dma_start(
                out=st_dram, out_offset=bass.IndirectOffsetOnAxis(ap=fix_row_i[:, 1:2], axis=0),
                in_=s_last[:], in_offset=None, bounds_check=E - 1, oob_is_err=False).then_inc(fix_out, 16)
            pool.wait_ge(fix_out, 16)
            pool.wait_ge(zd_scattered, 16 * T)
            for t in range(T):
                gp.indirect_dma_start(out=agg[:, t, :], out_offset=None, in_=st_dram,
                                      in_offset=bass.IndirectOffsetOnAxis(ap=end_row[:, t:t + 1], axis=0)).then_inc(agg_in[t // GT], 16)

        @block.scalar
        def _(act):
            sc = nc.scalar
            def layernorm_roots(n):
                act.wait_ge(stat_ready, n + 1)
                sc.activation(sd[:, (n % G) * GT:(n % G + 1) * GT, :], mv[:, (n % G) * GT:(n % G + 1) * GT, 1:2], ACT.Sqrt).then_inc(root_ready, 1)

            def evict_zu(t):
                act.wait_ge(zu_done, t + 1)
                sc.activation(zu_sb[:, t, :], bank[2 + t % 2][0:P, 0:KR], ACT.Copy).then_inc(zu_ready, 1)

            layernorm_roots(0)
            for t in range(T):
                if t % GT == 0 and t // GT + 1 < G:
                    layernorm_roots(t // GT + 1)
                act.wait_ge(xn_turned, t + 1)
                sc.activation(xT[:, :, t * P:(t + 1) * P],
                              bank[t % 2][:, 0:2 * P].rearrange("p (c n) -> p c n", c=2), ACT.Copy).then_inc(xT_ready, 1)
                if t >= 1:
                    evict_zu(t - 1)
            evict_zu(T - 1)
            for h in range(K):
                act.dma_start(hw_own[h * R:(h + 1) * R, :], head_w[h:h + 1].rearrange("(a b) -> a b", a=1).to_broadcast([R, 1])).then_inc(gnn_in, 16)
            act.dma_start(hw_all[:], head_w.rearrange("(a k) -> a k", a=1).to_broadcast([KR, K])).then_inc(gnn_in, 16)
            act.dma_start(D_sb[:], two(Dmat)).then_inc(gnn_in, 16)
            act.dma_start(wqkv[:], two(w_qkv)).then_inc(mix_in, 16)
            act.dma_start(bqkv_row[:], b_qkv.rearrange("(a f) -> a f", a=1)).then_inc(mix_in, 16)
            for h in range(H):
                act.dma_start(bq_col[(h % 4) * HC:(h % 4 + 1) * HC, h // 4:h // 4 + 1],
                              b_qkv[h * 3 * HC:h * 3 * HC + HC].rearrange("(a b) -> a b", b=1)).then_inc(mix_in, 16)
            for row, v in ((gk_row, kln_g), (bk_row, kln_b)):
                act.dma_start(row[:, 0, :], v.rearrange("(a f) -> a f", a=1).to_broadcast([128, HC])).then_inc(mix_in, 16)
            for col, v in ((gv_col, vln_g), (bv_col, vln_b)):
                for q in range(4):
                    act.dma_start(col[q * HC:(q + 1) * HC, :], v.rearrange("(a b) -> a b", b=1)).then_inc(mix_in, 16)
            act.dma_start(w1_sb[:], two(w1)).then_inc(mix_in, 16)
            act.dma_start(w2_sb[:], two(w2)).then_inc(mix_in, 16)
            act.dma_start(b2_row[:], b2.rearrange("(a f) -> a f", a=1)).then_inc(mix_in, 16)
            for m in range(2):
                act.dma_start(b1_col[:, m:m + 1], b1[m * 128:(m + 1) * 128].rearrange("(a b) -> a b", b=1)).then_inc(mix_in, 16)
            act.dma_start(rw_in[:], router_w).then_inc(moe_in, 16)
            act.dma_start(eb1_in[:], eb1.rearrange("e (m p) -> (e m) p", p=128)).then_inc(moe_in, 16)
            act.dma_start(eb2_sb[:], eb2).then_inc(moe_in, 16)
            act.wait_ge(hw_exp_in, 1)
            sc.activation(hw_all[:], hw_all[:], ACT.Exp, bias=hw_m[:, 1:2]).then_inc(hw_exp, 1)
            sc.activation(hw_own[:], hw_own[:], ACT.Exp, bias=hw_m[:, 1:2]).then_inc(hw_exp, 1)

            def edge_exps(c):
                act.wait_ge(exp_in, 2 * c + 1)
                sc.activation(weight[:, 0:SIZES[c], :], dl[:, 0:SIZES[c], :], ACT.Exp, scale=LOGIT_SCALE).then_inc(exp_done, 1)
                act.wait_ge(exp_in, 2 * c + 2)
                sc.activation(rescale[:, 0:SIZES[c], :], dm[:, 0:SIZES[c], :], ACT.Exp, scale=LOGIT_SCALE).then_inc(exp_done, 1)

            def kv_root(t):
                act.wait_ge(var_ready, t + 1)
                sc.activation(ss[:, t % 3, :], ss[:, t % 3, :], ACT.Sqrt).then_inc(std_ready, 1)

            for t in range(T):
                if t in KV_AT[1:4]:
                    edge_exps(KV_AT.index(t) - 1)
                act.wait_ge(kv_done, t + 1)
                if t >= 2:
                    act.wait_ge(var_ready, t - 1)
                sc.activation(sq[:, t % 2, :], bank[t % 3][0:P, :], ACT.Square).then_inc(sq_ready, 1)
                if t >= 1:
                    kv_root(t - 1)
            kv_root(T - 1)

            for g in range(G):
                if g >= 2:
                    edge_exps(g + 1)
                for q in range(4):
                    u = g * 4 + q
                    m, (o, w) = q // 2, HALF[q % 2]
                    act.wait_ge(up_done, u + 1)
                    sc.activation(hT[:, g % 2, m, o:o + w], bank[q][:, 0:w], ACT.Gelu, bias=bh_col[:, m:m + 1]).then_inc(h_ready, 1)
            for n in range(4):
                act.wait_ge(cexp_in, n + 1)
                if n < 2:
                    buf = rows[:, n, 0:P]
                else:
                    buf = ew_r[:, n - 2, :]
                sc.activation(buf, buf, ACT.Exp, scale=LOGIT_SCALE).then_inc(cexp_done, 1)
            for t in range(T):
                act.wait_ge(agg_turned, t + 1)
                if t >= 2:
                    act.wait_ge(ssa_done, t - 1)
                sc.activation(aggT[:, t % 2, :], bank[t % 2][0:KR, 0:P], ACT.Copy).then_inc(aggT_ready, 1)
            for g in range(G):
                layernorm_roots(G + g)
            for t in range(T):
                act.wait_ge(xn2_turned, t + 1)
                sc.activation(xT[:, :, t * P:(t + 1) * P],
                              bank[4 + t % 2][:, 0:2 * P].rearrange("p (c n) -> p c n", c=2), ACT.Copy).then_inc(xT2_ready, 1)
            act.wait_ge(pexp_in, 1)
            sc.activation(pr[:], lg[:], ACT.Exp).then_inc(pexp_done, 1)
            for t in range(T):
                act.wait_ge(comb_turned, t + 1)
                if t >= 2:
                    act.wait_ge(bias_done, t - 1)
                sc.activation(combT[:, t % 2, :], bank[t % 2][0:X, 0:P], ACT.Copy).then_inc(combT_ready, 1)
            NU = 2 * G * 4
            with act.Fori(0, X // 2) as ep:
                act.wait_ge(eb_ready, ep + 1)
                for n in range(2 * G):
                    s, g = n // G, n % G
                    for q in range(4):
                        m, (o, w) = q // 2, HALF[q % 2]
                        act.wait_ge(eup_done, ep * NU + (n * 4 + q + 1))
                        sc.activation(hT[:, n % 2, m, o:o + w], bank[q][:, 0:w], ACT.Gelu,
                                      bias=eb_pair[:, s * 2 + m:s * 2 + m + 1]).then_inc(eh_ready, 1)

        @block.tensor
        def _(pe):
            mm = nc.tensor.matmul
            tr = nc.tensor.transpose
            pe.wait_ge(const_pool, 2)
            pe.wait_ge(u_in, 32)

            def zu(t):
                pe.wait_ge(xT_ready, t + 1)
                if t >= 2:
                    pe.wait_ge(zu_ready, t - 1)
                for c in range(2):
                    last = mm(bank[2 + t % 2][0:P, 0:KR], xT[:, c, t * P:(t + 1) * P], U_sb[:, c, :], start=c == 0, stop=c == 1)
                last.then_inc(zu_done, 1)

            for t in range(T):
                pe.wait_ge(xn_ready, t + 1)
                if t >= 2:
                    pe.wait_ge(xT_ready, t - 1)
                for c in range(2):
                    last = tr(bank[t % 2][:, c * P:(c + 1) * P], xn[:, t % 3, c * 128:(c + 1) * 128], ident[0:P, 0:P])
                last.then_inc(xn_turned, 1)
                if t >= 1:
                    zu(t - 1)
            zu(T - 1)

            pe.wait_ge(const_ready, 1)
            mm(bank[4][0:P, 0:T], zero_b[:, :], zero_b[:, 0:T], start=True, stop=False)
            def add_chunk(buf, c):
                pe.wait_ge(hot_ready, c + 1)
                for j in range(HCE):
                    last = mm(bank[4][0:P, 0:T], oh_i[buf][:, j, :], oh_t[buf][:, j, :], start=False, stop=False)
                last.then_inc(hot_used, 1)

            with pe.Fori(0, HCH - 1, 2) as c:
                add_chunk(0, c)
                add_chunk(1, c + 1)
            add_chunk(0, HCH - 1)
            mm(bank[4][0:P, 0:T], zero_b[:, :], zero_b[:, 0:T], start=False, stop=True).then_inc(hot_used, 1)
            pe.wait_ge(tot_ready, 1)
            mm(bank[4][0:P, T:T + 1], tri[:, :], incl[:, T - 1:T], start=True, stop=True).then_inc(base_done, 1)

            pe.wait_ge(gnn_in, 16 * (K + 2))
            pe.wait_ge(const_ready, 1)
            for a in range(2):
                for c in range(2):
                    last = mm(bank[5][:, a * D:(a + 1) * D], D_sb[:, c, a * 128:(a + 1) * 128], D_sb[:, c, :], start=c == 0, stop=c == 1)
            last.then_inc(prep_pe, 1)
            pe.wait_ge(prep_dve, 1)
            for a in range(2):
                for c in range(2):
                    last = mm(bank[6][:, a * D:(a + 1) * D], Q_sb[:, c, a * 128:(a + 1) * 128], D_sb[:, c, :], start=c == 0, stop=c == 1)
            last.then_inc(prep_pe, 1)
            pe.wait_ge(prep_dve, 2)
            for c in range(2):
                last = mm(bank[5][0:KR, 0:D], U_sb[:, c, :], M_sb[:, c, :], start=c == 0, stop=c == 1)
            last.then_inc(prep_pe, 1)
            pe.wait_ge(prep_dve, 4)
            for g in range(2):
                for c in range(2):
                    last = tr(bank[6][:, g * D + c * 128:g * D + (c + 1) * 128], wq[:, c, g * 128:(g + 1) * 128], ident[:, :])
            last.then_inc(prep_pe, 1)
            pe.wait_ge(moe_in, 48)
            for c in range(2):
                tr(bank[7][:, c * X:(c + 1) * X], rw_in[:, c * 128:(c + 1) * 128], ident[0:X, 0:X])
            tr(bank[7][:, 32:32 + 2 * X], eb1_in[:, :], ident[0:2 * X, 0:2 * X]).then_inc(prep_pe, 1)

            pe.wait_ge(prep_dve, 6)

            def kvt(t):
                pe.wait_ge(khv_ready, t + 1)
                for g in range(2):
                    kg = khv[:, t % 2, g * 128:(g + 1) * 128]
                    vg = khv[:, t % 2, D + g * 128:D + (g + 1) * 128]
                    first = t == 0 and g == 0
                    mm(bank[5][:, g * D:g * D + 128], vg, kg, start=first, stop=t == T - 1, skip_group_check=True)
                    mm(bank[5][:, g * D + 128:g * D + 129], vg, ones[:, 0:1], start=False, stop=t == T - 1, skip_group_check=True)
                mm(bank[6][:, 0:D], ones[:, :], khv[:, t % 2, 0:D], start=t == 0, stop=t == T - 1).then_inc(kvt_step, 1)

            for t in range(T):
                if t >= 3:
                    pe.wait_ge(khv_ready, t - 2)
                for c in range(2):
                    mm(bank[t % 3][0:P, :], xT[:, c, t * P:(t + 1) * P], wkv[:, c, :], start=c == 0, stop=False)
                mm(bank[t % 3][0:P, :], ones[0:1, 0:P], bkv_row[:, :], start=False, stop=True).then_inc(kv_done, 1)
                if t >= 2:
                    kvt(t - 2)
            kvt(T - 2)
            kvt(T - 1)
            pe.wait_ge(prep_dve, 7)
            for g in range(2):
                last = mm(bank[7][:, g * D:(g + 1) * D], KVT[:, g, :], w1_sb[:, g, :], start=True, stop=True)
            last.then_inc(prep_pe, 1)
            pe.wait_ge(prep_dve, 8)
            for c in range(2):
                for g in range(2):
                    mm(bank[5][:, c * D:(c + 1) * D], WqT[:, g, c * 128:(c + 1) * 128], B_sb[:, g, :], start=g == 0, stop=g == 1)
            for m in range(2):
                for g in range(2):
                    last = mm(bank[6][:, m:m + 1], B_sb[:, g, m * 128:(m + 1) * 128], bq_col[:, g:g + 1], start=g == 0, stop=g == 1)
            last.then_inc(prep_pe, 1)
            pe.wait_ge(prep_dve, 9)

            def mix_up(g):
                for q in range(4):
                    m, (o, w) = q // 2, HALF[q % 2]
                    if g:
                        pe.wait_ge(h_ready, (g - 1) * 4 + q + 1)
                    for c in range(2):
                        last = mm(bank[q][:, 0:w], A_sb[:, c, m * 128:(m + 1) * 128],
                                  xT[:, c, g * COLS + o:g * COLS + o + w], start=c == 0, stop=c == 1)
                    last.then_inc(up_done, 1)

            def mix_down(g):
                pe.wait_ge(h_ready, (g + 1) * 4)
                for u in range(GT):
                    y = g * GT + u
                    if y >= 4:
                        pe.wait_ge(y_used, y - 3)
                    for m in range(2):
                        mm(bank[4 + y % 4][0:P, 0:D], hT[:, g % 2, m, u * P:(u + 1) * P], w2_sb[:, m, :], start=m == 0, stop=False)
                    mm(bank[4 + y % 4][0:P, 0:D], ones[0:1, 0:P], b2_row[:, :], start=False, stop=True).then_inc(down_done, 1)

            mix_up(0)
            for g in range(G):
                if g + 1 < G:
                    mix_up(g + 1)
                mix_down(g)

            pe.wait_ge(cat_ready, 1)
            pe.wait_ge(y_used, T)
            for n in range(3):
                last = tr(bank[n][0:KR + K, 0:P], cat[:, n, :], ident[0:P, 0:P])
            last.then_inc(cat_turned, 1)
            pe.wait_ge(car_ready, 1)
            for n in range(2):
                last = tr(bank[4 + n][0:P, 0:KR + K], rows[:, 2 + n, 0:P], ident[0:KR + K, 0:KR + K])
            last.then_inc(car_turned, 1)

            def grad_xn(t):
                if t >= 4:
                    pe.wait_ge(grad_ready, t - 3)
                for c in range(2):
                    mm(bank[4 + t % 4][0:P, 0:D], xT[:, c, t * P:(t + 1) * P], M_sb[:, c, :], start=c == 0, stop=False)

            def grad_agg(t):
                pe.wait_ge(aggT_ready, t + 1)
                mm(bank[4 + t % 4][0:P, 0:D], aggT[:, t % 2, :], UM_sb[:, :], start=False, stop=True).then_inc(ssa_done, 1)

            pe.wait_ge(fix_rows, 2)
            for t in range(2):
                grad_xn(t)
            for t in range(T):
                pe.wait_ge(agg_ready, t // GT + 1)
                if t >= 2:
                    pe.wait_ge(aggT_ready, t - 1)
                tr(bank[t % 2][0:KR, 0:P], agg[:, t, 0:KR], ident[0:P, 0:P]).then_inc(agg_turned, 1)
                if t >= 1:
                    grad_agg(t - 1)
                if t + 2 < T:
                    grad_xn(t + 2)
            grad_agg(T - 1)

            def route(t):
                pe.wait_ge(xT2_ready, t + 1)
                for c in range(2):
                    last = mm(bank[6][0:P, t * X:(t + 1) * X], xT[:, c, t * P:(t + 1) * P], rwT[:, c, :], start=c == 0, stop=c == 1)
                last.then_inc(logit_done, 1)

            pe.wait_ge(grad_ready, T)
            for t in range(T):
                pe.wait_ge(xn2_ready, t + 1)
                if t >= 2:
                    pe.wait_ge(xT2_ready, t - 1)
                for c in range(2):
                    last = tr(bank[4 + t % 2][:, c * P:(c + 1) * P], xn[:, t % 3, c * 128:(c + 1) * 128], ident[0:P, 0:P])
                last.then_inc(xn2_turned, 1)
                if t >= 1:
                    route(t - 1)
            route(T - 1)
            pe.wait_ge(comb_ready, 1)

            def moe_bias(t):
                pe.wait_ge(combT_ready, t + 1)
                if t >= 2:
                    pe.wait_ge(acc_step, t - 1)
                mm(bank[2 + t % 2][0:P, 0:D], combT[:, t % 2, :], eb2_sb[:, :], start=True, stop=True).then_inc(bias_done, 1)

            for t in range(T):
                if t >= 2:
                    pe.wait_ge(combT_ready, t - 1)
                tr(bank[t % 2][0:X, 0:P], comb[:, t, :], ident[0:P, 0:P]).then_inc(comb_turned, 1)
                if t >= 1:
                    moe_bias(t - 1)
            moe_bias(T - 1)
            pe.wait_ge(acc_step, T)

            NU = 2 * G * 4
            with pe.Fori(0, X // 2) as ep:
                def up(n):
                    s, g = n // G, n % G
                    if g == 0:
                        pe.wait_ge(ew_in[s], (ep + 1) * 32)
                    for q in range(4):
                        m, (o, w) = q // 2, HALF[q % 2]
                        if n:
                            pe.wait_ge(eh_ready, ep * NU + ((n - 1) * 4 + q + 1))
                        for c in range(2):
                            last = mm(bank[q][:, 0:w], ew[:, s, 0, c, m * 128:(m + 1) * 128],
                                      xT[:, c, g * COLS + o:g * COLS + o + w], start=c == 0, stop=c == 1)
                        last.then_inc(eup_done, 1)

                def down(n):
                    s, g = n // G, n % G
                    pe.wait_ge(eh_ready, ep * NU + (n + 1) * 4)
                    for u in range(GT):
                        y = n * GT + u
                        pe.wait_ge(acc_step, ep * (2 * T) + (T + y - 3))
                        for m in range(2):
                            last = mm(bank[4 + y % 4][0:P, 0:D], hT[:, n % 2, m, u * P:(u + 1) * P], ew[:, s, 1, m, :],
                                      start=m == 0, stop=m == 1)
                        last.then_inc(edown_done, 1)

                up(0)
                for n in range(2 * G):
                    if n + 1 < 2 * G:
                        up(n + 1)
                    down(n)

        @block.vector
        def _(dve):
            v = nc.vector
            link = chain(dve, vch)

            def layernorm_stats(g, n):
                for u in range(GT):
                    link(v.bn_stats(stats[:, g * GT + u, :], acc[:, g * GT + u, :]), u == GT - 1)
                for u in range(GT):
                    link(v.bn_aggr(mv[:, g * GT + u, :], stats[:, g * GT + u, :]), u == GT - 1)
                part = mv[:, g * GT:(g + 1) * GT, 1:2]
                v.tensor_scalar(part, part, EPS, None, ALU.add).then_inc(stat_ready, 1)

            def reciprocal_roots(g, n):
                dve.wait_ge(root_ready, n + 1)
                link(v.reciprocal(rstd[:, g * GT:(g + 1) * GT, :], sd[:, g * GT:(g + 1) * GT, :]))

            def normalise(t, ready, turned):
                if t >= 3:
                    dve.wait_ge(turned, t - 2)
                v.tensor_scalar(xn[:, t % 3, :], acc[:, t, :], mv[:, t, 0:1], rstd[:, t, :], ALU.subtract, ALU.mult).then_inc(ready, 1)

            dve.wait_ge(x_in[0], 16)
            layernorm_stats(0, 0)
            for g in range(G):
                if g + 1 < G:
                    dve.wait_ge(x_in[g + 1], 16)
                    layernorm_stats(g + 1, g + 1)
                reciprocal_roots(g, g)
                for u in range(GT):
                    t = g * GT + u
                    normalise(t, xn_ready, xn_turned)

            def add_normalised(ready, n, normalised):
                dve.wait_ge(normalised, T)
                link(v.tensor_tensor(mv[:, :, 0:1], mv[:, :, 0:1], rstd[:], ALU.mult))
                link(v.tensor_scalar(rstd[:], rstd[:], 1.0, None, ALU.add))
                for t in range(T):
                    v.tensor_scalar(acc[:, t, :], acc[:, t, :], rstd[:, t, :], mv[:, t, 0:1], ALU.mult, ALU.subtract).then_inc(ready, 1)
                dve.wait_ge(ready, n)

            dve.wait_ge(const_pool, 5)
            link(v.memset(ones[:], 1.0), False)
            link(v.memset(zero_b[:], 0.0), False)
            link(v.tensor_copy(iota_f[:], iota_i[:]), False)
            link(v.tensor_copy(rank8[:, 0, :], rank8_i[:]), False)
            link(v.tensor_copy(part_row[:], part_row_i[:]), False)
            link(v.memset(eye2[:], 0.0))
            for c in range(2):
                link(v.tensor_copy(eye2[:, c, c * 128:(c + 1) * 128], ident[:, :]), c == 1)
            v.memset(KVT[:], 0.0).then_inc(const_ready, 1)
            dve.wait_ge(dst_in, 16)
            dve.wait_ge(near_in, 32)
            link(v.tensor_copy(dst_f[:], dst_i[:]))
            link(v.tensor_scalar(quo_i[:], dst_f[:], 1.0 / T, -(T - 1) / 2.0 / T, ALU.mult, ALU.add))
            link(v.tensor_copy(quo_f[:], quo_i[:]))
            for lim, op, sign in ((-0.5, ALU.is_lt, -1.0), (T - 0.5, ALU.is_gt, 1.0)):
                link(v.scalar_tensor_tensor(rem_f[:], quo_f[:], -float(T), dst_f[:], ALU.mult, ALU.add))
                link(v.tensor_scalar(fix_f, rem_f[:], lim, sign, op, ALU.mult))
                link(v.tensor_tensor(quo_f[:], quo_f[:], fix_f, ALU.add))
            link(v.scalar_tensor_tensor(rem_f[:], quo_f[:], -float(T), dst_f[:], ALU.mult, ALU.add))
            link(v.tensor_copy(quo_b[:, :, 0], quo_f[:]), False)
            link(v.tensor_copy(rem_b[:, :, 0], rem_f[:]))
            dve.wait_ge(xn_turned, T)
            for c in range(HCH):
                if c == 1:
                    dve.wait_ge(zero_stored, 16 * (EP // CE))
                if c >= 2:
                    dve.wait_ge(hot_used, c - 1)
                link(v.tensor_tensor(oh_i[c % 2], quo_b[:, c * HCE:(c + 1) * HCE, :].to_broadcast([P, HCE, P]),
                                     iota_f[0:P, 0:P].rearrange("p (a b) -> p a b", a=1).to_broadcast([P, HCE, P]), ALU.is_equal), False)
                v.tensor_tensor(oh_t[c % 2], rem_b[:, c * HCE:(c + 1) * HCE, :].to_broadcast([P, HCE, T]),
                                iota_f[0:P, 0:T].rearrange("p (a b) -> p a b", a=1).to_broadcast([P, HCE, T]), ALU.is_equal).then_inc(hot_ready, 1)
            link(v.tensor_copy(edge_f[:, 0:1], prev_last[:]), False)
            link(v.tensor_copy(edge_f[:, 1:2], next_first[:]))
            cont_in, cont_out, whole, joins, pos, tmp = (cont[:, n:n + 1] for n in range(6))
            link(v.tensor_tensor(cont_in, edge_f[:, 0:1], dst_f[:, 0:1], ALU.is_equal), False)
            link(v.tensor_tensor(cont_out, edge_f[:, 1:2], dst_f[:, EP - 1:EP], ALU.is_equal), False)
            link(v.tensor_tensor(same[:, 1:EP, 0], dst_f[:, 1:EP], dst_f[:, 0:EP - 1], ALU.is_equal))
            link(v.tensor_copy(same[:, 0, :], cont_in))
            link(v.tensor_scalar(forget[:, :, 0], same[:, :, 0], -1.0, BIG, ALU.add, ALU.mult))
            link(v.memset(forget[:, 0, :], -BIG), False)
            link(v.memset(first_run[:, 0:1], 1.0), False)
            link(v.tensor_tensor_scan(first_run[:, 1:EP], same[:, 1:EP, 0], same[:, 1:EP, 0], 1.0, ALU.mult, ALU.mult))
            link(v.tensor_reduce(pos, first_run[:, 1:EP], AX.X, ALU.add), False)
            link(v.tensor_copy(whole, first_run[:, EP - 1:EP]))
            link(v.tensor_tensor(joins, whole, cont_in, ALU.mult), False)
            link(v.tensor_tensor(pos, pos, part_row[:], ALU.add), False)
            link(v.tensor_tensor(tmp, whole, cont_out, ALU.mult))
            link(v.tensor_scalar(tmp, tmp, -1.0, 1.0, ALU.mult, ALU.add))
            link(v.tensor_tensor(tmp, tmp, cont_in, ALU.mult))
            link(v.tensor_copy(fix_row_i[:, 0:1], pos), False)
            link(v.tensor_scalar(tmp, tmp, -OUT_OF_RANGE, OUT_OF_RANGE, ALU.mult, ALU.add))
            link(v.tensor_tensor(tmp, tmp, pos, ALU.add))
            v.tensor_copy(fix_row_i[:, 1:2], tmp).then_inc(fix_rows, 1)
            dve.wait_ge(hot_used, HCH + 1)
            link(v.tensor_copy(count[:], bank[4][0:P, 0:T]))
            link(v.memset(empty[:], 1.0))
            v.tensor_tensor_scan(incl[:], empty[:], count[:], 0.0, ALU.mult, ALU.add).then_inc(tot_ready, 1)
            link(v.tensor_scalar(has_edge[:, :, 0], count[:], 1.0, None, ALU.min), False)
            dve.wait_ge(base_done, 1)
            link(v.tensor_copy(row_base[:], bank[4][0:P, T:T + 1]))
            link(v.tensor_scalar(ends[:], incl[:], row_base[:], None, ALU.add))
            link(v.tensor_tensor(starts[:], ends[:], count[:], ALU.subtract), False)
            link(v.tensor_scalar(empty[:], has_edge[:, :, 0], -OUT_OF_RANGE, OUT_OF_RANGE, ALU.mult, ALU.add), False)
            link(v.tensor_scalar(ends[:], ends[:], -1.0, 0.0, ALU.add, ALU.max))
            link(v.tensor_tensor(starts[:], starts[:], empty[:], ALU.add), False)
            link(v.tensor_copy(end_row[:], ends[:]))
            v.tensor_copy(start_row[:], starts[:]).then_inc(rows_ready, 1)

            dve.wait_ge(gnn_in, 16 * (K + 2))
            link(v.tensor_reduce(hw_m[:, 0:1], hw_all[:], AX.X, ALU.max))
            v.tensor_scalar(hw_m[:, 1:2], hw_m[:, 0:1], -1.0, None, ALU.mult).then_inc(hw_exp_in, 1)
            dve.wait_ge(prep_pe, 1)
            v.scalar_tensor_tensor(Q_sb[:], bank[5][:, :].rearrange("p (c f) -> p c f", c=2), -1.0, eye2[:], ALU.mult, ALU.add).then_inc(prep_dve, 1)
            dve.wait_ge(prep_pe, 2)
            link(v.scalar_tensor_tensor(M_sb[:], bank[6][:, :].rearrange("p (c f) -> p c f", c=2), 0.5, eye2[:], ALU.mult, ALU.add))
            v.tensor_scalar(M_sb[:], M_sb[:], 0.5, None, ALU.mult).then_inc(prep_dve, 1)
            dve.wait_ge(hw_exp, 2)
            link(v.tensor_reduce(hw_m[:, 2:3], hw_all[:], AX.X, ALU.add))
            link(v.reciprocal(hw_m[:, 3:4], hw_m[:, 2:3]))
            dve.wait_ge(prep_pe, 3)
            v.tensor_scalar(UM_sb[:], bank[5][0:KR, 0:D], hw_own[:], hw_m[:, 3:4], ALU.mult, ALU.mult).then_inc(prep_dve, 1)
            dve.wait_ge(mix_in, 16 * 25)
            for c in range(2):
                wh = wqkv[:, c, :].rearrange("p (h s f) -> p h s f", s=3, f=HC)
                for s in range(2):
                    link(v.tensor_reduce(wmean[:, c, s * H:(s + 1) * H], wh[:, :, 1 + s, :], AX.X, ALU.add), False)
            bh = bqkv_row[:, :].rearrange("p (h s f) -> p h s f", s=3, f=HC)
            for s in range(2):
                link(v.tensor_reduce(bmean[:, s * H:(s + 1) * H], bh[:, :, 1 + s, :], AX.X, ALU.add), s == 1)
            link(v.tensor_scalar(wmean[:], wmean[:], -1.0 / HC, None, ALU.mult), False)
            link(v.tensor_scalar(bmean[:], bmean[:], -1.0 / HC, None, ALU.mult))
            for s in range(2):
                for c in range(2):
                    wh = wqkv[:, c, :].rearrange("p (h s f) -> p h s f", s=3, f=HC)
                    link(v.tensor_tensor(wkv[:, c, s * D:(s + 1) * D].rearrange("p (h f) -> p h f", f=HC), wh[:, :, 1 + s, :],
                                         wmean[:, c, s * H:(s + 1) * H].rearrange("p (h a) -> p h a", a=1).to_broadcast([128, H, HC]), ALU.add), False)
                link(v.tensor_tensor(bkv_row[:, s * D:(s + 1) * D].rearrange("p (h f) -> p h f", f=HC), bh[:, :, 1 + s, :],
                                     bmean[:, s * H:(s + 1) * H].rearrange("p (h a) -> p h a", a=1).to_broadcast([1, H, HC]), ALU.add), s == 1)
            for c in range(2):
                wh = wqkv[:, c, :].rearrange("p (h s f) -> p h s f", s=3, f=HC)
                last = v.tensor_copy(wq[:, c, :].rearrange("p (h f) -> p h f", f=HC), wh[:, :, 0, :])
            last.then_inc(prep_dve, 1)
            dve.wait_ge(prep_pe, 4)
            link(v.tensor_copy(WqT[:], bank[6][:, :].rearrange("p (c f) -> p c f", c=2)), False)
            dve.wait_ge(prep_pe, 5)
            v.tensor_copy(rwT[:], bank[7][:, 0:2 * X].rearrange("p (c f) -> p c f", c=2)).then_inc(prep_dve, 1)
            v.tensor_copy(eb1_col[:], bank[7][:, 32:32 + 2 * X]).then_inc(prep_dve, 1)

            def fill_rows(c):
                dve.wait_ge(zd_in[c], 16)
                init = z_first if c == 0 else z_last
                n, cs = SIZES[c], slice(AT[c], AT[c + 1])
                with dve.Fori(0, K) as k:
                    for r in range(R):
                        col = zd[:, 0:n, bass.ds(k * R + r, 1)].rearrange("p j a -> p (j a)")
                        last = v.tensor_tensor_scan(col, same[:, cs, 0], col, init[:, bass.ds(k * R + r, 1)], ALU.mult, ALU.add)
                    last.then_inc(fill_done, 1)
                dve.wait_ge(fill_done, (c + 1) * K)
                link(v.tensor_copy(z_last[:], zd[:, n - 1, :]))

            def edge_chunk(c):
                n, cs = SIZES[c], slice(AT[c], AT[c + 1])
                st, z = slot[c % 2][:, 0:n, :], zd[:, 0:n, :]
                lo_, dm_, dl_, re_, we_ = (b[:, 0:n, :] for b in (logit, dm, dl, rescale, weight))
                dve.wait_ge(zs_in[c], 16 * n)
                link(v.tensor_tensor(z, z, st[:, :, 0:KR], ALU.mult))
                v.tensor_reduce(lo_, z.rearrange("p j (k r) -> p j k r", r=R), AX.X, ALU.add).then_inc(zd_free, 1)
                dve.wait_ge(zd_free, c + 1)
                for k in range(K):
                    link(v.tensor_tensor_scan(st[:, :, KR + K + k], forget[:, cs, 0], lo_[:, :, k],
                                              0.0 if c == 0 else s_last[:, KR + K + k:KR + K + k + 1], ALU.add, ALU.max), k == K - 1)
                m = st[:, :, KR + K:SW]
                v.tensor_tensor(dl_, lo_, m, ALU.subtract).then_inc(exp_in, 1)
                link(v.tensor_tensor(dm_[:, 1:n, :], m[:, 0:n - 1, :], m[:, 1:n, :], ALU.subtract), False)
                if c == 0:
                    link(v.memset(dm_[:, 0:1, :], 0.0))
                else:
                    link(v.tensor_tensor(dm_[:, 0:1, :], s_last[:, KR + K:SW].rearrange("p (a k) -> p a k", a=1), m[:, 0:1, :], ALU.subtract))
                v.tensor_tensor(dm_, dm_, forget[:, cs, :].to_broadcast([P, n, K]), ALU.add).then_inc(exp_in, 1)
                dve.wait_ge(exp_done, 2 * c + 2)
                link(v.tensor_copy(st[:, :, KR:KR + K], we_), False)
                z4 = st[:, :, 0:KR].rearrange("p j (k r) -> p j k r", r=R)
                link(v.tensor_tensor(z4, z4, we_.rearrange("p j (k a) -> p j k a", a=1).to_broadcast([P, n, K, R]), ALU.mult))
                def state_scan(col, fac, init):
                    return v.tensor_tensor_scan(col, fac, col, init, ALU.mult, ALU.add)
                with dve.Fori(0, K) as k:
                    fac = re_[:, :, bass.ds(k, 1)].rearrange("p j a -> p (j a)")
                    for r in range(R + 1):
                        f = k * R + r if r < R else k + KR
                        last = state_scan(st[:, :, bass.ds(f, 1)].rearrange("p j a -> p (j a)"), fac,
                                          0.0 if c == 0 else s_last[:, bass.ds(f, 1)])
                    last.then_inc(scan_done, 1)
                dve.wait_ge(scan_done, (c + 1) * K)
                v.tensor_copy(s_last[:], st[:, n - 1, :]).then_inc(state_ready, 1)
                dve.wait_ge(state_ready, c + 1)


            def kv_scale(t):
                dve.wait_ge(std_ready, t + 1)
                link(v.reciprocal(ss[:, t % 3, :], ss[:, t % 3, :]))
                if t >= 2:
                    dve.wait_ge(kvt_step, t - 1)
                v.tensor_tensor(khv[:, t % 2, :].rearrange("p (h f) -> p h f", f=HC),
                                bank[t % 3][0:P, :].rearrange("p (h f) -> p h f", f=HC),
                                ss[:, t % 3, :].rearrange("p (h a) -> p h a", a=1).to_broadcast([P, 2 * H, HC]), ALU.mult).then_inc(khv_ready, 1)

            def kv_tile(t):
                dve.wait_ge(sq_ready, t + 1)
                link(v.tensor_reduce(ss[:, t % 3, :], sq[:, t % 2, :].rearrange("p (h f) -> p h f", f=HC), AX.X, ALU.add))
                v.tensor_scalar(ss[:, t % 3, :], ss[:, t % 3, :], 1.0 / HC, EPS, ALU.mult, ALU.add).then_inc(var_ready, 1)
                if t >= 1:
                    kv_scale(t - 1)
                if t == T - 1:
                    kv_scale(t)

            def kv_tiles(n):
                for t in range(KV_AT[n], KV_AT[n + 1]):
                    kv_tile(t)

            kv_tiles(0)
            dve.wait_ge(zfirst_in, 16)
            fill_rows(0)
            edge_chunk(0)
            kv_tiles(1)
            fill_rows(1)
            edge_chunk(1)
            kv_tiles(2)
            fill_rows(2)
            edge_chunk(2)
            kv_tiles(3)
            dve.wait_ge(kvt_step, T)
            for g in range(2):
                b5 = bank[5][:, g * D:g * D + 129]
                link(v.tensor_scalar(kvt_a[:], bank[6][:, g * 128:(g + 1) * 128], bv_col[:], None, ALU.mult), False)
                link(v.tensor_scalar(kvt_c[:], b5[:, 128:129], gv_col[:], None, ALU.mult), False)
                link(v.tensor_scalar(kvt_b[:, 0:1], bv_col[:], float(N), None, ALU.mult))
                link(v.tensor_tensor(kvt_c[:], kvt_c[:], kvt_b[:, 0:1], ALU.add), False)
                link(v.scalar_tensor_tensor(kvt_a[:], b5[:, 0:128], gv_col[:], kvt_a[:], ALU.mult, ALU.add))
                a4, b4 = (q[:, :].rearrange("p (h f) -> p h f", f=HC) for q in (kvt_a, kvt_b))
                link(v.tensor_tensor(a4, a4, gk_row[:, :, :].to_broadcast([128, 4, HC]), ALU.mult), False)
                link(v.tensor_scalar(b4, bk_row[:, :, :].to_broadcast([128, 4, HC]), kvt_c[:], None, ALU.mult))
                link(v.tensor_tensor(kvt_a[:], kvt_a[:], kvt_b[:], ALU.add))
                for q in range(4):
                    blk = slice(q * HC, (q + 1) * HC)
                    last = v.tensor_copy(KVT[blk, g, blk], kvt_a[blk, blk])
                if g == 0:
                    link(last)
            last.then_inc(prep_dve, 1)
            dve.wait_ge(prep_pe, 6)
            v.tensor_scalar(B_sb[:], bank[7][:, :].rearrange("p (c f) -> p c f", c=2), 1.0 / N, None, ALU.mult).then_inc(prep_dve, 1)
            dve.wait_ge(prep_pe, 7)
            link(v.tensor_tensor(A_sb[:], bank[5][:, :].rearrange("p (c f) -> p c f", c=2), w1_sb[:], ALU.add), False)
            v.tensor_tensor(bh_col[:], bank[6][:, 0:2], b1_col[:], ALU.add).then_inc(prep_dve, 1)

            add_normalised(base_ready, T, xn_ready)
            for c in range(3, C):
                fill_rows(c)
                edge_chunk(c)
                for t in range(MIX_AT[c - 3], MIX_AT[c - 2]):
                    dve.wait_ge(down_done, t + 1)
                    v.tensor_tensor(acc[:, t, :], acc[:, t, :], bank[4 + t % 4][0:P, 0:D], ALU.add).then_inc(y_used, 1)

            v.tensor_copy(loc[:], s_last[:]).then_inc(loc_ready, 1)
            dve.wait_ge(loc_ready, 1)
            mk = loc[:, KA:SW].rearrange("p (k a) -> p k a", a=1)
            link(v.tensor_copy(cat[:, 0, :], loc[:, 0:KA]), False)
            link(v.tensor_copy(cat[:, 1, 0:KR].rearrange("p (k r) -> p k r", r=R), mk.to_broadcast([P, K, R])), False)
            link(v.tensor_copy(cat[:, 1, KR:KA], loc[:, KA:SW]), False)
            link(v.tensor_copy(cat[:, 2, :], joins.to_broadcast([P, KA])), False)
            v.memset(rows[:, 2:4, 0:1], 0.0).then_inc(cat_ready, 1)
            dve.wait_ge(cat_turned, 1)
            mx, sm = rows[:, 3, :], rows[:, 2, :]
            link(v.tensor_scalar(rows[:, 0, 0:P], bank[2][0:KA, 0:P], -1.0, BIG, ALU.add, ALU.mult), False)
            link(v.tensor_copy(rows[:, 1, 0:P], bank[1][0:KA, 0:P]))
            link(v.tensor_tensor_scan(mx[:, 1:P + 1], rows[:, 0, 0:P], rows[:, 1, 0:P], -BIG, ALU.add, ALU.max))
            link(v.tensor_tensor(rows[:, 1, 0:P], rows[:, 1, 0:P], mx[:, 1:P + 1], ALU.subtract), False)
            link(v.tensor_tensor(rows[:, 0, 0:P], rows[:, 0, 0:P], mx[:, 0:P], ALU.add))
            v.tensor_tensor(rows[:, 0, 0:P], rows[:, 0, 0:P], mx[:, 1:P + 1], ALU.subtract).then_inc(cexp_in, 2)
            dve.wait_ge(cexp_done, 2)
            link(v.tensor_tensor(rows[:, 1, 0:P], rows[:, 1, 0:P], bank[0][0:KA, 0:P], ALU.mult))
            v.tensor_tensor_scan(sm[:, 1:P + 1], rows[:, 0, 0:P], rows[:, 1, 0:P], 0.0, ALU.mult, ALU.add).then_inc(car_ready, 1)
            dve.wait_ge(car_turned, 1)
            link(v.tensor_copy(car[:, 0, :], bank[4][0:P, 0:KA]), False)
            link(v.tensor_copy(car[:, 1, :], bank[5][0:P, 0:KA]), False)
            link(v.tensor_scalar(tmp, cont_in, -1.0, BIG, ALU.add, ALU.mult))
            dve.wait_ge(fix_in, 16)
            cm = ew_r[:, 0, :]
            lm = ew_r[:, 1, :]
            nm = ew_r[:, 2, :]
            link(v.tensor_scalar(cm, car[:, 1, KR:KA], tmp, None, ALU.add), False)
            link(v.tensor_copy(lm, s_last[:, KA:SW]))
            link(v.tensor_tensor(nm, cm, lm, ALU.max))
            link(v.tensor_copy(s_last[:, KA:SW], nm), False)
            link(v.tensor_tensor(cm, cm, nm, ALU.subtract), False)
            v.tensor_tensor(lm, lm, nm, ALU.subtract).then_inc(cexp_in, 2)
            dve.wait_ge(cexp_done, 4)
            for e_, buf in ((cm, car[:, 0, :]), (lm, s_last[:, 0:KA])):
                b4 = buf[:, 0:KR].rearrange("p (k r) -> p k r", r=R)
                link(v.tensor_tensor(b4, b4, e_.rearrange("p (k a) -> p k a", a=1).to_broadcast([P, K, R]), ALU.mult), False)
                link(v.tensor_tensor(buf[:, KR:KA], buf[:, KR:KA], e_, ALU.mult))
            v.tensor_tensor(s_last[:, 0:KA], s_last[:, 0:KA], car[:, 0, :], ALU.add).then_inc(fix_rows, 1)

            def normalise_sums(g):
                dve.wait_ge(agg_in[g], 16 * GT)
                ts = slice(g * GT, (g + 1) * GT)
                link(v.tensor_scalar(rden[:, ts], agg[:, ts, KR:KA], 1e-16, None, ALU.add))
                link(v.reciprocal(rden[:, ts], rden[:, ts]))
                link(v.tensor_tensor(rden[:, ts], rden[:, ts], has_edge[:, ts].to_broadcast([P, GT, K]), ALU.mult))
                a4 = agg[:, ts, 0:KR].rearrange("p t (k r) -> p t k r", r=R)
                v.tensor_tensor(a4, a4, rden[:, ts].rearrange("p t (k a) -> p t k a", a=1).to_broadcast([P, GT, K, R]), ALU.mult).then_inc(agg_ready, 1)

            normalise_sums(0)
            for t in range(T):
                if t % GT == 1 and t // GT + 1 < G:
                    normalise_sums(t // GT + 1)
                dve.wait_ge(ssa_done, t + 1)
                v.tensor_scalar(grad[:, t % 2, :], bank[4 + t % 4][0:P, 0:D], -0.05, 0.0, ALU.add, ALU.max).then_inc(grad_ready, 1)
                dve.wait_ge(grad_ready, t + 1)
                link(v.tensor_tensor(acc[:, t, :], grad[:, t % 2, :], acc[:, t, :], ALU.add), t % GT == GT - 1)
                if t % GT == GT - 1:
                    layernorm_stats(t // GT, 0)
            for g in range(G):
                reciprocal_roots(g, G + g)
                for u in range(GT):
                    t = g * GT + u
                    if t < 3:
                        dve.wait_ge(xn_turned, T)
                    normalise(t, xn2_ready, xn2_turned)
            add_normalised(base_ready, 2 * T, xn2_ready)
            dve.wait_ge(logit_done, T)
            link(v.tensor_copy(lg[:], bank[6][0:P, 0:T * X].rearrange("p (t e) -> p t e", e=X)))
            mxl, den, p1, p2, pick, nrm = (tp[:, n, :, :] for n in range(6))
            wide = [P, T, X]
            link(v.tensor_reduce(mxl[:, :, 0], lg[:], AX.X, ALU.max))
            v.tensor_tensor(lg[:], lg[:], mxl.to_broadcast(wide), ALU.subtract).then_inc(pexp_in, 1)
            dve.wait_ge(pexp_done, 1)
            link(v.tensor_reduce(den[:, :, 0], pr[:], AX.X, ALU.add))
            link(v.reciprocal(den, den))
            link(v.tensor_tensor(pr[:], pr[:], den.to_broadcast(wide), ALU.mult))
            r8 = rank8[:, :, :].to_broadcast(wide)
            for n, top in enumerate((p1, p2)):
                link(v.tensor_reduce(top[:, :, 0], pr[:], AX.X, ALU.max))
                link(v.tensor_tensor(oh[:, n], pr[:], top.to_broadcast(wide), ALU.is_equal))
                link(v.tensor_tensor(oh[:, n], oh[:, n], r8, ALU.mult))
                link(v.tensor_reduce(pick[:, :, 0], oh[:, n], AX.X, ALU.max))
                link(v.tensor_tensor(oh[:, n], pick.to_broadcast(wide), r8, ALU.is_equal))
                if n == 0:
                    link(v.scalar_tensor_tensor(pr[:], oh[:, 0], -2.0, pr[:], ALU.mult, ALU.add))
            link(v.tensor_tensor(nrm, p1, p2, ALU.add))
            link(v.tensor_scalar(nrm, nrm, 1e-12, None, ALU.max))
            link(v.reciprocal(nrm, nrm))
            for n, top in enumerate((p1, p2)):
                link(v.tensor_tensor(top, top, nrm, ALU.mult))
                link(v.tensor_tensor(oh[:, n], oh[:, n], top.to_broadcast(wide), ALU.mult))
            v.tensor_tensor(comb[:], oh[:, 0], oh[:, 1], ALU.add).then_inc(comb_ready, 1)
            for t in range(T):
                dve.wait_ge(bias_done, t + 1)
                v.tensor_tensor(acc[:, t, :], acc[:, t, :], bank[2 + t % 2][0:P, 0:D], ALU.add).then_inc(acc_step, 1)
            with dve.Fori(0, X // 2) as ep:
                v.tensor_copy(eb_pair[:], eb1_col[:, bass.ds(ep * 4, 4)]).then_inc(eb_ready, 1)
                for y in range(2 * T):
                    s, t = y // T, y % T
                    dve.wait_ge(edown_done, ep * (2 * T) + (y + 1))
                    dve.wait_ge(acc_step, ep * (2 * T) + (y + 1))
                    v.scalar_tensor_tensor(acc[:, t, :], bank[4 + y % 4][0:P, 0:D],
                                           comb[:, t, bass.ds(ep * 2 + s, 1)], acc[:, t, :], ALU.mult, ALU.add).then_inc(acc_step, 1)


_INS = ["x", "src", "dst", "L0_gnn_U", "L0_gnn_Dmat", "L0_gnn_head_w", "L0_mix_w_qkv", "L0_mix_b_qkv",
        "L0_mix_kln_g", "L0_mix_kln_b", "L0_mix_vln_g", "L0_mix_vln_b", "L0_mix_w1", "L0_mix_b1",
        "L0_mix_w2", "L0_mix_b2", "L0_ffn_router_w", "L0_ffn_w1", "L0_ffn_b1", "L0_ffn_w2", "L0_ffn_b2"]


def kernel(**inputs):
    import concourse.bacc as bacc
    from concourse.bass_utils import run_bass_kernel_spmd

    nc = bacc.Bacc("TRN2", target_bir_lowering=False, num_devices=1)
    arrays, args = {}, []
    for name in _INS:
        a = np.ascontiguousarray(inputs[name])
        arrays[f"in_{name}"] = a
        args.append(nc.dram_tensor(f"in_{name}", a.shape, mybir.dt.from_np(a.dtype), kind="ExternalInput").ap())
    out = nc.dram_tensor("out_0", (N, D), F32, kind="ExternalOutput").ap()
    build(nc, *args, out)
    r = run_bass_kernel_spmd(nc, [arrays], core_ids=[0])
    return r.results[0]["out_0"]
```

```python
import concourse.bass as bass
from concourse import mybir
from contextlib import ExitStack
import numpy as np

F32 = mybir.dt.float32
BF16 = mybir.dt.bfloat16
I32 = mybir.dt.int32
ALU = mybir.AluOpType
ACT = mybir.ActivationFunctionType
AX = mybir.AxisListType

N, D, E = 3125, 256, 53125
P = 125
T = N // P
GT = 5
G = T // GT
EP = E // P
SIZES = (85, 85, 85, 85, 50, 35)
C = len(SIZES)
AT = [sum(SIZES[:c]) for c in range(C + 1)]
CE = max(SIZES)
FILLS = EP // CE
HCE = 85
HCH = EP // HCE
KV_FIRST = 8
KV_STEPS, MIX_STEPS = (1, 1, 1, 1, 1, 1), (2, 2, 1, 1, 2, 1)
K, R = 4, 16
KR = K * R
SW = KR + 2 * K
H, HC = 8, 32
X = 8
BIG = 1.0e38
OUT_OF_RANGE = 60000.0
LOGIT_SCALE = 1.0 / np.sqrt(np.float32(R))
EPS = 1e-5
COLS = GT * P
LAG = 4
PAIRS = [range(t, min(t + 2, T)) for t in range(0, T, 2)]
NP = len(PAIRS)
QUADS = [range(t, min(t + 4, T)) for t in range(0, T, 4)]
NQ = len(QUADS)


def background_tile(c, step):
    steps = KV_STEPS if c < 3 else MIX_STEPS
    return min((c % 3) * sum(steps) + sum(steps[:step]) + (KV_FIRST if c < 3 else 0), T)

HALF = ((0, 313), (313, 312))
TOP = 2
M = TOP * T
ST = (TOP * N + X * 127) // 128
PIECE = 10
ZERO = 2500
NZERO = -(-EP * KR // ZERO)
RING = 4


def build(nc, x, src, dst, U, Dmat, head_w, w_qkv, b_qkv, kln_g, kln_b, vln_g, vln_b,
          w1, b1, w2, b2, router_w, ew1, eb1, ew2, eb2, out):
    ctx = ExitStack()

    def sb(name, shape, dt=F32):
        return ctx.enter_context(nc.sbuf_tensor(name, shape, dt))

    def sem(name):
        return ctx.enter_context(nc.semaphore(name))

    with ctx:
        zu_dram = nc.dram_tensor("zu_table", (N, KR), F32).ap()
        zd_dram = nc.dram_tensor("zd_rows", (E, KR), F32).ap()
        xn2_dram = nc.dram_tensor("xn2_table", (N, D), F32).ap()
        y_dram = nc.dram_tensor("expert_rows", (TOP * N, D), F32).ap()
        st_dram = nc.dram_tensor("edge_states", (E, SW), F32).ap()

        acc = sb("acc", [P, T, D])
        xT = sb("xT", [128, 2, N])
        edge_buf = sb("edge_buf", [128, 2, CE * SW])
        slot = [edge_buf[0:P, s, :].rearrange("p (j f) -> p j f", f=SW) for s in range(2)]
        small = sb("small", [128, 5 * CE * K])
        logit, dm, dl, rescale, weight = (small[0:P, n * CE * K:(n + 1) * CE * K].rearrange("p (j k) -> p j k", k=K)
                                          for n in range(5))
        xn_grad = sb("xn_grad", [128, 5 * D])
        xn = xn_grad[0:P, 0:4 * D].rearrange("p (b f) -> p b f", f=D)
        grad = xn_grad[0:P, 0:4 * D].rearrange("p (b f) -> p b f", b=2)
        oh_t = [b.bitcast(BF16)[:, 0:HCE * T].rearrange("p (j a) -> p j a", a=T) for b in (xn_grad[0:P, :], small[0:P, :])]

        def small_part(at, shape):
            size = int(np.prod(shape[1:]))
            part = small[0:shape[0], at:at + size]
            if len(shape) == 3:
                part = part.rearrange("p (a b) -> p a b", b=shape[2])
            if len(shape) == 4:
                part = part.rearrange("p (a b c) -> p a b c", b=shape[2], c=shape[3])
            return part
        KA = KR + K
        cat = small_part(0, [P, 3, KA])
        car = small_part(3 * KA, [P, 2, KA])
        rows = small_part(5 * KA, [KA, 4, P + 1])
        moe_at = 5 * KA + 4 * (P + 1)
        lg = small_part(moe_at, [P, T, X])
        pr = small_part(moe_at + T * X, [P, T, X])
        oh = small_part(moe_at + 2 * T * X, [P, X, M])
        zd_buf = sb("zd_buf", [128, CE * KR])
        oh_i = [b.bitcast(BF16)[:, 0:HCE * P].rearrange("p (j a) -> p j a", a=P)
                for b in (edge_buf[0:P, 1, :], zd_buf[0:P, :])]
        zd = zd_buf[0:P, :].rearrange("p (j f) -> p j f", f=KR)
        edge_flat = edge_buf[:, :, :].rearrange("p s f -> p (s f)")
        xn2 = edge_flat[0:P, 0:T * D].rearrange("p (t f) -> p t f", f=D)
        ew1_sb = edge_flat[:, T * D:T * D + X * 2 * D].rearrange("p (e c f) -> p e c f", c=2, f=D)
        ew2_sb = zd_buf[:, 0:X * 2 * D].rearrange("p (e c f) -> p e c f", c=2, f=D)
        y_ring = zd_buf[:, X * 2 * D:X * 2 * D + RING * D].rearrange("p (s f) -> p s f", f=D)
        xT_flat = xT[:, :, :].rearrange("p c n -> p (c n)")
        back = [b.rearrange("p (k t f) -> p k t f", k=TOP, f=D)
                for b in [edge_flat[0:P, g * TOP * GT * D:(g + 1) * TOP * GT * D] for g in range(G - 1)]
                + [xT_flat[0:P, 0:TOP * GT * D]]]
        xT_bf = xT_flat.bitcast(BF16)
        hot_lane = [xT_bf[0:P, n * PIECE * 128:(n + 1) * PIECE * 128].rearrange("p (m b) -> p m b", b=128) for n in range(2)]
        at = 2 * PIECE * 128
        hot_tile = xT_bf[0:P, at:at + M * ST].rearrange("p (m a) -> p m a", a=ST)
        at += M * ST
        hot_val = xT_bf[0:P, at:at + M * 2 * ST].rearrange("p (m v a) -> p m v a", v=2, a=ST)
        x_ring = xn_grad[:, 0:RING * D].rearrange("p (s f) -> p s f", f=D)
        hbuf = sb("hbuf", [128, 2 * 2 * COLS])
        hT = hbuf[:, :].rearrange("p (b m n) -> p b m n", b=2, m=2)
        khv = hbuf[0:P, 0:1024].rearrange("p (b f) -> p b f", b=2)
        wqkv = hbuf[:, 0:6 * D].rearrange("p (c f) -> p c f", c=2)
        Q_sb = hbuf[:, 6 * D:8 * D].rearrange("p (c f) -> p c f", c=2)
        eb2_all = hbuf[:, 0:X * D].rearrange("p (e f) -> p e f", f=D)
        sq = hbuf[0:P, 1024:2048].rearrange("p (b f) -> p b f", b=2)
        agg = sb("agg", [P, T, SW])
        zu_sb = agg[:, :, 0:KR]

        ident = sb("ident", [128, 128])
        eye2 = sb("eye2", [128, 2, D])
        tri = sb("tri", [P, P])
        iota_i = sb("iota_i", [128, 128], I32)
        iota_f = sb("iota_f", [128, 128], BF16)
        rank8_i = sb("rank8_i", [P, X], I32)
        rank8 = sb("rank8", [P, 1, X])
        ones = sb("ones", [P, 128])
        zero_b = sb("zero_b", [P, P], BF16)

        U_sb = sb("U_sb", [128, 2, KR])
        D_sb = sb("D_sb", [128, 2, D])
        M_sb = sb("M_sb", [128, 2, D])
        UM_sb = sb("UM_sb", [KR, D])
        hw_all = sb("hw_all", [KR, K])
        hw_own = sb("hw_own", [KR, 1])
        hw_m = sb("hw_m", [KR, 4])
        wq = sb("wq", [128, 2, D])
        wkv = sb("wkv", [128, 2, 2 * D])
        wmean = sb("wmean", [128, 2, 2 * H])
        bqkv_row = sb("bqkv_row", [1, 3 * D])
        bkv_row = sb("bkv_row", [1, 2 * D])
        bmean = sb("bmean", [1, 2 * H])
        bq_col = sb("bq_col", [128, 2])
        gk_row = sb("gk_row", [128, 1, HC])
        bk_row = sb("bk_row", [128, 1, HC])
        gv_col = sb("gv_col", [128, 1])
        bv_col = sb("bv_col", [128, 1])
        kvt_a = sb("kvt_a", [128, 128])
        kvt_b = sb("kvt_b", [128, 128])
        kvt_c = sb("kvt_c", [128, 1])
        KVT = sb("KVT", [128, 2, 128])
        WqT = sb("WqT", [128, 2, D])
        w1_sb = sb("w1_sb", [128, 2, D])
        w2_sb = sb("w2_sb", [128, 2, D])
        b1_col = sb("b1_col", [128, 2])
        b2_row = sb("b2_row", [1, D])
        A_sb = sb("A_sb", [128, 2, D])
        B_sb = sb("B_sb", [128, 2, D])
        bh_col = sb("bh_col", [128, 2])
        rw_in = sb("rw_in", [X, D])
        rwT = sb("rwT", [128, 2, X])
        eb1_in = sb("eb1_in", [2 * X, 128])
        eb1_col = sb("eb1_col", [128, 2 * X])
        w1_tile = wkv[:, :, :].rearrange("p b (c f) -> p b c f", c=2)
        xg_T = wq[:, :, :].rearrange("p b (c n) -> p b c n", c=2)
        eh_T = WqT[:, :, :].rearrange("p b (m n) -> p b m n", m=2)
        b1_tile = sb("b1_tile", [128, 2, 2])
        tile_i = sb("tile_i", [128, ST], I32)
        tile_start = sb("tile_start", [128, 1, ST])
        val_i = sb("val_i", [P, M], I32)
        val = sb("val", [P, M, 1])
        part_i = sb("part_i", [P, 1])
        cnt = sb("cnt", [P, X])
        ntile = sb("ntile", [P, X])
        tile_end = sb("tile_end", [P, X])
        off = sb("off", [P, X, 1])
        pos_m = sb("pos_m", [P, M, 1])
        lane = sb("lane", [P, M, 1])
        lane_i = sb("lane_i", [P, M], I32)
        fixl = sb("fixl", [P, M, 1])
        expert_i = sb("expert_i", [P, ST], I32)
        expert_f = sb("expert_f", [P, ST])
        slot_v = sb("slot_v", [128, ST])
        slot_c = sb("slot_c", [128, ST])
        slot_e = w1_sb[:, 1, 0:ST]
        in_row = sb("in_row", [128, ST], I32)
        out_row = sb("out_row", [128, ST], I32)

        stats = sb("stats", [P, T, 6])
        mv = sb("mv", [P, T, 2])
        sd = sb("sd", [P, T, 1])
        rstd = sb("rstd", [P, T, 1])
        ss = sb("ss", [P, 3, 2 * H])

        src_i = sb("src_i", [P, EP], I32)
        dst_i = sb("dst_i", [P, EP], I32)
        dst_f = sb("dst_f", [P, EP])
        quo_i = sb("quo_i", [P, EP], I32)
        quo_f = sb("quo_f", [P, EP])
        rem_f = sb("rem_f", [P, EP])
        fix_f = quo_i[:, :].bitcast(F32)
        quo_b = sb("quo_b", [P, EP, 1], BF16)
        rem_b = sb("rem_b", [P, EP, 1], BF16)
        same = sb("same", [P, EP, 1])
        forget = sb("forget", [P, EP, 1])
        first_run = quo_f
        prev_last = sb("prev_last", [P, 1], I32)
        next_first = sb("next_first", [P, 1], I32)
        edge_f = sb("edge_f", [P, 8])
        cont = sb("cont", [P, 8])
        fix_row_i = sb("fix_row_i", [P, 2], I32)
        count = sb("count", [P, T])
        incl = sb("incl", [P, T])
        ends = sb("ends", [P, T])
        starts = sb("starts", [P, T])
        empty = sb("empty", [P, T])
        has_edge = sb("has_edge", [P, T, 1])
        row_base = sb("row_base", [P, 1])
        start_row = sb("start_row", [P, T], I32)
        end_row = sb("end_row", [P, T], I32)
        part_row = sb("part_row", [P, 1])
        part_row_i = sb("part_row_i", [P, 1], I32)
        z_first = sb("z_first", [P, KR])
        z_last = sb("z_last", [P, KR])
        s_last = sb("s_last", [P, SW])

        loc = sb("loc", [P, SW])
        ew_r = sb("ew_r", [P, 4, K])

        rden = sb("rden", [P, T, K])
        aggT = sb("aggT", [KR, 2, 2 * P])
        shift = sb("shift", [P, 1])
        tp = w1_sb[0:P, 0, 0:6 * T].rearrange("p (n t a) -> p n t a", n=6, a=1)

        bank = [ctx.enter_context(nc.psum_tensor(f"bank{i}", [128, 512], F32)) for i in range(8)]

        x_in = [sem(f"x_in{g}") for g in range(G)]
        dst_in, src_in, near_in = sem("dst_in"), sem("src_in"), sem("near_in")
        near_clear = sem("near_clear")
        u_in, gnn_in, mix_in, moe_in = sem("u_in"), sem("gnn_in"), sem("mix_in"), sem("moe_in")
        const_pool, const_ready = sem("const_pool"), sem("const_ready")
        zero_ready, zero_stored = sem("zero_ready"), sem("zero_stored")
        vch, ach, pch = sem("vector_chain"), sem("scalar_chain"), sem("pool_chain")
        stat_ready, root_ready = sem("stat_ready"), sem("root_ready")
        rstd_ready = sem("rstd_ready")
        xn_ready, xn_turned, xT_ready = sem("xn_ready"), sem("xn_turned"), sem("xT_ready")
        zu_done, zu_ready, zu_stored = sem("zu_done"), sem("zu_ready"), sem("zu_stored")
        hot_ready, hot_used = sem("hot_ready"), sem("hot_used")
        tot_ready, base_done = sem("tot_ready"), sem("base_done")
        rows_ready, zfirst_in, zd_scattered = sem("rows_ready"), sem("zfirst_in"), sem("zd_scattered")
        zd_in = [sem(f"zd_in{c}") for c in range(FILLS)]
        zd_free = sem("zd_free")
        zs_in = [sem(f"zs_in{c}") for c in range(C)]
        exp_in, exp_done = sem("exp_in"), sem("exp_done")
        fill_done, scan_done = sem("fill_done"), sem("scan_done")
        state_ready = sem("state_ready")
        state_stored = [sem(f"state_stored{c}") for c in range(C)]
        prep_pe, prep_dve = sem("prep_pe"), sem("prep_dve")
        hw_exp_in, hw_exp = sem("hw_exp_in"), sem("hw_exp")
        kv_done, sq_ready, var_ready = sem("kv_done"), sem("sq_ready"), sem("var_ready")
        std_ready, khv_ready, kvt_step = sem("std_ready"), sem("khv_ready"), sem("kvt_step")
        grad_added = sem("grad_added")
        factors_ready = sem("factors_ready")
        relu_done = sem("relu_done")
        base_ready = sem("base_ready")
        up_done, h_ready, down_done, y_used = sem("up_done"), sem("h_ready"), sem("down_done"), sem("y_used")
        fix_in, fix_out = sem("fix_in"), sem("fix_out")
        fix_rows = sem("fix_rows")
        cat_ready, cat_turned, car_ready, car_turned = sem("cat_ready"), sem("cat_turned"), sem("car_ready"), sem("car_turned")
        cexp_in, cexp_done = sem("cexp_in"), sem("cexp_done")
        loc_ready = sem("loc_ready")
        agg_in = [sem(f"agg_in{n}") for n in range(NQ)]
        agg_ready, agg_turned, aggT_ready = sem("agg_ready"), sem("agg_turned"), sem("aggT_ready")
        ssa_done = sem("ssa_done")
        xn2_ready, xn2_turned, xT2_ready = sem("xn2_ready"), sem("xn2_turned"), sem("xT2_ready")
        logit_done, pexp_in, pexp_done = sem("logit_done"), sem("pexp_in"), sem("pexp_done")
        xn2_stored, ew_in = sem("xn2_stored"), sem("ew_in")
        cnt_ready, cnt_summed = sem("cnt_ready"), sem("cnt_summed")
        map_hot, map_used, slots_ready = sem("map_hot"), sem("map_used"), sem("slots_ready")
        map_part, map_choice = sem("map_part"), sem("map_choice")
        xg_in = [sem(f"xg_in{s}") for s in range(RING)]
        xg_turned, xgT_ready, w1_ready = sem("xg_turned"), sem("xgT_ready"), sem("w1_ready")
        eup_done, eh_ready, edown_done, y_ready = sem("eup_done"), sem("eh_ready"), sem("edown_done"), sem("y_ready")
        y_out = [sem(f"y_out{s}") for s in range(RING)]
        back_in = [sem(f"back_in{g}") for g in range(G)]
        acc_step = sem("acc_step")
        out_stored = sem("out_stored")

        block = ctx.enter_context(nc.Block())

        def chain(eng, s):
            count_ = [0]

            def link(ins, wait=True):
                count_[0] += 1
                ins.then_inc(s, 1)
                if wait:
                    eng.wait_ge(s, count_[0])
                return count_[0]
            return link

        def tile_steps(eng, step):
            for n in range(RING):
                step(0, n)
            with eng.Fori(0, ST // RING - 2) as i:
                for n in range(RING, 2 * RING):
                    step(i, n)
            for n in range(ST - RING, ST):
                step(0, n)

        def expert_of(eng, i, n):
            return eng.value_load(expert_i[0:1, bass.ds(i * RING + n, 1)] if not isinstance(i, int) else expert_i[0:1, n:n + 1],
                                  min_val=0, max_val=X - 1)

        x_v = x.rearrange("(i t) f -> i t f", t=T)
        out_v = out.rearrange("(i t) f -> i t f", t=T)
        xn2_v = xn2_dram.rearrange("(i t) f -> i t f", t=T)
        y_v = y_dram.rearrange("(k i t) f -> i k t f", k=TOP, t=T)
        zu_v = zu_dram.rearrange("(i t) f -> i t f", t=T)
        zd_v = zd_dram.rearrange("(p j) f -> p (j f)", p=P)
        st_v = st_dram.rearrange("(p j) f -> p (j f)", p=P)
        dst_v = dst.rearrange("(p j) -> p j", j=EP)

        def two(w):
            return w.rearrange("(c p) f -> p c f", p=128)

        @block.sync
        def _(sp):
            for g in range(G):
                sp.dma_start(acc[:, g * GT:(g + 1) * GT, :], x_v[:, g * GT:(g + 1) * GT, :]).then_inc(x_in[g], 16)
            for h in range(2):
                sp.dma_start(U_sb[:, h, :].rearrange("p (k r) -> p k r", r=R),
                             U[:, h * 128:(h + 1) * 128, :].rearrange("k p r -> p k r")).then_inc(u_in, 16)
            sp.dma_start(dst_i[:], dst_v).then_inc(dst_in, 16)
            sp.dma_start(src_i[:], src.rearrange("(p j) -> p j", j=EP)).then_inc(src_in, 16)
            sp.wait_ge(near_clear, 2)
            sp.dma_start(prev_last[1:P, :], dst_v[0:P - 1, EP - 1:EP], allow_slow_non_contiguous=True).then_inc(near_in, 16)
            sp.dma_start(next_first[0:P - 1, :], dst_v[1:P, 0:1], allow_slow_non_contiguous=True).then_inc(near_in, 16)
            sp.wait_ge(zero_ready, 1)
            def store_zeros(lo, hi):
                for n in range(lo, hi):
                    a, b = n * ZERO, min((n + 1) * ZERO, EP * KR)
                    sp.dma_start(zd_v[:, a:b], hbuf[0:P, 0:b - a]).then_inc(zero_stored, 16)

            store_zeros(0, NZERO // 2)
            for g in range(G):
                sp.wait_ge(zu_ready, (g * GT + GT - 1) // 2 + 1)
                sp.dma_start(zu_v[:, g * GT:(g + 1) * GT, :], zu_sb[:, g * GT:(g + 1) * GT, :]).then_inc(zu_stored, 16)
            store_zeros(NZERO // 2, NZERO)
            sp.wait_ge(zd_scattered, 16 * T)

            def store_states(c):
                sp.wait_ge(state_ready, c + 1)
                sp.dma_start(st_v[:, AT[c] * SW:AT[c + 1] * SW], edge_buf[0:P, c % 2, 0:SIZES[c] * SW]).then_inc(state_stored[c], 16)

            for c in range(C):
                if c:
                    sp.wait_ge(zd_free, c)
                if c < FILLS:
                    sp.dma_start(zd_buf[0:P, 0:CE * KR], zd_v[:, c * CE * KR:(c + 1) * CE * KR]).then_inc(zd_in[c], 16)
                if c >= 1:
                    store_states(c - 1)
            sp.wait_ge(zd_free, C)
            store_states(C - 1)
            for n in range(NQ):
                sp.wait_ge(agg_in[n], 16 * len(QUADS[n]))
            sp.dma_start(ew2_sb[:], ew2.rearrange("e (c p) f -> p e c f", p=128)).then_inc(ew_in, 16)
            for c in range(C):
                sp.wait_ge(state_stored[c], 16)
            sp.dma_start(ew1_sb[:], ew1.rearrange("e (c p) f -> p e c f", p=128)).then_inc(ew_in, 16)
            sp.wait_ge(down_done, T)
            sp.dma_start(eb2_all[:], eb2.rearrange("(a e) f -> a e f", a=1).to_broadcast([128, X, D])).then_inc(ew_in, 16)
            for g in range(G):
                sp.wait_ge(xn2_ready, (g + 1) * GT)
                sp.dma_start(xn2_v[:, g * GT:(g + 1) * GT, :], xn2[:, g * GT:(g + 1) * GT, :]).then_inc(xn2_stored, 16)
            for s in range(RING):
                sp.wait_ge(y_out[s], 16 * (ST // RING))
            for g in range(G):
                sp.dma_start(back[g][:], y_v[:, :, g * GT:(g + 1) * GT, :]).then_inc(back_in[g], 16)
            for g in range(G):
                sp.wait_ge(acc_step, NQ + (g + 1) * GT * TOP)
                sp.dma_start(out_v[:, g * GT:(g + 1) * GT, :], acc[:, g * GT:(g + 1) * GT, :]).then_inc(out_stored, 16)
            sp.wait_ge(out_stored, 16 * G)

        @block.gpsimd
        def _(pool):
            link = chain(pool, pch)
            gp = nc.gpsimd
            gp.memset(prev_last[:], -1).then_inc(near_clear, 1)
            gp.memset(next_first[:], -1).then_inc(near_clear, 1)
            link(gp.memset(ident[:], 0.0), False)
            link(gp.memset(tri[:], 1.0))
            gp.affine_select(out=ident[:], in_=ident[:], compare_op=ALU.not_equal, fill=1.0, base=0,
                             pattern=[[-1, 128]], channel_multiplier=1).then_inc(const_pool, 1)
            gp.affine_select(out=tri[:], in_=tri[:], compare_op=ALU.is_gt, fill=0.0, base=0,
                             pattern=[[1, P]], channel_multiplier=-1).then_inc(const_pool, 1)
            gp.iota(iota_i[:], pattern=[[1, 128]], base=0, channel_multiplier=0).then_inc(const_pool, 1)
            gp.iota(rank8_i[:], pattern=[[-1, X]], base=X, channel_multiplier=0).then_inc(const_pool, 1)
            gp.iota(tile_i[:], pattern=[[128, ST]], base=0, channel_multiplier=0).then_inc(const_pool, 1)
            gp.iota(val_i[:], pattern=[[32, TOP], [1, T]], base=1, channel_multiplier=0).then_inc(const_pool, 1)
            gp.iota(part_row_i[:], pattern=[[0, 1]], base=0, channel_multiplier=EP).then_inc(const_pool, 1)
            gp.memset(hbuf[0:P, 0:ZERO], 0.0).then_inc(zero_ready, 1)
            def gather(c):
                for j in range(SIZES[c]):
                    gp.indirect_dma_start(
                        out=slot[c % 2][:, j, 0:KR], out_offset=None, in_=zu_dram,
                        in_offset=bass.IndirectOffsetOnAxis(ap=src_i[:, AT[c] + j:AT[c] + j + 1], axis=0)
                    ).then_inc(zs_in[c], 16)

            pool.wait_ge(src_in, 16)
            pool.wait_ge(dst_in, 16)
            pool.wait_ge(zu_stored, 16 * G)
            gp.indirect_dma_start(out=z_first[:], out_offset=None, in_=zu_dram,
                                  in_offset=bass.IndirectOffsetOnAxis(ap=dst_i[:, 0:1], axis=0)).then_inc(zfirst_in, 16)
            gather(0)
            pool.wait_ge(rows_ready, 1)
            pool.wait_ge(zero_stored, 16 * NZERO)
            for t in range(T):
                gp.indirect_dma_start(
                    out=zd_dram, out_offset=bass.IndirectOffsetOnAxis(ap=start_row[:, t:t + 1], axis=0),
                    in_=zu_sb[:, t, :], in_offset=None, bounds_check=E - 1, oob_is_err=False).then_inc(zd_scattered, 16)
            pool.wait_ge(hot_used, HCH)
            gather(1)
            for c in range(2, C):
                pool.wait_ge(state_stored[c - 2], 16)
                gather(c)
            for c in range(C):
                pool.wait_ge(state_stored[c], 16)
            pool.wait_ge(fix_rows, 1)
            pool.wait_ge(loc_ready, 1)
            gp.indirect_dma_start(out=s_last[:], out_offset=None, in_=st_dram,
                                  in_offset=bass.IndirectOffsetOnAxis(ap=fix_row_i[:, 0:1], axis=0)).then_inc(fix_in, 16)
            pool.wait_ge(fix_rows, 2)
            gp.indirect_dma_start(
                out=st_dram, out_offset=bass.IndirectOffsetOnAxis(ap=fix_row_i[:, 1:2], axis=0),
                in_=s_last[:], in_offset=None, bounds_check=E - 1, oob_is_err=False).then_inc(fix_out, 16)
            pool.wait_ge(fix_out, 16)
            pool.wait_ge(zd_scattered, 16 * T)
            for t in range(T):
                gp.indirect_dma_start(out=agg[:, t, :], out_offset=None, in_=st_dram,
                                      in_offset=bass.IndirectOffsetOnAxis(ap=end_row[:, t:t + 1], axis=0)).then_inc(agg_in[t // 4], 16)
            for q in QUADS:
                pool.wait_ge(xn2_ready, q[-1] + 1)
                ts = slice(q[0], q[-1] + 1)
                gp.tensor_tensor(acc[:, ts, :], acc[:, ts, :], xn2[:, ts, :], ALU.add).then_inc(acc_step, 1)
            for n in range(M // PIECE):
                ms = slice(n * PIECE, (n + 1) * PIECE)
                pool.wait_ge(map_hot, n + 1)
                gp.tensor_tensor(hot_val[:, ms, 1], hot_tile[:, ms], val[:, ms].to_broadcast([P, PIECE, ST]), ALU.mult).then_inc(map_choice, 1)

            def gather_tokens(u):
                if u >= RING:
                    pool.wait_ge(xg_turned, u - RING + 1)
                gp.indirect_dma_start(out=x_ring[:, u % RING, :], out_offset=None, in_=xn2_dram,
                                      in_offset=bass.IndirectOffsetOnAxis(ap=in_row[:, u:u + 1], axis=0)).then_inc(xg_in[u % RING], 16)

            LEAD = 5
            pool.wait_ge(xn2_stored, 16 * G)
            pool.wait_ge(slots_ready, 1)
            for u in range(ST + LEAD):
                if u < ST:
                    gather_tokens(u)
                if u >= LEAD:
                    o = u - LEAD
                    pool.wait_ge(y_ready, o + 1)
                    gp.indirect_dma_start(
                        out=y_dram, out_offset=bass.IndirectOffsetOnAxis(ap=out_row[:, o:o + 1], axis=0),
                        in_=y_ring[:, o % RING, :], in_offset=None, bounds_check=TOP * N - 1, oob_is_err=False).then_inc(y_out[o % RING], 16)

        @block.scalar
        def _(act):
            sc = nc.scalar
            def layernorm_roots(n):
                act.wait_ge(stat_ready, n + 1)
                sc.activation(sd[:, (n % G) * GT:(n % G + 1) * GT, :], mv[:, (n % G) * GT:(n % G + 1) * GT, 1:2], ACT.Sqrt).then_inc(root_ready, 1)

            def evict_turned(q, bnk, ready):
                t, w = PAIRS[q][0], len(PAIRS[q]) * P
                sc.activation(xT[:, :, t * P:t * P + w],
                              bnk[:, 0:4 * P].rearrange("p (c n) -> p c n", c=2)[:, :, 0:w], ACT.Copy).then_inc(ready, 1)

            def evict_zu(q):
                w = len(PAIRS[q])
                act.wait_ge(zu_done, q + 1)
                sc.activation(zu_sb[:, PAIRS[q][0]:PAIRS[q][0] + w, :],
                              bank[2 + q % 2][0:P, 0:w * KR].rearrange("p (t f) -> p t f", f=KR), ACT.Copy).then_inc(zu_ready, 1)

            layernorm_roots(0)
            for q in range(NP):
                n = PAIRS[q][0] // GT + 1
                if PAIRS[q][0] % GT < 2 and n < G:
                    layernorm_roots(n)
                act.wait_ge(xn_turned, q + 1)
                evict_turned(q, bank[q % 2], xT_ready)
                if q >= 1:
                    evict_zu(q - 1)
            evict_zu(NP - 1)
            for h in range(K):
                act.dma_start(hw_own[h * R:(h + 1) * R, :], head_w[h:h + 1].rearrange("(a b) -> a b", a=1).to_broadcast([R, 1])).then_inc(gnn_in, 16)
            act.dma_start(hw_all[:], head_w.rearrange("(a k) -> a k", a=1).to_broadcast([KR, K])).then_inc(gnn_in, 16)
            act.dma_start(D_sb[:], two(Dmat)).then_inc(gnn_in, 16)
            act.dma_start(bqkv_row[:], b_qkv.rearrange("(a f) -> a f", a=1)).then_inc(mix_in, 16)
            for h in range(H):
                act.dma_start(bq_col[(h % 4) * HC:(h % 4 + 1) * HC, h // 4:h // 4 + 1],
                              b_qkv[h * 3 * HC:h * 3 * HC + HC].rearrange("(a b) -> a b", b=1)).then_inc(mix_in, 16)
            for row, v in ((gk_row, kln_g), (bk_row, kln_b)):
                act.dma_start(row[:, 0, :], v.rearrange("(a f) -> a f", a=1).to_broadcast([128, HC])).then_inc(mix_in, 16)
            for col, v in ((gv_col, vln_g), (bv_col, vln_b)):
                for q in range(4):
                    act.dma_start(col[q * HC:(q + 1) * HC, :], v.rearrange("(a b) -> a b", b=1)).then_inc(mix_in, 16)
            act.dma_start(w1_sb[:], two(w1)).then_inc(mix_in, 16)
            act.dma_start(w2_sb[:], two(w2)).then_inc(mix_in, 16)
            act.dma_start(b2_row[:], b2.rearrange("(a f) -> a f", a=1)).then_inc(mix_in, 16)
            for m in range(2):
                act.dma_start(b1_col[:, m:m + 1], b1[m * 128:(m + 1) * 128].rearrange("(a b) -> a b", b=1)).then_inc(mix_in, 16)
            act.dma_start(rw_in[:], router_w).then_inc(moe_in, 16)
            act.dma_start(eb1_in[:], eb1.rearrange("e (m p) -> (e m) p", p=128)).then_inc(moe_in, 16)
            act.wait_ge(zero_stored, 16 * NZERO)
            act.dma_start(wqkv[:], two(w_qkv)).then_inc(mix_in, 16)
            act.wait_ge(factors_ready, 1)
            for t in range(T):
                sc.activation(acc[:, t, :], acc[:, t, :], ACT.Identity, scale=rstd[:, t, :], bias=mv[:, t, 0:1]).then_inc(base_ready, 1)
            act.wait_ge(hw_exp_in, 1)
            sc.activation(hw_all[:], hw_all[:], ACT.Exp, bias=hw_m[:, 1:2]).then_inc(hw_exp, 1)
            sc.activation(hw_own[:], hw_own[:], ACT.Exp, bias=hw_m[:, 1:2]).then_inc(hw_exp, 1)

            def edge_exps(c):
                act.wait_ge(exp_in, 2 * c + 1)
                sc.activation(weight[:, 0:SIZES[c], :], dl[:, 0:SIZES[c], :], ACT.Exp, scale=LOGIT_SCALE).then_inc(exp_done, 1)
                act.wait_ge(exp_in, 2 * c + 2)
                sc.activation(rescale[:, 0:SIZES[c], :], dm[:, 0:SIZES[c], :], ACT.Exp, scale=LOGIT_SCALE).then_inc(exp_done, 1)

            def kv_root(t):
                act.wait_ge(var_ready, t + 1)
                sc.activation(ss[:, t % 3, :], ss[:, t % 3, :], ACT.Sqrt).then_inc(std_ready, 1)

            for t in range(T):
                for c in range(3):
                    if t == background_tile(c, 3):
                        edge_exps(c)
                act.wait_ge(kv_done, t + 1)
                if t >= 2:
                    act.wait_ge(var_ready, t - 1)
                sc.activation(sq[:, t % 2, :], bank[t % 3][0:P, :], ACT.Square).then_inc(sq_ready, 1)
                if t >= 1:
                    kv_root(t - 1)
            kv_root(T - 1)

            for g in range(G):
                for q in range(4):
                    u = g * 4 + q
                    m, (o, w) = q // 2, HALF[q % 2]
                    act.wait_ge(up_done, u + 1)
                    sc.activation(hT[:, g % 2, m, o:o + w], bank[q][:, 0:w], ACT.Gelu, bias=bh_col[:, m:m + 1]).then_inc(h_ready, 1)
                if g in (1, 3, 4):
                    edge_exps(g // 2 + 3 if g < 4 else 5)
            for n in range(4):
                act.wait_ge(cexp_in, n + 1)
                if n < 2:
                    buf = rows[:, n, 0:P]
                else:
                    buf = ew_r[:, n - 2, :]
                sc.activation(buf, buf, ACT.Exp, scale=LOGIT_SCALE).then_inc(cexp_done, 1)
            def evict_sums(q):
                w = len(PAIRS[q]) * P
                act.wait_ge(agg_turned, q + 1)
                if q >= 2:
                    act.wait_ge(ssa_done, q - 1)
                sc.activation(aggT[:, q % 2, 0:w], bank[q % 2][0:KR, 0:w], ACT.Copy).then_inc(aggT_ready, 1)

            def relu_grad(q):
                w = len(PAIRS[q]) * D
                act.wait_ge(ssa_done, q + 1)
                if q >= 2:
                    act.wait_ge(grad_added, q - 1)
                sc.activation(grad[:, q % 2, 0:w], bank[2 + q % 4][0:P, 0:w], ACT.Relu, bias=shift[:, :]).then_inc(relu_done, 1)

            def quad_roots(n):
                act.wait_ge(stat_ready, G + n + 1)
                ts = slice(QUADS[n][0], QUADS[n][-1] + 1)
                sc.activation(sd[:, ts, :], mv[:, ts, 1:2], ACT.Sqrt).then_inc(root_ready, 1)

            def evict_xn2(q):
                act.wait_ge(xn2_turned, q + 1)
                evict_turned(q, bank[6], xT2_ready)

            for q in range(NP + LAG):
                if q < NP:
                    evict_sums(q)
                if 1 <= q <= NP:
                    relu_grad(q - 1)
                if q >= 2 and (q % 2 == 0 or q == NP + 1):
                    if (q - 2) // 2 < NQ - 1:
                        quad_roots((q - 2) // 2)
                    elif q == NP + 1:
                        quad_roots(NQ - 1)
                if LAG <= q:
                    evict_xn2(q - LAG)
            def evict_tokens(i, n):
                act.wait_ge(xg_turned, i * RING + (n + 1))
                if n >= 2:
                    act.wait_ge(eup_done, i * RING + (n - 1))
                sc.activation(xg_T[:, n % 2], bank[n % 2][:, 0:2 * 128].rearrange("p (c n) -> p c n", c=2), ACT.Copy).then_inc(xgT_ready, 1)

            def gelu_tile(i, n):
                act.wait_ge(eup_done, i * RING + (n + 1))
                if n >= 2:
                    act.wait_ge(edown_done, i * RING + (n - 1))
                for m in range(2):
                    sc.activation(eh_T[:, n % 2, m, :], bank[2 + n % 2][:, m * 128:(m + 1) * 128], ACT.Gelu,
                                  bias=b1_tile[:, n % 2, m:m + 1]).then_inc(eh_ready, 1)

            act.wait_ge(pexp_in, 1)
            sc.activation(pr[:], pr[:], ACT.Exp).then_inc(pexp_done, 1)
            sc.activation(tp[:, 3:5], tp[:, 3:5], ACT.Exp).then_inc(pexp_done, 1)
            for n in range(M // PIECE):
                ms = slice(n * PIECE, (n + 1) * PIECE)
                act.wait_ge(map_hot, n + 1)
                sc.activation(hot_val[:, ms, 0], hot_tile[:, ms], ACT.Copy, scale=part_i[:, :]).then_inc(map_part, 1)
            evict_tokens(0, 0)
            evict_tokens(0, 1)
            gelu_tile(0, 0)

            def act_step(i, n):
                if n + 2 < ST:
                    evict_tokens(i, n + 2)
                if n + 1 < ST:
                    gelu_tile(i, n + 1)

            tile_steps(act, act_step)

        @block.tensor
        def _(pe):
            mm = nc.tensor.matmul
            tr = nc.tensor.transpose
            pe.wait_ge(const_pool, 2)
            pe.wait_ge(u_in, 32)

            def turn_pair(bnk, rows_of, q):
                for h, t in enumerate(PAIRS[q]):
                    for c in range(2):
                        last = tr(bnk[:, (c * 2 + h) * P:(c * 2 + h + 1) * P], rows_of(t)[:, c * 128:(c + 1) * 128], ident[0:P, 0:P])
                return last

            def zu(q):
                pe.wait_ge(xT_ready, q + 1)
                if q >= 2:
                    pe.wait_ge(zu_ready, q - 1)
                for h, t in enumerate(PAIRS[q]):
                    for c in range(2):
                        last = mm(bank[2 + q % 2][0:P, h * KR:(h + 1) * KR], xT[:, c, t * P:(t + 1) * P], U_sb[:, c, :], start=c == 0, stop=c == 1)
                last.then_inc(zu_done, 1)

            for q in range(NP):
                pe.wait_ge(xn_ready, PAIRS[q][-1] + 1)
                if q >= 2:
                    pe.wait_ge(xT_ready, q - 1)
                turn_pair(bank[q % 2], lambda t: xn[:, t % 4, :], q).then_inc(xn_turned, 1)
                if q >= 1:
                    zu(q - 1)
            zu(NP - 1)

            pe.wait_ge(const_ready, 1)
            mm(bank[4][0:P, 0:T], zero_b[:, :], zero_b[:, 0:T], start=True, stop=False)
            def add_chunk(buf, c):
                pe.wait_ge(hot_ready, c + 1)
                for j in range(HCE):
                    last = mm(bank[4][0:P, 0:T], oh_i[buf][:, j, :], oh_t[buf][:, j, :], start=False, stop=False)
                last.then_inc(hot_used, 1)

            with pe.Fori(0, HCH - 1, 2) as c:
                add_chunk(0, c)
                add_chunk(1, c + 1)
            add_chunk(0, HCH - 1)
            mm(bank[4][0:P, 0:T], zero_b[:, :], zero_b[:, 0:T], start=False, stop=True).then_inc(hot_used, 1)
            pe.wait_ge(tot_ready, 1)
            mm(bank[4][0:P, T:T + 1], tri[:, :], incl[:, T - 1:T], start=True, stop=True).then_inc(base_done, 1)

            pe.wait_ge(gnn_in, 16 * (K + 2))
            pe.wait_ge(const_ready, 1)
            for a in range(2):
                for c in range(2):
                    last = mm(bank[5][:, a * D:(a + 1) * D], D_sb[:, c, a * 128:(a + 1) * 128], D_sb[:, c, :], start=c == 0, stop=c == 1)
            last.then_inc(prep_pe, 1)
            pe.wait_ge(prep_dve, 1)
            for a in range(2):
                for c in range(2):
                    last = mm(bank[6][:, a * D:(a + 1) * D], Q_sb[:, c, a * 128:(a + 1) * 128], D_sb[:, c, :], start=c == 0, stop=c == 1)
            last.then_inc(prep_pe, 1)
            pe.wait_ge(prep_dve, 2)
            for c in range(2):
                last = mm(bank[5][0:KR, 0:D], U_sb[:, c, :], M_sb[:, c, :], start=c == 0, stop=c == 1)
            last.then_inc(prep_pe, 1)
            pe.wait_ge(prep_dve, 4)
            for g in range(2):
                for c in range(2):
                    last = tr(bank[6][:, g * D + c * 128:g * D + (c + 1) * 128], wq[:, c, g * 128:(g + 1) * 128], ident[:, :])
            last.then_inc(prep_pe, 1)
            pe.wait_ge(moe_in, 32)
            for c in range(2):
                tr(bank[7][:, c * X:(c + 1) * X], rw_in[:, c * 128:(c + 1) * 128], ident[0:X, 0:X])
            tr(bank[7][:, 32:32 + 2 * X], eb1_in[:, :], ident[0:2 * X, 0:2 * X]).then_inc(prep_pe, 1)

            pe.wait_ge(prep_dve, 6)

            def kvt(t):
                pe.wait_ge(khv_ready, t + 1)
                for g in range(2):
                    kg = khv[:, t % 2, g * 128:(g + 1) * 128]
                    vg = khv[:, t % 2, D + g * 128:D + (g + 1) * 128]
                    first = t == 0 and g == 0
                    mm(bank[5][:, g * D:g * D + 128], vg, kg, start=first, stop=t == T - 1, skip_group_check=True)
                    mm(bank[5][:, g * D + 128:g * D + 129], vg, ones[:, 0:1], start=False, stop=t == T - 1, skip_group_check=True)
                mm(bank[6][:, 0:D], ones[:, :], khv[:, t % 2, 0:D], start=t == 0, stop=t == T - 1).then_inc(kvt_step, 1)

            for t in range(T):
                if t >= 3:
                    pe.wait_ge(khv_ready, t - 2)
                for c in range(2):
                    mm(bank[t % 3][0:P, :], xT[:, c, t * P:(t + 1) * P], wkv[:, c, :], start=c == 0, stop=False)
                mm(bank[t % 3][0:P, :], ones[0:1, 0:P], bkv_row[:, :], start=False, stop=True).then_inc(kv_done, 1)
                if t >= 2:
                    kvt(t - 2)
            kvt(T - 2)
            kvt(T - 1)
            pe.wait_ge(prep_dve, 7)
            for g in range(2):
                last = mm(bank[7][:, g * D:(g + 1) * D], KVT[:, g, :], w1_sb[:, g, :], start=True, stop=True)
            last.then_inc(prep_pe, 1)
            pe.wait_ge(prep_dve, 8)
            for c in range(2):
                for g in range(2):
                    mm(bank[5][:, c * D:(c + 1) * D], WqT[:, g, c * 128:(c + 1) * 128], B_sb[:, g, :], start=g == 0, stop=g == 1)
            for m in range(2):
                for g in range(2):
                    last = mm(bank[6][:, m:m + 1], B_sb[:, g, m * 128:(m + 1) * 128], bq_col[:, g:g + 1], start=g == 0, stop=g == 1)
            last.then_inc(prep_pe, 1)
            pe.wait_ge(prep_dve, 9)

            def mix_up(g):
                for q in range(4):
                    m, (o, w) = q // 2, HALF[q % 2]
                    if g:
                        pe.wait_ge(h_ready, (g - 1) * 4 + q + 1)
                    for c in range(2):
                        last = mm(bank[q][:, 0:w], A_sb[:, c, m * 128:(m + 1) * 128],
                                  xT[:, c, g * COLS + o:g * COLS + o + w], start=c == 0, stop=c == 1)
                    last.then_inc(up_done, 1)

            def mix_down(g):
                pe.wait_ge(h_ready, (g + 1) * 4)
                for u in range(GT):
                    y = g * GT + u
                    if y >= 4:
                        pe.wait_ge(y_used, y - 3)
                    for m in range(2):
                        mm(bank[4 + y % 4][0:P, 0:D], hT[:, g % 2, m, u * P:(u + 1) * P], w2_sb[:, m, :], start=m == 0, stop=False)
                    mm(bank[4 + y % 4][0:P, 0:D], ones[0:1, 0:P], b2_row[:, :], start=False, stop=True).then_inc(down_done, 1)

            mix_up(0)
            for g in range(G):
                if g + 1 < G:
                    mix_up(g + 1)
                mix_down(g)

            def grad_xn(q):
                if q >= 4:
                    pe.wait_ge(relu_done, q - 3)
                for h, t in enumerate(PAIRS[q]):
                    for c in range(2):
                        mm(bank[2 + q % 4][0:P, h * D:(h + 1) * D], xT[:, c, t * P:(t + 1) * P], M_sb[:, c, :],
                           start=h == 0 and c == 0, stop=False, skip_group_check=True)

            pe.wait_ge(y_used, T)
            for q in range(4):
                grad_xn(q)
            pe.wait_ge(cat_ready, 1)
            for n in range(3):
                last = tr(bank[0][0:KR + K, n * 128:n * 128 + P], cat[:, n, :], ident[0:P, 0:P])
            last.then_inc(cat_turned, 1)
            pe.wait_ge(car_ready, 1)
            for n in range(2):
                last = tr(bank[1][0:P, n * 128:n * 128 + KR + K], rows[:, 2 + n, 0:P], ident[0:KR + K, 0:KR + K])
            last.then_inc(car_turned, 1)

            pe.wait_ge(fix_rows, 2)

            def turn_sums(q):
                pe.wait_ge(agg_ready, PAIRS[q][-1] // 4 + 1)
                if q >= 2:
                    pe.wait_ge(aggT_ready, q - 1)
                for h, t in enumerate(PAIRS[q]):
                    last = tr(bank[q % 2][0:KR, h * P:(h + 1) * P], agg[:, t, 0:KR], ident[0:P, 0:P])
                last.then_inc(agg_turned, 1)

            def grad_agg(q):
                pe.wait_ge(aggT_ready, q + 1)
                for h, t in enumerate(PAIRS[q]):
                    last = mm(bank[2 + q % 4][0:P, h * D:(h + 1) * D], aggT[:, q % 2, h * P:(h + 1) * P], UM_sb[:, :],
                              start=False, stop=True, skip_group_check=True)
                last.then_inc(ssa_done, 1)

            def turn_xn2(q):
                pe.wait_ge(xn2_ready, PAIRS[q][-1] + 1)
                if q >= 1:
                    pe.wait_ge(xT2_ready, q)
                turn_pair(bank[6], lambda t: xn2[:, t, :], q).then_inc(xn2_turned, 1)

            def route(q):
                pe.wait_ge(xT2_ready, q + 1)
                for t in PAIRS[q]:
                    for c in range(2):
                        last = mm(bank[7][0:P, t * X:(t + 1) * X], xT[:, c, t * P:(t + 1) * P], rwT[:, c, :], start=c == 0, stop=c == 1)
                last.then_inc(logit_done, 1)

            for q in range(NP + LAG + 1):
                if 1 <= q <= NP:
                    grad_agg(q - 1)
                if q < NP:
                    turn_sums(q)
                if 2 <= q and q + 2 < NP:
                    grad_xn(q + 2)
                if LAG <= q < NP + LAG:
                    turn_xn2(q - LAG)
                if LAG < q:
                    route(q - LAG - 1)
            pe.wait_ge(cnt_ready, 1)
            mm(bank[7][0:P, 0:X], tri[:, :], cnt[:, :], start=True, stop=True)
            mm(bank[7][0:P, X:2 * X], ones[:, 0:P], cnt[:, :], start=True, stop=True).then_inc(cnt_summed, 1)
            for m in range(M):
                if m % PIECE == 0:
                    pe.wait_ge(map_hot, m // PIECE + 1)
                    pe.wait_ge(map_part, m // PIECE + 1)
                    pe.wait_ge(map_choice, m // PIECE + 1)
                last = mm(bank[0][:, 0:2 * ST], hot_lane[m // PIECE % 2][:, m % PIECE, :],
                          hot_val[:, m].rearrange("p v a -> p (v a)"), start=m == 0, stop=m == M - 1)
                if m % PIECE == PIECE - 1:
                    last.then_inc(map_used, 1)

            pe.wait_ge(slots_ready, 1)
            pe.wait_ge(ew_in, 48)

            def turn_tokens(i, n):
                pe.wait_ge(xg_in[n % RING], i * 16 + 16 * (n // RING + 1))
                if n >= 2:
                    pe.wait_ge(xgT_ready, i * RING + (n - 1))
                for c in range(2):
                    last = tr(bank[n % 2][:, c * 128:(c + 1) * 128], x_ring[:, n % RING, c * 128:(c + 1) * 128], ident[:, :])
                last.then_inc(xg_turned, 1)

            def up_tile(i, n):
                pe.wait_ge(xgT_ready, i * RING + (n + 1))
                pe.wait_ge(w1_ready, i * RING + (n + 1))
                if n >= 2:
                    pe.wait_ge(eh_ready, i * (2 * RING) + 2 * (n - 1))
                for m in range(2):
                    for c in range(2):
                        last = mm(bank[2 + n % 2][:, m * 128:(m + 1) * 128], w1_tile[:, n % 2, c, m * 128:(m + 1) * 128],
                                  xg_T[:, n % 2, c, :], start=c == 0, stop=c == 1)
                last.then_inc(eup_done, 1)

            def down_tile(i, n):
                e = expert_of(pe, i, n)
                pe.wait_ge(eh_ready, i * (2 * RING) + 2 * (n + 1))
                if n >= 2:
                    pe.wait_ge(y_ready, i * RING + (n - 1))
                for m in range(2):
                    last = mm(bank[4 + n % 2][:, 0:D], eh_T[:, n % 2, m, :],
                              ew2_sb[:, bass.ds(e, 1), m, :].rearrange("p e f -> p (e f)"), start=m == 0, stop=m == 1)
                last.then_inc(edown_done, 1)

            turn_tokens(0, 0)
            turn_tokens(0, 1)
            up_tile(0, 0)

            def pe_step(i, n):
                if n + 2 < ST:
                    turn_tokens(i, n + 2)
                if n + 1 < ST:
                    up_tile(i, n + 1)
                down_tile(i, n)

            tile_steps(pe, pe_step)

        @block.vector
        def _(dve):
            v = nc.vector
            link = chain(dve, vch)

            def layernorm_stats(g, n):
                for u in range(GT):
                    link(v.bn_stats(stats[:, g * GT + u, :], acc[:, g * GT + u, :]), u == GT - 1)
                for u in range(GT):
                    link(v.bn_aggr(mv[:, g * GT + u, :], stats[:, g * GT + u, :]), u == GT - 1)
                part = mv[:, g * GT:(g + 1) * GT, 1:2]
                v.tensor_scalar(part, part, EPS, None, ALU.add).then_inc(stat_ready, 1)

            def reciprocal_roots(g, n):
                dve.wait_ge(root_ready, n + 1)
                link(v.reciprocal(rstd[:, g * GT:(g + 1) * GT, :], sd[:, g * GT:(g + 1) * GT, :]))

            dve.wait_ge(x_in[0], 16)
            layernorm_stats(0, 0)
            for g in range(G):
                if g + 1 < G:
                    dve.wait_ge(x_in[g + 1], 16)
                    layernorm_stats(g + 1, g + 1)
                reciprocal_roots(g, g)
                for u in range(GT):
                    t = g * GT + u
                    if t >= 4:
                        dve.wait_ge(xn_turned, t // 2 - 1)
                    v.tensor_scalar(xn[:, t % 4, :], acc[:, t, :], mv[:, t, 0:1], rstd[:, t, :], ALU.subtract, ALU.mult).then_inc(xn_ready, 1)

            dve.wait_ge(xn_ready, T)
            link(v.scalar_tensor_tensor(mv[:, :, 0:1], mv[:, :, 0:1], -1.0, rstd[:], ALU.mult, ALU.mult))
            v.tensor_scalar(rstd[:], rstd[:], 1.0, None, ALU.add).then_inc(factors_ready, 1)

            dve.wait_ge(const_pool, 7)
            link(v.memset(ones[:], 1.0), False)
            link(v.memset(shift[:], -0.05), False)
            link(v.memset(zero_b[:], 0.0), False)
            link(v.tensor_copy(iota_f[:], iota_i[:]), False)
            link(v.tensor_copy(rank8[:, 0, :], rank8_i[:]), False)
            link(v.tensor_copy(part_row[:], part_row_i[:]), False)
            link(v.tensor_copy(tile_start[:, 0, :], tile_i[:]), False)
            link(v.tensor_copy(val[:, :, 0], val_i[:]), False)
            link(v.tensor_scalar(part_i[:], part_row_i[:], 1.0 / EP, None, ALU.mult), False)
            link(v.memset(eye2[:], 0.0))
            for c in range(2):
                link(v.tensor_copy(eye2[:, c, c * 128:(c + 1) * 128], ident[:, :]), c == 1)
            v.memset(KVT[:], 0.0).then_inc(const_ready, 1)
            dve.wait_ge(dst_in, 16)
            dve.wait_ge(near_in, 32)
            link(v.tensor_copy(dst_f[:], dst_i[:]))
            link(v.tensor_scalar(quo_i[:], dst_f[:], 1.0 / T, -(T - 1) / 2.0 / T, ALU.mult, ALU.add))
            link(v.tensor_copy(quo_f[:], quo_i[:]))
            for lim, op, sign in ((-0.5, ALU.is_lt, -1.0), (T - 0.5, ALU.is_gt, 1.0)):
                link(v.scalar_tensor_tensor(rem_f[:], quo_f[:], -float(T), dst_f[:], ALU.mult, ALU.add))
                link(v.tensor_scalar(fix_f, rem_f[:], lim, sign, op, ALU.mult))
                link(v.tensor_tensor(quo_f[:], quo_f[:], fix_f, ALU.add))
            link(v.scalar_tensor_tensor(rem_f[:], quo_f[:], -float(T), dst_f[:], ALU.mult, ALU.add))
            link(v.tensor_copy(quo_b[:, :, 0], quo_f[:]), False)
            link(v.tensor_copy(rem_b[:, :, 0], rem_f[:]))
            dve.wait_ge(xn_turned, NP)
            for c in range(HCH):
                if c >= 2:
                    dve.wait_ge(hot_used, c - 1)
                link(v.tensor_tensor(oh_i[c % 2], quo_b[:, c * HCE:(c + 1) * HCE, :].to_broadcast([P, HCE, P]),
                                     iota_f[0:P, 0:P].rearrange("p (a b) -> p a b", a=1).to_broadcast([P, HCE, P]), ALU.is_equal), False)
                v.tensor_tensor(oh_t[c % 2], rem_b[:, c * HCE:(c + 1) * HCE, :].to_broadcast([P, HCE, T]),
                                iota_f[0:P, 0:T].rearrange("p (a b) -> p a b", a=1).to_broadcast([P, HCE, T]), ALU.is_equal).then_inc(hot_ready, 1)
            link(v.tensor_copy(edge_f[:, 0:1], prev_last[:]), False)
            link(v.tensor_copy(edge_f[:, 1:2], next_first[:]))
            cont_in, cont_out, whole, joins, pos, tmp = (cont[:, n:n + 1] for n in range(6))
            link(v.tensor_tensor(cont_in, edge_f[:, 0:1], dst_f[:, 0:1], ALU.is_equal), False)
            link(v.tensor_tensor(cont_out, edge_f[:, 1:2], dst_f[:, EP - 1:EP], ALU.is_equal), False)
            link(v.tensor_tensor(same[:, 1:EP, 0], dst_f[:, 1:EP], dst_f[:, 0:EP - 1], ALU.is_equal))
            link(v.tensor_copy(same[:, 0, :], cont_in))
            link(v.tensor_scalar(forget[:, :, 0], same[:, :, 0], -1.0, BIG, ALU.add, ALU.mult))
            link(v.memset(forget[:, 0, :], -BIG), False)
            link(v.memset(first_run[:, 0:1], 1.0), False)
            link(v.tensor_tensor_scan(first_run[:, 1:EP], same[:, 1:EP, 0], same[:, 1:EP, 0], 1.0, ALU.mult, ALU.mult))
            link(v.tensor_reduce(pos, first_run[:, 1:EP], AX.X, ALU.add), False)
            link(v.tensor_copy(whole, first_run[:, EP - 1:EP]))
            link(v.tensor_tensor(joins, whole, cont_in, ALU.mult), False)
            link(v.tensor_tensor(pos, pos, part_row[:], ALU.add), False)
            link(v.tensor_tensor(tmp, whole, cont_out, ALU.mult))
            link(v.tensor_scalar(tmp, tmp, -1.0, 1.0, ALU.mult, ALU.add))
            link(v.tensor_tensor(tmp, tmp, cont_in, ALU.mult))
            link(v.tensor_copy(fix_row_i[:, 0:1], pos), False)
            link(v.tensor_scalar(tmp, tmp, -OUT_OF_RANGE, OUT_OF_RANGE, ALU.mult, ALU.add))
            link(v.tensor_tensor(tmp, tmp, pos, ALU.add))
            v.tensor_copy(fix_row_i[:, 1:2], tmp).then_inc(fix_rows, 1)
            dve.wait_ge(hot_used, HCH + 1)
            link(v.tensor_copy(count[:], bank[4][0:P, 0:T]))
            link(v.memset(empty[:], 1.0))
            v.tensor_tensor_scan(incl[:], empty[:], count[:], 0.0, ALU.mult, ALU.add).then_inc(tot_ready, 1)
            link(v.tensor_scalar(has_edge[:, :, 0], count[:], 1.0, None, ALU.min), False)
            dve.wait_ge(base_done, 1)
            link(v.tensor_copy(row_base[:], bank[4][0:P, T:T + 1]))
            link(v.tensor_scalar(ends[:], incl[:], row_base[:], None, ALU.add))
            link(v.tensor_tensor(starts[:], ends[:], count[:], ALU.subtract), False)
            link(v.tensor_scalar(empty[:], has_edge[:, :, 0], -OUT_OF_RANGE, OUT_OF_RANGE, ALU.mult, ALU.add), False)
            link(v.tensor_scalar(ends[:], ends[:], -1.0, 0.0, ALU.add, ALU.max))
            link(v.tensor_tensor(starts[:], starts[:], empty[:], ALU.add), False)
            link(v.tensor_copy(end_row[:], ends[:]))
            v.tensor_copy(start_row[:], starts[:]).then_inc(rows_ready, 1)

            dve.wait_ge(gnn_in, 16 * (K + 2))
            link(v.tensor_reduce(hw_m[:, 0:1], hw_all[:], AX.X, ALU.max))
            v.tensor_scalar(hw_m[:, 1:2], hw_m[:, 0:1], -1.0, None, ALU.mult).then_inc(hw_exp_in, 1)
            dve.wait_ge(prep_pe, 1)
            dve.wait_ge(zero_stored, 16 * NZERO)
            v.scalar_tensor_tensor(Q_sb[:], bank[5][:, :].rearrange("p (c f) -> p c f", c=2), -1.0, eye2[:], ALU.mult, ALU.add).then_inc(prep_dve, 1)
            dve.wait_ge(prep_pe, 2)
            link(v.scalar_tensor_tensor(M_sb[:], bank[6][:, :].rearrange("p (c f) -> p c f", c=2), 0.5, eye2[:], ALU.mult, ALU.add))
            v.tensor_scalar(M_sb[:], M_sb[:], 0.5, None, ALU.mult).then_inc(prep_dve, 1)
            dve.wait_ge(hw_exp, 2)
            link(v.tensor_reduce(hw_m[:, 2:3], hw_all[:], AX.X, ALU.add))
            link(v.reciprocal(hw_m[:, 3:4], hw_m[:, 2:3]))
            dve.wait_ge(prep_pe, 3)
            v.tensor_scalar(UM_sb[:], bank[5][0:KR, 0:D], hw_own[:], hw_m[:, 3:4], ALU.mult, ALU.mult).then_inc(prep_dve, 1)
            dve.wait_ge(mix_in, 16 * 25)
            for c in range(2):
                wh = wqkv[:, c, :].rearrange("p (h s f) -> p h s f", s=3, f=HC)
                for s in range(2):
                    link(v.tensor_reduce(wmean[:, c, s * H:(s + 1) * H], wh[:, :, 1 + s, :], AX.X, ALU.add), False)
            bh = bqkv_row[:, :].rearrange("p (h s f) -> p h s f", s=3, f=HC)
            for s in range(2):
                link(v.tensor_reduce(bmean[:, s * H:(s + 1) * H], bh[:, :, 1 + s, :], AX.X, ALU.add), s == 1)
            link(v.tensor_scalar(wmean[:], wmean[:], -1.0 / HC, None, ALU.mult), False)
            link(v.tensor_scalar(bmean[:], bmean[:], -1.0 / HC, None, ALU.mult))
            for s in range(2):
                for c in range(2):
                    wh = wqkv[:, c, :].rearrange("p (h s f) -> p h s f", s=3, f=HC)
                    link(v.tensor_tensor(wkv[:, c, s * D:(s + 1) * D].rearrange("p (h f) -> p h f", f=HC), wh[:, :, 1 + s, :],
                                         wmean[:, c, s * H:(s + 1) * H].rearrange("p (h a) -> p h a", a=1).to_broadcast([128, H, HC]), ALU.add), False)
                link(v.tensor_tensor(bkv_row[:, s * D:(s + 1) * D].rearrange("p (h f) -> p h f", f=HC), bh[:, :, 1 + s, :],
                                     bmean[:, s * H:(s + 1) * H].rearrange("p (h a) -> p h a", a=1).to_broadcast([1, H, HC]), ALU.add), s == 1)
            for c in range(2):
                wh = wqkv[:, c, :].rearrange("p (h s f) -> p h s f", s=3, f=HC)
                last = v.tensor_copy(wq[:, c, :].rearrange("p (h f) -> p h f", f=HC), wh[:, :, 0, :])
            last.then_inc(prep_dve, 1)
            dve.wait_ge(prep_pe, 4)
            link(v.tensor_copy(WqT[:], bank[6][:, :].rearrange("p (c f) -> p c f", c=2)), False)
            dve.wait_ge(prep_pe, 5)
            v.tensor_copy(rwT[:], bank[7][:, 0:2 * X].rearrange("p (c f) -> p c f", c=2)).then_inc(prep_dve, 1)
            v.tensor_copy(eb1_col[:], bank[7][:, 32:32 + 2 * X]).then_inc(prep_dve, 1)

            def kv_scale(t):
                dve.wait_ge(std_ready, t + 1)
                link(v.reciprocal(ss[:, t % 3, :], ss[:, t % 3, :]))
                if t >= 2:
                    dve.wait_ge(kvt_step, t - 1)
                v.tensor_tensor(khv[:, t % 2, :].rearrange("p (h f) -> p h f", f=HC),
                                bank[t % 3][0:P, :].rearrange("p (h f) -> p h f", f=HC),
                                ss[:, t % 3, :].rearrange("p (h a) -> p h a", a=1).to_broadcast([P, 2 * H, HC]), ALU.mult).then_inc(khv_ready, 1)

            def kv_tile(t):
                dve.wait_ge(sq_ready, t + 1)
                link(v.tensor_reduce(ss[:, t % 3, :], sq[:, t % 2, :].rearrange("p (h f) -> p h f", f=HC), AX.X, ALU.add))
                v.tensor_scalar(ss[:, t % 3, :], ss[:, t % 3, :], 1.0 / HC, EPS, ALU.mult, ALU.add).then_inc(var_ready, 1)
                if t >= 1:
                    kv_scale(t - 1)
                if t == T - 1:
                    kv_scale(t)

            def add_mixer_tile(t):
                if t == 0:
                    dve.wait_ge(base_ready, T)
                dve.wait_ge(down_done, t + 1)
                v.tensor_tensor(acc[:, t, :], acc[:, t, :], bank[4 + t % 4][0:P, 0:D], ALU.add).then_inc(y_used, 1)

            def background(c, step):
                for t in range(background_tile(c, step), background_tile(c, step + 1)):
                    if c < 3:
                        kv_tile(t)
                    else:
                        add_mixer_tile(t)

            def fill_rows(c):
                dve.wait_ge(zd_in[c], 16)
                init = z_first if c == 0 else z_last
                n, cs = CE, slice(c * CE, (c + 1) * CE)
                with dve.Fori(0, K) as k:
                    for r in range(R):
                        col = zd[:, 0:n, bass.ds(k * R + r, 1)].rearrange("p j a -> p (j a)")
                        last = v.tensor_tensor_scan(col, same[:, cs, 0], col, init[:, bass.ds(k * R + r, 1)], ALU.mult, ALU.add)
                    last.then_inc(fill_done, 1)
                dve.wait_ge(fill_done, (c + 1) * K)
                link(v.tensor_copy(z_last[:], zd[:, n - 1, :]))

            def edge_chunk(c):
                n, cs = SIZES[c], slice(AT[c], AT[c + 1])
                z0 = AT[c] % CE
                st, z = slot[c % 2][:, 0:n, :], zd[:, z0:z0 + n, :]
                lo_, dm_, dl_, re_, we_ = (b[:, 0:n, :] for b in (logit, dm, dl, rescale, weight))
                background(c, 0)
                dve.wait_ge(zs_in[c], 16 * n)
                products = link(v.tensor_tensor(z, z, st[:, :, 0:KR], ALU.mult), False)
                background(c, 1)
                dve.wait_ge(vch, products)
                v.tensor_reduce(lo_, z.rearrange("p j (k r) -> p j k r", r=R), AX.X, ALU.add).then_inc(zd_free, 1)
                background(c, 2)
                dve.wait_ge(zd_free, c + 1)
                for k in range(K):
                    link(v.tensor_tensor_scan(st[:, :, KR + K + k], forget[:, cs, 0], lo_[:, :, k],
                                              0.0 if c == 0 else s_last[:, KR + K + k:KR + K + k + 1], ALU.add, ALU.max), k == K - 1)
                m = st[:, :, KR + K:SW]
                v.tensor_tensor(dl_, lo_, m, ALU.subtract).then_inc(exp_in, 1)
                link(v.tensor_tensor(dm_[:, 1:n, :], m[:, 0:n - 1, :], m[:, 1:n, :], ALU.subtract), False)
                if c == 0:
                    link(v.memset(dm_[:, 0:1, :], 0.0))
                else:
                    link(v.tensor_tensor(dm_[:, 0:1, :], s_last[:, KR + K:SW].rearrange("p (a k) -> p a k", a=1), m[:, 0:1, :], ALU.subtract))
                v.tensor_tensor(dm_, dm_, forget[:, cs, :].to_broadcast([P, n, K]), ALU.add).then_inc(exp_in, 1)
                background(c, 3)
                dve.wait_ge(exp_done, 2 * c + 2)
                link(v.tensor_copy(st[:, :, KR:KR + K], we_), False)
                z4 = st[:, :, 0:KR].rearrange("p j (k r) -> p j k r", r=R)
                link(v.tensor_tensor(z4, z4, we_.rearrange("p j (k a) -> p j k a", a=1).to_broadcast([P, n, K, R]), ALU.mult))
                background(c, 4)
                def state_scan(col, fac, init):
                    return v.tensor_tensor_scan(col, fac, col, init, ALU.mult, ALU.add)
                with dve.Fori(0, K) as k:
                    fac = re_[:, :, bass.ds(k, 1)].rearrange("p j a -> p (j a)")
                    for r in range(R + 1):
                        f = k * R + r if r < R else k + KR
                        last = state_scan(st[:, :, bass.ds(f, 1)].rearrange("p j a -> p (j a)"), fac,
                                          0.0 if c == 0 else s_last[:, bass.ds(f, 1)])
                    last.then_inc(scan_done, 1)
                dve.wait_ge(scan_done, (c + 1) * K)
                v.tensor_copy(s_last[:], st[:, n - 1, :]).then_inc(state_ready, 1)
                dve.wait_ge(state_ready, c + 1)
                background(c, 5)


            for t in range(KV_FIRST):
                kv_tile(t)
            dve.wait_ge(zfirst_in, 16)
            for c in range(3):
                if c < FILLS:
                    fill_rows(c)
                edge_chunk(c)
            dve.wait_ge(kvt_step, T)
            for g in range(2):
                b5 = bank[5][:, g * D:g * D + 129]
                link(v.tensor_scalar(kvt_a[:], bank[6][:, g * 128:(g + 1) * 128], bv_col[:], None, ALU.mult), False)
                link(v.tensor_scalar(kvt_c[:], b5[:, 128:129], gv_col[:], None, ALU.mult), False)
                link(v.tensor_scalar(kvt_b[:, 0:1], bv_col[:], float(N), None, ALU.mult))
                link(v.tensor_tensor(kvt_c[:], kvt_c[:], kvt_b[:, 0:1], ALU.add), False)
                link(v.scalar_tensor_tensor(kvt_a[:], b5[:, 0:128], gv_col[:], kvt_a[:], ALU.mult, ALU.add))
                a4, b4 = (q[:, :].rearrange("p (h f) -> p h f", f=HC) for q in (kvt_a, kvt_b))
                link(v.tensor_tensor(a4, a4, gk_row[:, :, :].to_broadcast([128, 4, HC]), ALU.mult), False)
                link(v.tensor_scalar(b4, bk_row[:, :, :].to_broadcast([128, 4, HC]), kvt_c[:], None, ALU.mult))
                link(v.tensor_tensor(kvt_a[:], kvt_a[:], kvt_b[:], ALU.add))
                for q in range(4):
                    blk = slice(q * HC, (q + 1) * HC)
                    last = v.tensor_copy(KVT[blk, g, blk], kvt_a[blk, blk])
                if g == 0:
                    link(last)
            last.then_inc(prep_dve, 1)
            dve.wait_ge(prep_pe, 6)
            v.tensor_scalar(B_sb[:], bank[7][:, :].rearrange("p (c f) -> p c f", c=2), 1.0 / N, None, ALU.mult).then_inc(prep_dve, 1)
            dve.wait_ge(prep_pe, 7)
            link(v.tensor_tensor(A_sb[:], bank[5][:, :].rearrange("p (c f) -> p c f", c=2), w1_sb[:], ALU.add), False)
            v.tensor_tensor(bh_col[:], bank[6][:, 0:2], b1_col[:], ALU.add).then_inc(prep_dve, 1)

            for c in range(3, C):
                if c < FILLS:
                    fill_rows(c)
                edge_chunk(c)

            v.tensor_copy(loc[:], s_last[:]).then_inc(loc_ready, 1)
            dve.wait_ge(loc_ready, 1)
            mk = loc[:, KA:SW].rearrange("p (k a) -> p k a", a=1)
            link(v.tensor_copy(cat[:, 0, :], loc[:, 0:KA]), False)
            link(v.tensor_copy(cat[:, 1, 0:KR].rearrange("p (k r) -> p k r", r=R), mk.to_broadcast([P, K, R])), False)
            link(v.tensor_copy(cat[:, 1, KR:KA], loc[:, KA:SW]), False)
            link(v.tensor_copy(cat[:, 2, :], joins.to_broadcast([P, KA])), False)
            v.memset(rows[:, 2:4, 0:1], 0.0).then_inc(cat_ready, 1)
            dve.wait_ge(cat_turned, 1)
            mx, sm = rows[:, 3, :], rows[:, 2, :]
            link(v.tensor_scalar(rows[:, 0, 0:P], bank[0][0:KA, 256:256 + P], -1.0, BIG, ALU.add, ALU.mult), False)
            link(v.tensor_copy(rows[:, 1, 0:P], bank[0][0:KA, 128:128 + P]))
            link(v.tensor_tensor_scan(mx[:, 1:P + 1], rows[:, 0, 0:P], rows[:, 1, 0:P], -BIG, ALU.add, ALU.max))
            link(v.tensor_tensor(rows[:, 1, 0:P], rows[:, 1, 0:P], mx[:, 1:P + 1], ALU.subtract), False)
            link(v.tensor_tensor(rows[:, 0, 0:P], rows[:, 0, 0:P], mx[:, 0:P], ALU.add))
            v.tensor_tensor(rows[:, 0, 0:P], rows[:, 0, 0:P], mx[:, 1:P + 1], ALU.subtract).then_inc(cexp_in, 2)
            dve.wait_ge(cexp_done, 2)
            link(v.tensor_tensor(rows[:, 1, 0:P], rows[:, 1, 0:P], bank[0][0:KA, 0:P], ALU.mult))
            v.tensor_tensor_scan(sm[:, 1:P + 1], rows[:, 0, 0:P], rows[:, 1, 0:P], 0.0, ALU.mult, ALU.add).then_inc(car_ready, 1)
            dve.wait_ge(car_turned, 1)
            link(v.tensor_copy(car[:, 0, :], bank[1][0:P, 0:KA]), False)
            link(v.tensor_copy(car[:, 1, :], bank[1][0:P, 128:128 + KA]), False)
            link(v.tensor_scalar(tmp, cont_in, -1.0, BIG, ALU.add, ALU.mult))
            dve.wait_ge(fix_in, 16)
            cm = ew_r[:, 0, :]
            lm = ew_r[:, 1, :]
            nm = ew_r[:, 2, :]
            link(v.tensor_scalar(cm, car[:, 1, KR:KA], tmp, None, ALU.add), False)
            link(v.tensor_copy(lm, s_last[:, KA:SW]))
            link(v.tensor_tensor(nm, cm, lm, ALU.max))
            link(v.tensor_copy(s_last[:, KA:SW], nm), False)
            link(v.tensor_tensor(cm, cm, nm, ALU.subtract), False)
            v.tensor_tensor(lm, lm, nm, ALU.subtract).then_inc(cexp_in, 2)
            dve.wait_ge(cexp_done, 4)
            for e_, buf in ((cm, car[:, 0, :]), (lm, s_last[:, 0:KA])):
                b4 = buf[:, 0:KR].rearrange("p (k r) -> p k r", r=R)
                link(v.tensor_tensor(b4, b4, e_.rearrange("p (k a) -> p k a", a=1).to_broadcast([P, K, R]), ALU.mult), False)
                link(v.tensor_tensor(buf[:, KR:KA], buf[:, KR:KA], e_, ALU.mult))
            v.tensor_tensor(s_last[:, 0:KA], s_last[:, 0:KA], car[:, 0, :], ALU.add).then_inc(fix_rows, 1)

            def normalise_sums(n):
                dve.wait_ge(agg_in[n], 16 * len(QUADS[n]))
                w, ts = len(QUADS[n]), slice(QUADS[n][0], QUADS[n][-1] + 1)
                link(v.tensor_scalar(rden[:, ts], agg[:, ts, KR:KA], 1e-16, None, ALU.add))
                link(v.reciprocal(rden[:, ts], rden[:, ts]))
                link(v.tensor_tensor(rden[:, ts], rden[:, ts], has_edge[:, ts].to_broadcast([P, w, K]), ALU.mult))
                a4 = agg[:, ts, 0:KR].rearrange("p t (k r) -> p t k r", r=R)
                v.tensor_tensor(a4, a4, rden[:, ts].rearrange("p t (k a) -> p t k a", a=1).to_broadcast([P, w, K, R]), ALU.mult).then_inc(agg_ready, 1)

            def add_grad(q):
                ts, w = slice(PAIRS[q][0], PAIRS[q][-1] + 1), len(PAIRS[q])
                dve.wait_ge(relu_done, q + 1)
                v.tensor_tensor(acc[:, ts, :], grad[:, q % 2, 0:w * D].rearrange("p (t f) -> p t f", f=D), acc[:, ts, :], ALU.add).then_inc(grad_added, 1)
                dve.wait_ge(grad_added, q + 1)
                for t in PAIRS[q]:
                    last = link(v.bn_stats(stats[:, t, :], acc[:, t, :]), False)
                return last

            def quad_stats(n):
                for t in QUADS[n]:
                    link(v.bn_aggr(mv[:, t, :], stats[:, t, :]), t == QUADS[n][-1])
                part = mv[:, QUADS[n][0]:QUADS[n][-1] + 1, 1:2]
                v.tensor_scalar(part, part, EPS, None, ALU.add).then_inc(stat_ready, 1)

            def normalise_quad(n):
                ts = slice(QUADS[n][0], QUADS[n][-1] + 1)
                dve.wait_ge(root_ready, G + n + 1)
                link(v.reciprocal(rstd[:, ts, :], sd[:, ts, :]))
                for t in QUADS[n]:
                    v.tensor_scalar(xn2[:, t, :], acc[:, t, :], mv[:, t, 0:1], rstd[:, t, :], ALU.subtract, ALU.mult).then_inc(xn2_ready, 1)

            normalise_sums(0)
            for q in range(NP):
                if q % 2 == 0 and q // 2 + 1 < NQ:
                    normalise_sums(q // 2 + 1)
                last = add_grad(q)
                if q % 2 == 1 or q == NP - 1:
                    dve.wait_ge(vch, last)
                    quad_stats(q // 2)
                if q % 2 == 0 and q >= 2:
                    normalise_quad(q // 2 - 1)
            normalise_quad(NQ - 1)
            one_m = same[:, 0:M * X, 0]
            link(v.memset(one_m, 1.0))
            dve.wait_ge(logit_done, NP)
            link(v.tensor_copy(lg[:], bank[7][0:P, 0:T * X].rearrange("p (t e) -> p t e", e=X)))
            top1, top2, den, c1, c2, pick = (tp[:, n, :, :] for n in range(6))
            nrm = den
            wide = [P, T, X]
            r8 = rank8[:, :, :].to_broadcast(wide)
            second = quo_f[:, 0:T * X].rearrange("p (t e) -> p t e", e=X)
            rest = lg
            for n, top in enumerate((top1, top2)):
                hot = oh[:, :, n * T:(n + 1) * T].rearrange("p e t -> p t e")
                link(v.tensor_reduce(top[:, :, 0], rest[:], AX.X, ALU.max))
                link(v.tensor_tensor(hot, rest[:], top.to_broadcast(wide), ALU.is_equal))
                link(v.tensor_tensor(hot, hot, r8, ALU.mult))
                link(v.tensor_reduce(pick[:, :, 0], hot, AX.X, ALU.max))
                link(v.tensor_tensor(hot, pick.to_broadcast(wide), r8, ALU.is_equal))
                if n == 0:
                    link(v.tensor_tensor(pr[:], lg[:], top.to_broadcast(wide), ALU.subtract), False)
                    rest = second
                    link(v.scalar_tensor_tensor(rest[:], hot, -BIG, lg[:], ALU.mult, ALU.add))
            link(v.tensor_tensor(c2, top2, top1, ALU.subtract), False)
            v.memset(c1, 0.0).then_inc(pexp_in, 1)
            scan = rem_f[:, 0:X * M].rearrange("p (e m) -> p e m", m=M)
            posx = quo_f[:, 0:X * M].rearrange("p (e m) -> p e m", m=M)
            over = dst_f[:, 0:X * T].rearrange("p (e a) -> p e a", a=T)
            link(v.tensor_tensor_scan(rem_f[:, 0:X * M], one_m, oh[:, :, :].rearrange("p e m -> p (e m)"), 0.0, ALU.mult, ALU.add))
            last_of = scan[:, :, M - 1:M].rearrange("p e a -> p (e a)")
            link(v.tensor_copy(cnt[:, 0:1], last_of[:, 0:1]), False)
            v.tensor_tensor(cnt[:, 1:X], last_of[:, 1:X], last_of[:, 0:X - 1], ALU.subtract).then_inc(cnt_ready, 1)
            dve.wait_ge(cnt_ready, 1)
            link(v.tensor_tensor(off[:, :, 0], cnt[:], last_of, ALU.subtract))
            dve.wait_ge(cnt_summed, 1)
            link(v.tensor_tensor(over, bank[7][0:P, X:2 * X].rearrange("p (e a) -> p e a", a=1).to_broadcast([P, X, T]),
                                 tile_start[0:P, :, 0:T].to_broadcast([P, X, T]), ALU.is_gt))
            link(v.tensor_reduce(ntile[:], over, AX.X, ALU.add), False)
            link(v.tensor_tensor(off[:, :, 0], bank[7][0:P, 0:X], off[:, :, 0], ALU.add))
            link(v.tensor_tensor_scan(tile_end[:], one_m[:, 0:X], ntile[:], 0.0, ALU.mult, ALU.add))
            link(v.tensor_tensor(ntile[:], tile_end[:], ntile[:], ALU.subtract))
            link(v.tensor_scalar(ntile[:], ntile[:], 128.0, -1.0, ALU.mult, ALU.add))
            link(v.tensor_tensor(off[:, :, 0], off[:, :, 0], ntile[:], ALU.add))
            link(v.tensor_tensor(posx, scan, off[:, :, :].to_broadcast([P, X, M]), ALU.add))
            link(v.tensor_tensor(posx, posx, oh[:], ALU.mult))
            link(v.tensor_reduce(pos_m[:, :, 0], posx.rearrange("p e m -> p m e"), AX.X, ALU.add))
            link(v.tensor_scalar(lane_i[:], pos_m[:, :, 0], -63.5, 1.0 / 128, ALU.add, ALU.mult))
            link(v.tensor_copy(lane[:, :, 0], lane_i[:]))
            link(v.scalar_tensor_tensor(lane[:], lane[:], -128.0, pos_m[:], ALU.mult, ALU.add))
            link(v.tensor_scalar(fixl[:], lane[:], 127.5, -128.0, ALU.is_gt, ALU.mult))
            link(v.tensor_tensor(lane[:], lane[:], fixl[:], ALU.add))
            link(v.tensor_tensor(pos_m[:], pos_m[:], lane[:], ALU.subtract))
            dve.wait_ge(logit_done, NP)
            for n in range(M // PIECE):
                ms = slice(n * PIECE, (n + 1) * PIECE)
                if n >= 2:
                    dve.wait_ge(map_used, n - 1)
                link(v.tensor_tensor(hot_lane[n % 2], lane[:, ms].to_broadcast([P, PIECE, 128]),
                                     iota_f[0:P, :].rearrange("p (a b) -> p a b", a=1).to_broadcast([P, PIECE, 128]), ALU.is_equal), False)
                v.tensor_tensor(hot_tile[:, ms], pos_m[:, ms].to_broadcast([P, PIECE, ST]),
                                tile_start[0:P].to_broadcast([P, PIECE, ST]), ALU.is_equal).then_inc(map_hot, 1)
            owner = rem_f[:, 0:0 + X * 50].rearrange("p (a e) -> p a e", e=X)
            for o, w in ((0, 50), (50, ST - 50)):
                link(v.tensor_scalar(tile_end[:], tile_end[:], 128.0, None, ALU.mult)) if o == 0 else None
                link(v.tensor_tensor(owner[:, 0:w], tile_end[:].rearrange("p (a e) -> p a e", a=1).to_broadcast([P, w, X]),
                                     tile_start[0:P, 0, o:o + w].rearrange("p (a b) -> p a b", b=1).to_broadcast([P, w, X]), ALU.is_le))
                link(v.tensor_reduce(expert_f[:, o:o + w], owner[:, 0:w], AX.X, ALU.add))
            link(v.tensor_scalar(expert_f[:], expert_f[:], float(X - 1), None, ALU.min))
            link(v.tensor_copy(expert_i[:], expert_f[:]))
            dve.wait_ge(map_used, M // PIECE)
            slot_i, slot_w = bank[0][:, 0:ST], bank[0][:, ST:2 * ST]
            link(v.tensor_scalar(slot_c[:], slot_w, 32.5, -32.0, ALU.is_gt, ALU.mult), False)
            link(v.tensor_scalar(slot_e[:], slot_w, 0.5, OUT_OF_RANGE, ALU.is_lt, ALU.mult), False)
            link(v.tensor_copy(slot_v[:], slot_w))
            link(v.scalar_tensor_tensor(slot_v[:], slot_i, float(T), slot_v[:], ALU.mult, ALU.add))
            link(v.tensor_tensor(slot_v[:], slot_v[:], slot_c[:], ALU.add))
            link(v.tensor_scalar(in_row[:], slot_v[:], -1.0, 0.0, ALU.add, ALU.max), False)
            link(v.scalar_tensor_tensor(slot_c[:], slot_c[:], -N / 32.0, slot_e[:], ALU.mult, ALU.add))
            v.scalar_tensor_tensor(out_row[:], slot_v[:], -1.0, slot_c[:], ALU.add, ALU.add).then_inc(slots_ready, 1)

            def fetch_w1(i, n):
                e = expert_of(dve, i, n)
                if n >= 2:
                    dve.wait_ge(eh_ready, i * (2 * RING) + 2 * (n - 1))
                link(v.tensor_scalar(b1_tile[:, n % 2, :], eb1_col[:, bass.ds(e * 2, 2)], 1.0, None, ALU.mult), False)
                v.tensor_scalar(w1_tile[:, n % 2], ew1_sb[:, bass.ds(e, 1)].rearrange("p e c f -> p (e c) f"), 1.0, None, ALU.mult).then_inc(w1_ready, 1)

            def add_b2(i, n):
                e = expert_of(dve, i, n)
                dve.wait_ge(edown_done, i * RING + (n + 1))
                if n >= RING:
                    dve.wait_ge(y_out[n % RING], i * 16 + 16 * (n // RING))
                v.tensor_tensor(y_ring[:, n % RING, :], bank[4 + n % 2][:, 0:D],
                                eb2_all[:, bass.ds(e, 1), :].rearrange("p e f -> p (e f)"), ALU.add).then_inc(y_ready, 1)

            dve.wait_ge(ew_in, 48)
            fetch_w1(0, 0)
            fetch_w1(0, 1)
            dve.wait_ge(pexp_done, 2)
            link(v.tensor_reduce(den[:, :, 0], pr[:], AX.X, ALU.add))
            link(v.reciprocal(den, den))
            for top in (c1, c2):
                link(v.tensor_tensor(top, top, den, ALU.mult))
            link(v.tensor_tensor(nrm, c1, c2, ALU.add))
            link(v.tensor_scalar(nrm, nrm, 1e-12, None, ALU.max))
            link(v.reciprocal(nrm, nrm))
            for top in (c1, c2):
                link(v.tensor_tensor(top, top, nrm, ALU.mult))

            def dve_step(i, n):
                if n + 2 < ST:
                    fetch_w1(i, n + 2)
                add_b2(i, n)

            tile_steps(dve, dve_step)
            for g in range(G):
                dve.wait_ge(back_in[g], 16)
                for k, top in enumerate((c1, c2)):
                    dve.wait_ge(acc_step, NQ + (g * TOP + k) * GT)
                    for u in range(GT):
                        t = g * GT + u
                        v.scalar_tensor_tensor(acc[:, t, :], back[g][:, k, u, :], top[:, t, :], acc[:, t, :], ALU.mult, ALU.add).then_inc(acc_step, 1)


_INS = ["x", "src", "dst", "L0_gnn_U", "L0_gnn_Dmat", "L0_gnn_head_w", "L0_mix_w_qkv", "L0_mix_b_qkv",
        "L0_mix_kln_g", "L0_mix_kln_b", "L0_mix_vln_g", "L0_mix_vln_b", "L0_mix_w1", "L0_mix_b1",
        "L0_mix_w2", "L0_mix_b2", "L0_ffn_router_w", "L0_ffn_w1", "L0_ffn_b1", "L0_ffn_w2", "L0_ffn_b2"]


def kernel(**inputs):
    import concourse.bacc as bacc
    from concourse.bass_utils import run_bass_kernel_spmd

    nc = bacc.Bacc("TRN2", target_bir_lowering=False, num_devices=1)
    arrays, args = {}, []
    for name in _INS:
        a = np.ascontiguousarray(inputs[name])
        arrays[f"in_{name}"] = a
        args.append(nc.dram_tensor(f"in_{name}", a.shape, mybir.dt.from_np(a.dtype), kind="ExternalInput").ap())
    out = nc.dram_tensor("out_0", (N, D), F32, kind="ExternalOutput").ap()
    build(nc, *args, out)
    r = run_bass_kernel_spmd(nc, [arrays], core_ids=[0])
    return r.results[0]["out_0"]
```
